# Optimizing a Trainium2 kernel written in Bass

```python
import numpy as np
import jax
import jax.numpy as jnp

def _softmax(x, axis=-1):
    return jax.nn.softmax(x, axis=axis)

def _gelu(x):
    return jax.nn.gelu(x, approximate=True)

def _silu(x):
    return jax.nn.silu(x)

def _sigmoid(x):
    return jax.nn.sigmoid(x)

def _layernorm(x, axis=-1, eps=1e-05):
    m = jnp.mean(x, axis=axis, keepdims=True)
    v = jnp.var(x, axis=axis, keepdims=True)
    return (x - m) / jnp.sqrt(v + eps)

def _scatter_add(tgt, idx, src, axis=0):
    return tgt.at[idx].add(src)

def _segment_sum(src, seg, n):
    return jax.ops.segment_sum(src, seg, n)
kernel_name = 'mk_gnn_ffn_d2_gnn_r32_dd5727'

def setup_inputs(seed: int=0):
    np.random.seed(seed)
    _w = jnp.asarray

    def _rec_inputs():
        import jax
        import jax.numpy as jnp
        _gk = jax.random.key(seed)
        x = -0.000202 + 1 * jax.random.normal(jax.random.fold_in(_gk, 1), (3125, 256), jnp.float32)
        _s = jax.random.randint(jax.random.fold_in(_gk, 2), (25000,), 0, 3125, jnp.int32)
        _d = jax.random.randint(jax.random.fold_in(_gk, 3), (25000,), 0, 3125, jnp.int32)
        _loop = jnp.arange(3125, dtype=jnp.int32)
        src = jnp.concatenate([_s, _d, _loop])
        dst = jnp.concatenate([_d, _s, _loop])
        _o = jnp.argsort(dst, stable=True)
        src = src[_o]
        dst = dst[_o]
        edge_attr_4 = 0.00121237 + 1.00026 * jax.random.normal(jax.random.fold_in(_gk, 12), (53125, 4), jnp.float32)
        edge_attr_8 = jax.random.uniform(jax.random.fold_in(_gk, 13), (53125, 8), jnp.float32, 0.0, 1)
        node_vec1 = jax.random.uniform(jax.random.fold_in(_gk, 15), (3125, 1), jnp.float32, 0.0, 1)
        return (x, src, dst, edge_attr_4, edge_attr_8, node_vec1)
    x, src, dst, edge_attr_4, edge_attr_8, node_vec1 = _rec_inputs()

    def _L0_gnn_setup():
        import jax, jax.numpy as jnp
        import numpy as np
        N = 25000
        E = 12500
        MUL = 64
        NB = 8
        RN = 64
        NUM_NEIGH = 16.0
        INV_SQRT3 = 1.0 / np.sqrt(3.0)

        def _forward(node_input, node_attr, edge_attr, edge_length_embedded, W_sc0, W_sc1, W_lin1_0, W_lin1_1, fc_w0, fc_w1, W_lin2_0, W_lin2_1, edge_src, edge_dst):
            Nn = node_input.shape[0]
            z = node_attr
            x0 = node_input[:, :MUL]
            x1 = node_input[:, MUL:].reshape(Nn, MUL, 3)
            inv_m = 1.0 / np.sqrt(MUL)
            s0 = x0 @ W_sc0 * z * inv_m
            s1 = jnp.einsum('nuc,uv->nvc', x1, W_sc1) * z[:, :, None] * inv_m
            h0 = x0 @ W_lin1_0 * z * inv_m
            h1 = jnp.einsum('nuc,uv->nvc', x1, W_lin1_1) * z[:, :, None] * inv_m
            hid = jax.nn.silu(edge_length_embedded @ fc_w0 / np.sqrt(NB))
            w = hid @ fc_w1 / np.sqrt(RN)
            wA, wB, wC, wD = (w[:, :MUL], w[:, MUL:2 * MUL], w[:, 2 * MUL:3 * MUL], w[:, 3 * MUL:])
            xs0 = h0[edge_src]
            xs1 = h1[edge_src]
            sh0 = edge_attr[:, :1]
            sh1 = edge_attr[:, 1:4]
            midA = wA * xs0 * sh0
            midD = wD * jnp.einsum('euc,ec->eu', xs1, sh1) * INV_SQRT3
            midB = (wB * xs0)[:, :, None] * sh1[:, None, :]
            midC = wC[:, :, None] * xs1 * sh0[:, None, :]
            mid0 = jnp.concatenate([midA, midD], axis=1)
            mid1 = jnp.concatenate([midB, midC], axis=1)
            inv_nb = 1.0 / np.sqrt(NUM_NEIGH)
            y0 = jax.ops.segment_sum(mid0, edge_dst, num_segments=Nn) * inv_nb
            y1 = jax.ops.segment_sum(mid1.reshape(mid1.shape[0], -1), edge_dst, num_segments=Nn).reshape(Nn, 2 * MUL, 3) * inv_nb
            inv_2m = 1.0 / np.sqrt(2 * MUL)
            o0 = y0 @ W_lin2_0 * z * inv_2m
            o1 = jnp.einsum('nuc,uv->nvc', y1, W_lin2_1) * z[:, :, None] * inv_2m
            c_s = np.float32(np.sin(np.pi / 8.0))
            c_x = np.float32(np.cos(np.pi / 8.0))
            out0 = c_s * s0 + c_x * o0
            out1 = c_s * s1 + c_x * o1
            return jnp.concatenate([out0, out1.reshape(Nn, 3 * MUL)], axis=1)
        key = jax.random.key(seed)
        ks = jax.random.split(key, 14)
        f32 = jnp.float32
        return {'node_input': jax.random.normal(ks[0], (N, 4 * MUL), f32), 'node_attr': jnp.ones((N, 1), f32), 'edge_src': jax.random.randint(ks[1], (E,), 0, N, dtype=jnp.int32), 'edge_dst': jax.random.randint(ks[2], (E,), 0, N, dtype=jnp.int32), 'edge_attr': jax.random.normal(ks[3], (E, 4), f32), 'edge_length_embedded': jax.random.uniform(ks[4], (E, NB), f32), 'W_sc0': jax.random.normal(ks[5], (MUL, MUL), f32), 'W_sc1': jax.random.normal(ks[6], (MUL, MUL), f32), 'W_lin1_0': jax.random.normal(ks[7], (MUL, MUL), f32), 'W_lin1_1': jax.random.normal(ks[8], (MUL, MUL), f32), 'fc_w0': jax.random.normal(ks[9], (NB, RN), f32), 'fc_w1': jax.random.normal(ks[10], (RN, 4 * MUL), f32), 'W_lin2_0': jax.random.normal(ks[11], (2 * MUL, MUL), f32), 'W_lin2_1': jax.random.normal(ks[12], (2 * MUL, MUL), f32)}
    _L0_gnn_all = _L0_gnn_setup()
    _L0_gnn_in = {k: v for k, v in _L0_gnn_all.items() if k in ('W_sc0', 'W_sc1', 'W_lin1_0', 'W_lin1_1', 'fc_w0', 'fc_w1', 'W_lin2_0', 'W_lin2_1')}
    del _L0_gnn_all

    def _L0_ffn_setup():
        import jax, jax.numpy as jnp
        import numpy as np
        E = 8
        K = 2
        D = 256
        H = 512
        DOUT = 256
        EPS = 1e-05
        key = jax.random.key(seed)
        ks = jax.random.split(key, 9)
        s = 0.02
        return {'x': jax.random.normal(ks[0], (4, 256, D), jnp.float32), 'gamma': 1.0 + 0.05 * jax.random.normal(ks[1], (D,), jnp.float32), 'beta': 0.05 * jax.random.normal(ks[2], (D,), jnp.float32), 'Wr': 0.01 * jax.random.normal(ks[3], (D, E), jnp.float32), 'br': jnp.zeros((E,), jnp.float32), 'W1': s * jax.random.normal(ks[4], (E, D, H), jnp.float32), 'b1': s * jax.random.normal(ks[5], (E, H), jnp.float32), 'W2': s * jax.random.normal(ks[6], (E, H, DOUT), jnp.float32), 'b2': s * jax.random.normal(ks[7], (E, DOUT), jnp.float32)}
    _L0_ffn_all = _L0_ffn_setup()
    _L0_ffn_in = {k: v for k, v in _L0_ffn_all.items() if k in ('gamma', 'beta', 'Wr', 'br', 'W1', 'b1', 'W2', 'b2')}
    del _L0_ffn_all

    def _L1_gnn_setup():
        import jax, jax.numpy as jnp
        import numpy as np
        N = 625
        E = 10000
        HEADS = 4
        C = 64
        NEG_SLOPE = 0.2

        def _gat_layer(x, src, dst, W, a_s, a_d, b):
            n = x.shape[0]
            h = (x @ W).reshape(n, HEADS, C)
            s_src = jnp.einsum('nhc,hc->nh', h, a_s)
            s_dst = jnp.einsum('nhc,hc->nh', h, a_d)
            e = jax.nn.leaky_relu(s_src[src] + s_dst[dst], NEG_SLOPE)
            m = jax.ops.segment_max(e, dst, num_segments=n)
            ex = jnp.exp(e - m[dst])
            denom = jax.ops.segment_sum(ex, dst, num_segments=n)
            alpha = ex / denom[dst]
            msg = h[src] * alpha[:, :, None]
            out = jax.ops.segment_sum(msg, dst, num_segments=n)
            return out.reshape(n, HEADS * C) + b
        key = jax.random.key(seed)
        ks = jax.random.split(key, 16)
        x = jax.random.normal(ks[0], (N, 256), dtype=jnp.float32)
        edge_index = jax.random.randint(ks[1], (2, E), 0, N, dtype=jnp.int64)
        d = {'x': x, 'edge_index': edge_index}
        i = 2
        for l, fin in ((1, 256), (2, 256), (3, 256)):
            scale = 1.0 / np.sqrt(fin)
            d[f'W{l}'] = jax.random.normal(ks[i], (fin, HEADS * C), dtype=jnp.float32) * scale
            i += 1
            d[f'a_src{l}'] = jax.random.normal(ks[i], (HEADS, C), dtype=jnp.float32) * scale
            i += 1
            d[f'a_dst{l}'] = jax.random.normal(ks[i], (HEADS, C), dtype=jnp.float32) * scale
            i += 1
            d[f'b{l}'] = jnp.zeros((HEADS * C,), dtype=jnp.float32)
        return d
    _L1_gnn_all = _L1_gnn_setup()
    _L1_gnn_in = {k: v for k, v in _L1_gnn_all.items() if k in ('W1', 'a_src1', 'a_dst1', 'b1', 'W2', 'a_src2', 'a_dst2', 'b2', 'W3', 'a_src3', 'a_dst3', 'b3')}
    del _L1_gnn_all

    def _L1_ffn_setup():
        import jax, jax.numpy as jnp
        import numpy as np
        B, N, D = (16, 128, 256)
        NUM_EXPERTS, TOP_K, HEADS = (4, 2, 4)
        N_EDGES = 32768
        LN_EPS = 1e-05

        def _layernorm(x, g, b):
            mu = x.mean(-1, keepdims=True)
            var = ((x - mu) ** 2).mean(-1, keepdims=True)
            return (x - mu) * jax.lax.rsqrt(var + LN_EPS) * g + b

        def _forward(x, edge_index, W_gat, att_src, att_dst, b_gat, ln_gamma, ln_beta, W1, b1, W2, b2):
            Bc, Nc, Dc = x.shape
            M = Bc * Nc
            x_flat = x.reshape(M, Dc)
            h = (x_flat @ W_gat).reshape(M, HEADS, NUM_EXPERTS)
            loops = jnp.arange(M, dtype=edge_index.dtype)
            src = jnp.concatenate([edge_index[0], loops])
            dst = jnp.concatenate([edge_index[1], loops])
            a_src = (h * att_src).sum(-1)
            a_dst = (h * att_dst).sum(-1)
            e = jax.nn.leaky_relu(a_src[src] + a_dst[dst], negative_slope=0.2)
            e_max = jax.ops.segment_max(e, dst, num_segments=M)
            ee = jnp.exp(e - e_max[dst])
            denom = jax.ops.segment_sum(ee, dst, num_segments=M)
            alpha = ee / (denom[dst] + 1e-16)
            msg = h[src] * alpha[:, :, None]
            agg = jax.ops.segment_sum(msg, dst, num_segments=M).reshape(M, HEADS * NUM_EXPERTS) + b_gat
            scores = _layernorm(agg, ln_gamma, ln_beta).reshape(M, HEADS, NUM_EXPERTS).mean(1)
            scores = scores.reshape(Bc, Nc, NUM_EXPERTS)
            topk_s, topk_i = jax.lax.top_k(scores, TOP_K)
            w = jax.nn.softmax(topk_s, axis=-1)
            out = jnp.zeros_like(x)
            for ei in range(NUM_EXPERTS):
                g = jnp.where(topk_i == ei, w, 0.0).sum(-1)
                hh = jax.nn.gelu(x @ W1[ei] + b1[ei], approximate=False)
                out = out + g[..., None] * (hh @ W2[ei] + b2[ei])
            return out
        key = jax.random.key(seed)
        ks = jax.random.split(key, 8)
        s = 0.05
        return {'x': jax.random.normal(ks[0], (B, N, D), jnp.float32), 'W_gat': jax.random.normal(ks[1], (D, HEADS * NUM_EXPERTS), jnp.float32) * s, 'att_src': jax.random.normal(ks[2], (HEADS, NUM_EXPERTS), jnp.float32) * s, 'att_dst': jax.random.normal(ks[3], (HEADS, NUM_EXPERTS), jnp.float32) * s, 'b_gat': jnp.zeros((HEADS * NUM_EXPERTS,), jnp.float32), 'ln_gamma': jnp.ones((HEADS * NUM_EXPERTS,), jnp.float32), 'ln_beta': jnp.zeros((HEADS * NUM_EXPERTS,), jnp.float32), 'W1': jax.random.normal(ks[4], (NUM_EXPERTS, D, 2 * D), jnp.float32) * s, 'b1': jnp.zeros((NUM_EXPERTS, 2 * D), jnp.float32), 'W2': jax.random.normal(ks[5], (NUM_EXPERTS, 2 * D, D), jnp.float32) * s, 'b2': jnp.zeros((NUM_EXPERTS, D), jnp.float32), 'edge_index': jax.random.randint(ks[6], (2, N_EDGES), 0, B * N, jnp.int32)}
    _L1_ffn_all = _L1_ffn_setup()
    _L1_ffn_in = {k: v for k, v in _L1_ffn_all.items() if k in ('W_gat', 'att_src', 'att_dst', 'b_gat', 'ln_gamma', 'ln_beta', 'W1', 'b1', 'W2', 'b2', 'edge_index')}
    del _L1_ffn_all
    return {'x': x, 'src': src, 'dst': dst, 'edge_attr_4': edge_attr_4, 'edge_attr_8': edge_attr_8, 'node_vec1': node_vec1, 'L0_gnn_W_sc0': _L0_gnn_in['W_sc0'], 'L0_gnn_W_sc1': _L0_gnn_in['W_sc1'], 'L0_gnn_W_lin1_0': _L0_gnn_in['W_lin1_0'], 'L0_gnn_W_lin1_1': _L0_gnn_in['W_lin1_1'], 'L0_gnn_fc_w0': _L0_gnn_in['fc_w0'], 'L0_gnn_fc_w1': _L0_gnn_in['fc_w1'], 'L0_gnn_W_lin2_0': _L0_gnn_in['W_lin2_0'], 'L0_gnn_W_lin2_1': _L0_gnn_in['W_lin2_1'], 'L0_ffn_gamma': _L0_ffn_in['gamma'], 'L0_ffn_beta': _L0_ffn_in['beta'], 'L0_ffn_Wr': _L0_ffn_in['Wr'], 'L0_ffn_br': _L0_ffn_in['br'], 'L0_ffn_W1': _L0_ffn_in['W1'], 'L0_ffn_b1': _L0_ffn_in['b1'], 'L0_ffn_W2': _L0_ffn_in['W2'], 'L0_ffn_b2': _L0_ffn_in['b2'], 'L1_gnn_W1': _L1_gnn_in['W1'], 'L1_gnn_a_src1': _L1_gnn_in['a_src1'], 'L1_gnn_a_dst1': _L1_gnn_in['a_dst1'], 'L1_gnn_b1': _L1_gnn_in['b1'], 'L1_gnn_W2': _L1_gnn_in['W2'], 'L1_gnn_a_src2': _L1_gnn_in['a_src2'], 'L1_gnn_a_dst2': _L1_gnn_in['a_dst2'], 'L1_gnn_b2': _L1_gnn_in['b2'], 'L1_gnn_W3': _L1_gnn_in['W3'], 'L1_gnn_a_src3': _L1_gnn_in['a_src3'], 'L1_gnn_a_dst3': _L1_gnn_in['a_dst3'], 'L1_gnn_b3': _L1_gnn_in['b3'], 'L1_ffn_W_gat': _L1_ffn_in['W_gat'], 'L1_ffn_att_src': _L1_ffn_in['att_src'], 'L1_ffn_att_dst': _L1_ffn_in['att_dst'], 'L1_ffn_b_gat': _L1_ffn_in['b_gat'], 'L1_ffn_ln_gamma': _L1_ffn_in['ln_gamma'], 'L1_ffn_ln_beta': _L1_ffn_in['ln_beta'], 'L1_ffn_W1': _L1_ffn_in['W1'], 'L1_ffn_b1': _L1_ffn_in['b1'], 'L1_ffn_W2': _L1_ffn_in['W2'], 'L1_ffn_b2': _L1_ffn_in['b2'], 'L1_ffn_edge_index': _L1_ffn_in['edge_index']}

def reference(x, src, dst, edge_attr_4, edge_attr_8, node_vec1, L0_gnn_W_sc0, L0_gnn_W_sc1, L0_gnn_W_lin1_0, L0_gnn_W_lin1_1, L0_gnn_fc_w0, L0_gnn_fc_w1, L0_gnn_W_lin2_0, L0_gnn_W_lin2_1, L0_ffn_gamma, L0_ffn_beta, L0_ffn_Wr, L0_ffn_br, L0_ffn_W1, L0_ffn_b1, L0_ffn_W2, L0_ffn_b2, L1_gnn_W1, L1_gnn_a_src1, L1_gnn_a_dst1, L1_gnn_b1, L1_gnn_W2, L1_gnn_a_src2, L1_gnn_a_dst2, L1_gnn_b2, L1_gnn_W3, L1_gnn_a_src3, L1_gnn_a_dst3, L1_gnn_b3, L1_ffn_W_gat, L1_ffn_att_src, L1_ffn_att_dst, L1_ffn_b_gat, L1_ffn_ln_gamma, L1_ffn_ln_beta, L1_ffn_W1, L1_ffn_b1, L1_ffn_W2, L1_ffn_b2, L1_ffn_edge_index):
    import jax
    import jax.numpy as jnp

    def _L0_gnn_ref(node_input, node_attr, edge_src, edge_dst, edge_attr, edge_length_embedded, W_sc0, W_sc1, W_lin1_0, W_lin1_1, fc_w0, fc_w1, W_lin2_0, W_lin2_1):
        import jax, jax.numpy as jnp
        import numpy as np
        N = 25000
        E = 12500
        MUL = 64
        NB = 8
        RN = 64
        NUM_NEIGH = 16.0
        INV_SQRT3 = 1.0 / np.sqrt(3.0)

        def _forward(node_input, node_attr, edge_attr, edge_length_embedded, W_sc0, W_sc1, W_lin1_0, W_lin1_1, fc_w0, fc_w1, W_lin2_0, W_lin2_1, edge_src, edge_dst):
            Nn = node_input.shape[0]
            z = node_attr
            x0 = node_input[:, :MUL]
            x1 = node_input[:, MUL:].reshape(Nn, MUL, 3)
            inv_m = 1.0 / np.sqrt(MUL)
            s0 = x0 @ W_sc0 * z * inv_m
            s1 = jnp.einsum('nuc,uv->nvc', x1, W_sc1) * z[:, :, None] * inv_m
            h0 = x0 @ W_lin1_0 * z * inv_m
            h1 = jnp.einsum('nuc,uv->nvc', x1, W_lin1_1) * z[:, :, None] * inv_m
            hid = jax.nn.silu(edge_length_embedded @ fc_w0 / np.sqrt(NB))
            w = hid @ fc_w1 / np.sqrt(RN)
            wA, wB, wC, wD = (w[:, :MUL], w[:, MUL:2 * MUL], w[:, 2 * MUL:3 * MUL], w[:, 3 * MUL:])
            xs0 = h0[edge_src]
            xs1 = h1[edge_src]
            sh0 = edge_attr[:, :1]
            sh1 = edge_attr[:, 1:4]
            midA = wA * xs0 * sh0
            midD = wD * jnp.einsum('euc,ec->eu', xs1, sh1) * INV_SQRT3
            midB = (wB * xs0)[:, :, None] * sh1[:, None, :]
            midC = wC[:, :, None] * xs1 * sh0[:, None, :]
            mid0 = jnp.concatenate([midA, midD], axis=1)
            mid1 = jnp.concatenate([midB, midC], axis=1)
            inv_nb = 1.0 / np.sqrt(NUM_NEIGH)
            y0 = jax.ops.segment_sum(mid0, edge_dst, num_segments=Nn) * inv_nb
            y1 = jax.ops.segment_sum(mid1.reshape(mid1.shape[0], -1), edge_dst, num_segments=Nn).reshape(Nn, 2 * MUL, 3) * inv_nb
            inv_2m = 1.0 / np.sqrt(2 * MUL)
            o0 = y0 @ W_lin2_0 * z * inv_2m
            o1 = jnp.einsum('nuc,uv->nvc', y1, W_lin2_1) * z[:, :, None] * inv_2m
            c_s = np.float32(np.sin(np.pi / 8.0))
            c_x = np.float32(np.cos(np.pi / 8.0))
            out0 = c_s * s0 + c_x * o0
            out1 = c_s * s1 + c_x * o1
            return jnp.concatenate([out0, out1.reshape(Nn, 3 * MUL)], axis=1)
        return _forward(node_input, node_attr, edge_attr, edge_length_embedded, W_sc0, W_sc1, W_lin1_0, W_lin1_1, fc_w0, fc_w1, W_lin2_0, W_lin2_1, edge_src, edge_dst)

    def _L0_ffn_ref(x, gamma, beta, Wr, br, W1, b1, W2, b2):
        import jax, jax.numpy as jnp
        import numpy as np
        E = 8
        K = 2
        D = 256
        H = 512
        DOUT = 256
        EPS = 1e-05
        mu = jnp.mean(x, axis=-1, keepdims=True)
        var = jnp.mean(jnp.square(x - mu), axis=-1, keepdims=True)
        xn = (x - mu) * jax.lax.rsqrt(var + EPS) * gamma + beta
        logits = jnp.einsum('bsd,de->bse', xn, Wr) + br
        top_vals, top_idx = jax.lax.top_k(logits, K)
        w = jax.nn.softmax(top_vals, axis=-1)
        w_full = jnp.einsum('bsk,bske->bse', w, jax.nn.one_hot(top_idx, E, dtype=w.dtype))
        y = jnp.zeros(x.shape[:-1] + (DOUT,), x.dtype)
        for e in range(E):
            h = jax.nn.gelu(jnp.einsum('bsd,dh->bsh', xn, W1[e]) + b1[e], approximate=False)
            y_e = jnp.einsum('bsh,hd->bsd', h, W2[e]) + b2[e]
            y = y + y_e * w_full[..., e, None]
        return y

    def _L1_gnn_ref(x, edge_index, W1, a_src1, a_dst1, b1, W2, a_src2, a_dst2, b2, W3, a_src3, a_dst3, b3):
        import jax, jax.numpy as jnp
        import numpy as np
        N = 625
        E = 10000
        HEADS = 4
        C = 64
        NEG_SLOPE = 0.2

        def _gat_layer(x, src, dst, W, a_s, a_d, b):
            n = x.shape[0]
            h = (x @ W).reshape(n, HEADS, C)
            s_src = jnp.einsum('nhc,hc->nh', h, a_s)
            s_dst = jnp.einsum('nhc,hc->nh', h, a_d)
            e = jax.nn.leaky_relu(s_src[src] + s_dst[dst], NEG_SLOPE)
            m = jax.ops.segment_max(e, dst, num_segments=n)
            ex = jnp.exp(e - m[dst])
            denom = jax.ops.segment_sum(ex, dst, num_segments=n)
            alpha = ex / denom[dst]
            msg = h[src] * alpha[:, :, None]
            out = jax.ops.segment_sum(msg, dst, num_segments=n)
            return out.reshape(n, HEADS * C) + b
        loops = jnp.arange(N, dtype=edge_index.dtype)
        src = jnp.concatenate([edge_index[0], loops])
        dst = jnp.concatenate([edge_index[1], loops])
        h = _gat_layer(x, src, dst, W1, a_src1, a_dst1, b1)
        h = jax.nn.relu(h)
        h = _gat_layer(h, src, dst, W2, a_src2, a_dst2, b2)
        h = jax.nn.relu(h)
        h = _gat_layer(h, src, dst, W3, a_src3, a_dst3, b3)
        norm = jnp.maximum(jnp.linalg.norm(h, axis=-1, keepdims=True), 1e-12)
        return h / norm

    def _L1_ffn_ref(x, W_gat, att_src, att_dst, b_gat, ln_gamma, ln_beta, W1, b1, W2, b2, edge_index):
        import jax, jax.numpy as jnp
        import numpy as np
        B, N, D = (16, 128, 256)
        NUM_EXPERTS, TOP_K, HEADS = (4, 2, 4)
        N_EDGES = 32768
        LN_EPS = 1e-05

        def _layernorm(x, g, b):
            mu = x.mean(-1, keepdims=True)
            var = ((x - mu) ** 2).mean(-1, keepdims=True)
            return (x - mu) * jax.lax.rsqrt(var + LN_EPS) * g + b

        def _forward(x, edge_index, W_gat, att_src, att_dst, b_gat, ln_gamma, ln_beta, W1, b1, W2, b2):
            Bc, Nc, Dc = x.shape
            M = Bc * Nc
            x_flat = x.reshape(M, Dc)
            h = (x_flat @ W_gat).reshape(M, HEADS, NUM_EXPERTS)
            loops = jnp.arange(M, dtype=edge_index.dtype)
            src = jnp.concatenate([edge_index[0], loops])
            dst = jnp.concatenate([edge_index[1], loops])
            a_src = (h * att_src).sum(-1)
            a_dst = (h * att_dst).sum(-1)
            e = jax.nn.leaky_relu(a_src[src] + a_dst[dst], negative_slope=0.2)
            e_max = jax.ops.segment_max(e, dst, num_segments=M)
            ee = jnp.exp(e - e_max[dst])
            denom = jax.ops.segment_sum(ee, dst, num_segments=M)
            alpha = ee / (denom[dst] + 1e-16)
            msg = h[src] * alpha[:, :, None]
            agg = jax.ops.segment_sum(msg, dst, num_segments=M).reshape(M, HEADS * NUM_EXPERTS) + b_gat
            scores = _layernorm(agg, ln_gamma, ln_beta).reshape(M, HEADS, NUM_EXPERTS).mean(1)
            scores = scores.reshape(Bc, Nc, NUM_EXPERTS)
            topk_s, topk_i = jax.lax.top_k(scores, TOP_K)
            w = jax.nn.softmax(topk_s, axis=-1)
            out = jnp.zeros_like(x)
            for ei in range(NUM_EXPERTS):
                g = jnp.where(topk_i == ei, w, 0.0).sum(-1)
                hh = jax.nn.gelu(x @ W1[ei] + b1[ei], approximate=False)
                out = out + g[..., None] * (hh @ W2[ei] + b2[ei])
            return out
        return _forward(x, edge_index, W_gat, att_src, att_dst, b_gat, ln_gamma, ln_beta, W1, b1, W2, b2)
    edge_index = jnp.stack([src, dst])
    x = x + _L0_gnn_ref(_layernorm(x, axis=-1), node_vec1, src, dst, edge_attr_4, edge_attr_8, L0_gnn_W_sc0, L0_gnn_W_sc1, L0_gnn_W_lin1_0, L0_gnn_W_lin1_1, L0_gnn_fc_w0, L0_gnn_fc_w1, L0_gnn_W_lin2_0, L0_gnn_W_lin2_1)
    x = x + _L0_ffn_ref(_layernorm(x, axis=-1)[None], L0_ffn_gamma, L0_ffn_beta, L0_ffn_Wr, L0_ffn_br, L0_ffn_W1, L0_ffn_b1, L0_ffn_W2, L0_ffn_b2)[0]
    x = x + _L1_gnn_ref(_layernorm(x, axis=-1), edge_index, L1_gnn_W1, L1_gnn_a_src1, L1_gnn_a_dst1, L1_gnn_b1, L1_gnn_W2, L1_gnn_a_src2, L1_gnn_a_dst2, L1_gnn_b2, L1_gnn_W3, L1_gnn_a_src3, L1_gnn_a_dst3, L1_gnn_b3)
    x = x + _L1_ffn_ref(_layernorm(x, axis=-1)[None], L1_ffn_W_gat, L1_ffn_att_src, L1_ffn_att_dst, L1_ffn_b_gat, L1_ffn_ln_gamma, L1_ffn_ln_beta, L1_ffn_W1, L1_ffn_b1, L1_ffn_W2, L1_ffn_b2, L1_ffn_edge_index)[0]
    return x

_drawn_inputs = setup_inputs


def setup_inputs(seed=0):
    import zlib

    import numpy as np

    out = dict(_drawn_inputs(seed))
    spreads = {'L0_ffn_br': (0.0, 0.1),
     'L1_gnn_b1': (0.0, 0.1),
     'L1_gnn_b2': (0.0, 0.1),
     'L1_gnn_b3': (0.0, 0.1),
     'L1_ffn_b_gat': (0.0, 0.1),
     'L1_ffn_ln_gamma': (1.0, 0.2),
     'L1_ffn_ln_beta': (0.0, 0.1),
     'L1_ffn_b1': (0.0, 0.1),
     'L1_ffn_b2': (0.0, 0.1)}
    factors = {'L0_ffn_gamma': 3.126,
     'L0_ffn_beta': 2.789,
     'L0_ffn_b1': 4.701,
     'L1_gnn_a_src1': 3.069,
     'L1_gnn_a_dst1': 141.054,
     'L1_gnn_a_src2': 8.0,
     'L1_gnn_a_dst2': 200.0,
     'L1_gnn_a_src3': 189.7,
     'L1_gnn_a_dst3': 200.0}
    for name, (base, spread) in spreads.items():
        noise = np.random.default_rng([zlib.crc32(name.encode()), seed]).standard_normal(out[name].shape)
        drawn = base * np.exp(spread * noise) if base else spread * noise
        out[name] = jnp.asarray(drawn.astype(out[name].dtype))
    for name, factor in factors.items():
        out[name] = (out[name] * factor).astype(out[name].dtype)
    return out
```

```python
import numpy as np
from contextlib import ExitStack
from collections import namedtuple

import concourse.bass as bass
from concourse import mybir

F32 = mybir.dt.float32
BF16 = mybir.dt.bfloat16
I32 = mybir.dt.int32
ALU = mybir.AluOpType
ACT = mybir.ActivationFunctionType
AX = mybir.AxisListType
ds = bass.ds

P = 128
N = 3125
D = 256
NB = -(-N // P)
NPAD = NB * P
SORT_G = 3
G = 4
FAR = -1.0e30
KEY_PAD = NPAD


Plan = namedtuple("Plan", "edges tiles out width rows")
Constants = namedtuple("Constants", "ident ident_b ramp ramp_b part before upper ones")


def edge_plan(edges, width):
    step = 2 * SORT_G
    tiles = -(-(-(-edges // P)) // step) * step
    fill = tiles * P - edges
    worst = (edges + NB * (P - 1)) // P + -(-fill // P)
    out = -(-worst // (2 * G)) * 2 * G
    return Plan(edges, tiles, out, width, out // G)


def serial(eng, sem, base=0):
    n = [0]

    def step(ins):
        ins.then_inc(sem, 1)
        n[0] += 1
        eng.wait_ge(sem, base + n[0])
    return step


class Scope:

    def __init__(self, nc, name):
        self.nc, self.name, self.ctx, self.used = nc, name, ExitStack(), []

    def __enter__(self):
        self.ctx.__enter__()
        return self

    def __exit__(self, *a):
        if self.used and a[0] is None:
            self.nc.clear_and_free_semaphores(self.used)
            self.nc.all_engine_barrier()
        return self.ctx.__exit__(*a)

    def sb(self, name, shape, dt=F32):
        return self.ctx.enter_context(self.nc.sbuf_tensor(f"{self.name}_{name}", shape, dt))

    def ps(self, name, shape, dt=F32):
        return self.ctx.enter_context(self.nc.psum_tensor(f"{self.name}_{name}", shape, dt))

    def sem(self, name):
        self.used.append(self.nc.alloc_semaphore(f"{self.name}_{name}"))
        return self.used[-1]

    def sems(self, name, n):
        return [self.sem(f"{name}{i}") for i in range(n)]


def make_constants(nc, S):
    c = Constants(
        ident=S.sb("ident", [P, P]), ident_b=S.sb("ident_b", [P, P], BF16),
        ramp=S.sb("ramp", [P, P]), ramp_b=S.sb("ramp_b", [P, P], BF16),
        part=S.sb("part", [P, 1]), before=S.sb("before", [P, P]), upper=S.sb("upper", [P, P]),
        ones=S.sb("ones", [P, 1]))
    with Scope(nc, "const") as L:
        ramp_i = L.sb("ramp_i", [P, P], I32)
        part_i = L.sb("part_i", [P, 1], I32)
        made = L.sem("made")
        chain = L.sem("chain")
        with nc.Block() as block:
            @block.gpsimd
            def _(pool):
                nc.gpsimd.iota(ramp_i[:, :], [[1, P]], base=0, channel_multiplier=0).then_inc(made, 1)
                nc.gpsimd.iota(part_i[:, :], [[0, 1]], base=0, channel_multiplier=1).then_inc(made, 1)

            @block.vector
            def _(dve):
                link = serial(dve, chain)
                dve.wait_ge(made, 2)
                nc.vector.memset(c.ones[:, :], 1.0)
                link(nc.vector.tensor_copy(c.ramp[:, :], ramp_i[:, :]))
                link(nc.vector.tensor_copy(c.ramp_b[:, :], ramp_i[:, :]))
                link(nc.vector.tensor_copy(c.part[:, :], part_i[:, :]))
                link(nc.vector.tensor_scalar(c.ident[:, :], c.ramp[:, :], c.part[:, :], None, ALU.is_equal))
                link(nc.vector.tensor_scalar(c.before[:, :], c.ramp[:, :], c.part[:, :], None, ALU.is_lt))
                link(nc.vector.tensor_scalar(c.upper[:, :], c.ramp[:, :], c.part[:, :], None, ALU.is_gt))
                link(nc.vector.tensor_copy(c.ident_b[:, :], c.ident[:, :]))
    return c


def sort_edges(nc, C, plan, tag, src, dst, attr, sorted_dram, block_of):
    T, KT, W, g = plan.tiles, plan.out, plan.width, SORT_G
    H = NB + 1
    with Scope(nc, f"sort{tag}") as L:
        src_i = L.sb("src_i", [P, T], I32)
        dst_i = L.sb("dst_i", [P, T], I32)
        blk_i = L.sb("blk_i", [P, T], I32)
        low_i = L.sb("low_i", [P, T], I32)
        key = L.sb("key", [P, T])
        key1 = L.sb("key1", [P, T])
        blk = L.sb("blk", [P, T], BF16)
        blk128 = L.sb("blk128", [P, T], BF16)
        low = L.sb("low", [P, T], BF16)
        rec = L.sb("rec", [P, T * W])
        rec3 = rec[:, :].rearrange("p (t w) -> p t w", w=W)
        empty = L.sb("empty", [P, 16 * W])
        oh_low = [L.sb(f"oh_low{s}", [P, g * P], BF16) for s in range(2)]
        oh_blk = [L.sb(f"oh_blk{s}", [P, g * H], BF16) for s in range(2)]
        zero_b = L.sb("zero_b", [P, P], BF16)
        hist_ps = L.ps("hist_ps", [P, 512])
        loaded, chain, blank, chain2 = L.sem("loaded"), L.sem("chain"), L.sem("blank"), L.sem("chain2")
        oh_made, hist_done = L.sem("oh_made"), L.sem("hist_done")

        def one_hots(s, t):
            nc.vector.tensor_tensor(
                oh_low[s][:, :].rearrange("p (t d) -> p t d", t=g),
                C.ramp_b[:, :].unsqueeze(1).to_broadcast([P, g, P]),
                low[:, ds(t, g)].unsqueeze(2).to_broadcast([P, g, P]), ALU.is_equal)
            return nc.vector.tensor_tensor(
                oh_blk[s][:, :].rearrange("p (t d) -> p t d", t=g),
                C.ramp_b[:, 0:H].unsqueeze(1).to_broadcast([P, g, H]),
                blk[:, ds(t, g)].unsqueeze(2).to_broadcast([P, g, H]), ALU.is_equal)

        with nc.Block() as block:
            @block.sync
            def _(sp):
                sp.dma_start(src_i[:, :], src).then_inc(loaded, 16)
                sp.dma_start(dst_i[:, :], dst).then_inc(loaded, 16)
                if attr is not None:
                    sp.dma_start(rec[:, :], attr).then_inc(loaded, 16)

            @block.gpsimd
            def _(pool):
                nc.gpsimd.memset(zero_b[:, :], 0.0)

            @block.vector
            def _(dve):
                link = serial(dve, chain)
                e3 = empty[:, :].rearrange("p (t w) -> p t w", w=W)
                link(nc.vector.memset(empty[:, :], 0.0))
                link(nc.vector.memset(e3[:, :, 1:2], -1.0))
                dve.wait_ge(loaded, 48 if attr is not None else 32)
                nc.vector.tensor_copy(key[:, :], dst_i[:, :])
                nc.vector.tensor_scalar(blk_i[:, :], dst_i[:, :], 7, None, ALU.arith_shift_right)
                nc.vector.tensor_scalar(low_i[:, :], dst_i[:, :], P - 1, None, ALU.bitwise_and)
                link(nc.vector.tensor_copy(rec3[:, :, 0], src_i[:, :]))
                nc.vector.tensor_copy(blk[:, :], blk_i[:, :])
                nc.vector.tensor_scalar(blk128[:, :], blk_i[:, :], float(P), None, ALU.mult)
                nc.vector.tensor_copy(low[:, :], low_i[:, :])
                link(nc.vector.tensor_scalar(key1[:, :], key[:, :], 1.0, None, ALU.add))
                link(nc.vector.scalar_tensor_tensor(key1[:, :], key[:, :], float(KEY_PAD), key1[:, :],
                                                    ALU.is_lt, ALU.mult))
                link(nc.vector.tensor_scalar(rec3[:, :, 1], key1[:, :], -1.0, None, ALU.add))

        with nc.Block() as block:
            @block.sync
            def _(sp):
                flat = sorted_dram.rearrange("(p k) w -> p (k w)", p=P)
                for k in range(0, KT, 16):
                    n = min(16, KT - k)
                    sp.dma_start(flat[:, k * W:(k + n) * W], empty[:, 0:n * W]).then_inc(blank, 16)
                sp.wait_ge(blank, 16 * -(-KT // 16))

            @block.vector
            def _(dve):
                with dve.Fori(0, T // (2 * g)) as i:
                    for s in range(2):
                        dve.wait_ge(hist_done, i * 2 + s)
                        one_hots(s, i * (2 * g) + s * g).then_inc(oh_made, 1)

            @block.tensor
            def _(pe):
                nc.tensor.matmul(hist_ps[0:H, 0:P], zero_b[:, 0:H], zero_b[:, :], start=True, stop=False)
                pe.sem_inc(hist_done, 1)
                with pe.Fori(0, T // (2 * g)) as i:
                    for s in range(2):
                        pe.wait_ge(oh_made, i * 2 + s + 1)
                        for q in range(g):
                            mm = nc.tensor.matmul(hist_ps[0:H, 0:P], oh_blk[s][:, q * H:(q + 1) * H],
                                                  oh_low[s][:, q * P:(q + 1) * P], start=False, stop=False)
                        mm.then_inc(hist_done, 1)
                nc.tensor.matmul(hist_ps[0:H, 0:P], zero_b[:, 0:H], zero_b[:, :], start=False, stop=True)

        first = L.sb("first", [P, P])
        with Scope(nc, f"base{tag}") as B:
            hist = B.sb("hist", [P, P])
            run = B.sb("run", [P, P])
            zero = B.sb("zero", [P, P])
            room = B.sb("room", [P, 2])
            room_i = B.sb("room_i", [P, 2], I32)
            start_blk = B.sb("start_blk", [P, 1])
            tile_i = B.sb("tile_i", [P, KT], I32)
            tile_f = B.sb("tile_f", [P, KT])
            begun = B.sb("begun", [P, KT])
            ps = B.ps("ps", [P, 512])
            ps2 = B.ps("ps2", [P, 512])
            bchain, tiles_made, roomy, excl, cmp, summed = (
                B.sem(n) for n in ("chain", "tiles_made", "roomy", "excl", "cmp", "summed"))
            with nc.Block() as block:
                @block.gpsimd
                def _(pool):
                    nc.gpsimd.iota(tile_i[:, :], [[P, KT]], base=0, channel_multiplier=0).then_inc(tiles_made, 1)

                @block.vector
                def _(dve):
                    link = serial(dve, bchain)
                    nc.vector.memset(zero[:, :], 0.0)
                    link(nc.vector.tensor_copy(hist[0:H, :], hist_ps[0:H, 0:P]))
                    link(nc.vector.tensor_tensor_scan(run[0:H, :], zero[0:H, :], hist[0:H, :], 0.0,
                                                      ALU.add, ALU.add))
                    link(nc.vector.tensor_scalar(room[0:H, 0:1], run[0:H, P - 1:P], float(P - 1), None, ALU.add))
                    link(nc.vector.tensor_copy(room_i[0:H, 0:1], room[0:H, 0:1]))
                    link(nc.vector.tensor_scalar(room_i[0:H, 1:2], room_i[0:H, 0:1], -P, None, ALU.bitwise_and))
                    nc.vector.tensor_copy(room[0:H, 1:2], room_i[0:H, 1:2]).then_inc(roomy, 1)
                    dve.wait_ge(excl, 1)
                    link(nc.vector.tensor_copy(start_blk[0:H, :], ps[0:H, 0:1]))
                    link(nc.vector.tensor_tensor(run[0:H, :], run[0:H, :], hist[0:H, :], ALU.subtract))
                    link(nc.vector.tensor_scalar(first[0:H, :], run[0:H, :], start_blk[0:H, :], None, ALU.add))
                    dve.wait_ge(tiles_made, 1)
                    link(nc.vector.tensor_copy(tile_f[:, :], tile_i[:, :]))
                    nc.vector.tensor_scalar(begun[0:NB, :], tile_f[0:NB, :], start_blk[0:NB, :], None,
                                            ALU.is_ge).then_inc(cmp, 1)
                    dve.wait_ge(summed, 1)
                    link(nc.vector.tensor_scalar(block_of[0:1, 0:KT], ps2[0:1, 0:KT], -1.0, None, ALU.add))

                @block.tensor
                def _(pe):
                    pe.wait_ge(roomy, 1)
                    nc.tensor.matmul(ps[0:H, 0:1], C.upper[0:H, 0:H], room[0:H, 1:2],
                                     start=True, stop=True).then_inc(excl, 1)
                    pe.wait_ge(cmp, 1)
                    nc.tensor.matmul(ps2[0:1, 0:KT], C.ones[0:NB, 0:1], begun[0:NB, :],
                                     start=True, stop=True).then_inc(summed, 1)

        blkT_ps = [L.ps(f"blkT_ps{s}", [P, 1024], BF16) for s in range(2)]
        row_ps = [L.ps(f"row_ps{s}", [P, 512]) for s in range(2)]
        at_ps = [L.ps(f"at_ps{s}", [P, 512]) for s in range(2)]
        blkT = [L.sb(f"blkT{s}", [P, g * P]) for s in range(2)]
        snap = [L.sb(f"snap{s}", [P, g * P]) for s in range(2)]
        scrap = L.sb("scrap", [P, 2 * g * P])
        place = [L.sb(f"place{s}", [P, 3 * g]) for s in range(2)]
        place_i = [L.sb(f"place_i{s}", [P, g], I32) for s in range(2)]
        rec_out = [L.sb(f"rec_out{s}", [P, g * W]) for s in range(2)]
        oh2, blkT_made, blkT_copied, rows_made, snapped, counted, looked, added, placed, rec_ready, gate = (
            L.sem(n) for n in ("oh2", "blkT_made", "blkT_copied", "rows_made", "snapped", "counted",
                               "looked", "added", "placed", "rec_ready", "gate"))
        sent = L.sems("sent", 2)
        n_it = T // (2 * g)
        with nc.Block() as block:
            @block.vector
            def _(dve):
                dve.sem_inc(placed, 1)
                with dve.Fori(0, n_it) as i:
                    for s in range(2):
                        t = i * (2 * g) + s * g
                        u = i * 2 + s
                        dve.wait_ge(counted, u * g)
                        one_hots(s, t).then_inc(oh2, 1)
                        dve.wait_ge(oh2, u + 1)
                        for q in range(g):
                            dve.wait_ge(rows_made, u + 1)
                            nc.vector.scalar_tensor_tensor(
                                scrap[:, q * P:(q + 1) * P], row_ps[s][:, q * P:(q + 1) * P], key[:, ds(t + q, 1)],
                                C.before[:, :], ALU.is_equal, ALU.mult,
                                accum_out=place[s][:, q:q + 1])
                        for q in range(g):
                            dve.wait_ge(looked, u * g + 2 * g)
                            last = nc.vector.scalar_tensor_tensor(
                                scrap[:, (g + q) * P:(g + q + 1) * P], at_ps[s][:, q * P:(q + 1) * P], 1.0,
                                oh_low[s][:, q * P:(q + 1) * P], ALU.mult, ALU.mult,
                                accum_out=place[s][:, g + q:g + q + 1])
                        last.then_inc(added, 1)
                        dve.wait_ge(added, u + 1)
                        dve.wait_ge(sent[s], i * (16 * g))
                        nc.vector.tensor_tensor(place_i[s][:, :], place[s][:, 0:g], place[s][:, g:2 * g],
                                                ALU.add).then_inc(placed, 1)

            @block.scalar
            def _(act):
                with act.Fori(0, n_it) as i:
                    for s in range(2):
                        t = i * (2 * g) + s * g
                        u = i * 2 + s
                        act.wait_ge(sent[s], i * (16 * g))
                        nc.scalar.activation(rec_out[s][:, :], rec[:, ds(t * W, g * W)], ACT.Copy).then_inc(rec_ready, 1)
                        act.wait_ge(blkT_made, u + 1)
                        act.wait_ge(looked, u * g)
                        nc.scalar.activation(blkT[s][0:H, :], blkT_ps[s][0:H, 0:g * P], ACT.Copy).then_inc(blkT_copied, 1)
                        for q in range(g):
                            act.wait_ge(counted, u * g + q + g)
                            nc.scalar.activation(snap[s][0:H, q * P:(q + 1) * P], hist_ps[0:H, 0:P],
                                                 ACT.Copy).then_inc(snapped, 1)

            @block.tensor
            def _(pe):
                nc.tensor.matmul(hist_ps[0:H, 0:P], C.ident[0:H, 0:H], first[0:H, :],
                                 start=True, stop=False, skip_group_check=True).then_inc(counted, g)
                pe.sem_inc(looked, g)
                with pe.Fori(0, n_it) as i:
                    for s in range(2):
                        t = i * (2 * g) + s * g
                        u = i * 2 + s
                        pe.wait_ge(oh2, u + 1)
                        pe.wait_ge(blkT_copied, u)
                        for q in range(g):
                            mm = nc.tensor.transpose(blkT_ps[s][0:H, q * P:(q + 1) * P],
                                                     oh_blk[s][:, q * H:(q + 1) * H], C.ident_b[:, :])
                        mm.then_inc(blkT_made, 1)
                        pe.wait_ge(placed, u)
                        for q in range(g):
                            out = row_ps[s][:, q * P:(q + 1) * P]
                            nc.tensor.matmul(out, blk128[:, ds(t + q, 1)].to_broadcast([P, P]), C.ident_b[:, :],
                                             start=True, stop=False)
                            mm = nc.tensor.matmul(out, low[:, ds(t + q, 1)].to_broadcast([P, P]), C.ident_b[:, :],
                                                  start=False, stop=True)
                        mm.then_inc(rows_made, 1)
                        pe.wait_ge(blkT_copied, u + 1)
                        for q in range(g):
                            pe.wait_ge(snapped, u * g + q + 1)
                            nc.tensor.matmul(hist_ps[0:H, 0:P], oh_blk[s][:, q * H:(q + 1) * H],
                                             oh_low[s][:, q * P:(q + 1) * P], start=False, stop=False,
                                             skip_group_check=True).then_inc(counted, 1)
                            nc.tensor.matmul(at_ps[s][:, q * P:(q + 1) * P], blkT[s][0:H, q * P:(q + 1) * P],
                                             snap[s][0:H, q * P:(q + 1) * P], start=True, stop=True).then_inc(looked, 1)
                nc.tensor.matmul(hist_ps[0:H, 0:P], zero_b[:, 0:H], zero_b[:, :], start=False, stop=True,
                                 skip_group_check=True)

            @block.gpsimd
            def _(pool):
                with pool.Fori(0, n_it) as i:
                    for s in range(2):
                        u = i * 2 + s
                        pool.wait_ge(placed, u + 2)
                        nc.gpsimd.sem_inc(gate, 1)
                        pool.wait_ge(rec_ready, u + 1)
                        nc.gpsimd.sem_inc(gate, 1)
                        for q in range(g):
                            nc.gpsimd.indirect_dma_start(
                                sorted_dram, bass.IndirectOffsetOnAxis(ap=place_i[s][:, q:q + 1], axis=0),
                                rec_out[s][:, q * W:(q + 1) * W], None).then_inc(sent[s], 16)
                for s in range(2):
                    pool.wait_ge(sent[s], n_it * 16 * g)


def loads(eng, sem, pairs):
    for dst, src in pairs:
        eng.dma_start(dst, src).then_inc(sem, 16)
    return 16 * len(pairs)


class Edges:

    def __init__(self, S, tag, plan):
        KT, R = plan.out, plan.rows
        self.plan = plan
        self.src = S.sb(f"{tag}src", [P, KT], I32)
        self.low = S.sb(f"{tag}low", [P, KT])
        self.low_b = S.sb(f"{tag}low_b", [P, KT], BF16)
        self.src_low = S.sb(f"{tag}src_low", [P, KT], BF16)
        self.src_blk = S.sb(f"{tag}src_blk", [P, KT], BF16)
        self.cut = S.sb(f"{tag}cut", [P, 4 * 512])
        self.cut_back = S.sb(f"{tag}cut_back", [P, 4 * 512])
        self.out_first = S.sb(f"{tag}out_first", [P, 512])
        self.out_last = S.sb(f"{tag}out_last", [P, 512])
        self.joins = S.sb(f"{tag}joins", [4, R + 1])
        self.carry_on = S.sb(f"{tag}carry_on", [4, R])
        self.carry_back = S.sb(f"{tag}carry_back", [4, R])
        self.rec3 = None


def prepare_edges(nc, C, E, tag, rec_dram, rec):
    KT, W, R = E.plan.out, E.plan.width, E.plan.rows
    E.rec3 = rec[:, :].rearrange("p (k w) -> p k w", w=W)
    with Scope(nc, f"prep{tag}") as L:
        a_i = L.sb("a_i", [P, KT], I32)
        b_i = L.sb("b_i", [P, KT], I32)
        b_f = L.sb("b_f", [P, KT])
        dst_s = L.sb("dst_s", [P, 512])
        dst_ps = L.ps("dst_ps", [P, 512])
        ends_ps = L.ps("ends_ps", [4, 512])
        ends = L.sb("ends", [4, 2 * R])
        whole = L.sb("whole", [4, R])
        got, chain, turned, copied, ended = (L.sem(n) for n in ("got", "chain", "turned", "copied", "ended"))
        with nc.Block() as block:
            @block.sync
            def _(sp):
                by_tile = rec_dram.rearrange("(k r) w -> r k w", r=P)
                for k in range(0, KT, 8 * G):
                    n = min(8 * G, KT - k)
                    sp.dma_start(E.rec3[:, k:k + n, :], by_tile[:, k:k + n, :]).then_inc(got, 16)

            @block.tensor
            def _(pe):
                pe.wait_ge(got, 16 * -(-KT // (8 * G)))
                for q in range(G):
                    mm = nc.tensor.transpose(dst_ps[0:R, q * P:(q + 1) * P], E.rec3[:, q::G, 1], C.ident[:, :])
                mm.then_inc(turned, 1)
                pe.wait_ge(copied, 1)
                nc.tensor.transpose(ends_ps[0:4, 0:R], dst_s[0:R, 0:1].to_broadcast([R, 4]), C.ident[0:R, 0:R])
                nc.tensor.transpose(ends_ps[0:4, R:2 * R], dst_s[0:R, 511:512].to_broadcast([R, 4]),
                                    C.ident[0:R, 0:R]).then_inc(ended, 1)

            @block.vector
            def _(dve):
                link = serial(dve, chain)
                dve.wait_ge(got, 16 * -(-KT // (8 * G)))
                nc.vector.tensor_copy(E.src[:, :], E.rec3[:, :, 0])
                link(nc.vector.tensor_copy(a_i[:, :], E.rec3[:, :, 0]))
                link(nc.vector.tensor_scalar(b_i[:, :], a_i[:, :], 7, None, ALU.arith_shift_right))
                link(nc.vector.tensor_copy(E.src_blk[:, :], b_i[:, :]))
                link(nc.vector.tensor_scalar(b_i[:, :], a_i[:, :], P - 1, None, ALU.bitwise_and))
                link(nc.vector.tensor_copy(E.src_low[:, :], b_i[:, :]))
                link(nc.vector.tensor_copy(a_i[:, :], E.rec3[:, :, 1]))
                link(nc.vector.tensor_scalar(b_i[:, :], a_i[:, :], P - 1, None, ALU.bitwise_and))
                link(nc.vector.tensor_copy(E.low[:, :], b_i[:, :]))
                link(nc.vector.tensor_scalar(b_f[:, :], E.rec3[:, :, 1], 0.0, 1024.0, ALU.min, ALU.mult))
                link(nc.vector.tensor_tensor(E.low[:, :], E.low[:, :], b_f[:, :], ALU.add))
                link(nc.vector.tensor_copy(E.low_b[:, :], E.low[:, :]))
                dve.wait_ge(turned, 1)
                nc.vector.tensor_copy(dst_s[0:R, :], dst_ps[0:R, :]).then_inc(copied, 1)
                dve.wait_ge(copied, 1)
                cut = E.cut[0:R, :].rearrange("p (h j) -> p h j", h=4)
                back = E.cut_back[0:R, :].rearrange("p (h j) -> p h j", h=4)
                nc.vector.memset(cut[:, :, 0:1], FAR)
                nc.vector.memset(back[:, :, 511:512], FAR)
                for h in range(4):
                    nc.vector.tensor_tensor(cut[:, h, 1:512], dst_s[0:R, 1:512], dst_s[0:R, 0:511], ALU.not_equal)
                    nc.vector.tensor_tensor(back[:, h, 0:511], dst_s[0:R, 1:512], dst_s[0:R, 0:511], ALU.not_equal)
                nc.vector.tensor_scalar(E.out_first[0:R, :], dst_s[0:R, :], dst_s[0:R, 0:1], FAR,
                                        ALU.not_equal, ALU.mult)
                link(nc.vector.tensor_scalar(E.out_last[0:R, :], dst_s[0:R, :], dst_s[0:R, 511:512], FAR,
                                             ALU.not_equal, ALU.mult))
                nc.vector.tensor_scalar(cut[:, :, 1:512], cut[:, :, 1:512], FAR, None, ALU.mult)
                link(nc.vector.tensor_scalar(back[:, :, 0:511], back[:, :, 0:511], FAR, None, ALU.mult))
                dve.wait_ge(ended, 1)
                link(nc.vector.tensor_copy(ends[:, :], ends_ps[0:4, 0:2 * R]))
                link(nc.vector.memset(E.joins[:, :], FAR))
                link(nc.vector.tensor_tensor(E.joins[:, 1:R], ends[:, 1:R], ends[:, R:2 * R - 1], ALU.not_equal))
                link(nc.vector.tensor_scalar(E.joins[:, 1:R], E.joins[:, 1:R], FAR, None, ALU.mult))
                link(nc.vector.tensor_tensor(whole[:, :], ends[:, 0:R], ends[:, R:2 * R], ALU.not_equal))
                link(nc.vector.tensor_scalar(whole[:, :], whole[:, :], FAR, None, ALU.mult))
                link(nc.vector.tensor_tensor(E.carry_on[:, :], whole[:, :], E.joins[:, 0:R], ALU.add))
                link(nc.vector.tensor_tensor(E.carry_back[:, :], whole[:, :], E.joins[:, 1:R + 1], ALU.add))


def layer_norm(nc, tag, src, dst, width=D, eps=1e-5, scale=None, shift=None):
    with Scope(nc, f"ln{tag}") as L:
        stats = L.sb("stats", [P, NB * 6])
        mean = L.sb("mean", [P, NB])
        gap = L.sb("gap", [P, NB])
        dev = L.sb("dev", [P, NB])
        counted, var_ready, root, chain, normed = (
            L.sem(n) for n in ("counted", "var_ready", "root", "chain", "normed"))
        s6 = stats[:, :].rearrange("p (b t) -> p b t", t=6)
        with nc.Block() as block:
            @block.vector
            def _(dve):
                link = serial(dve, chain)
                with dve.Fori(0, NB) as b:
                    nc.vector.bn_stats(stats[:, ds(b * 6, 6)], src[:, ds(b * width, width)]).then_inc(counted, 1)
                dve.wait_ge(counted, NB)
                nc.vector.tensor_tensor(mean[:, :], s6[:, :, 1], s6[:, :, 4], ALU.add)
                nc.vector.tensor_tensor(dev[:, :], s6[:, :, 2], s6[:, :, 5], ALU.add)
                link(nc.vector.tensor_tensor(gap[:, :], s6[:, :, 1], s6[:, :, 4], ALU.subtract))
                link(nc.vector.tensor_tensor(gap[:, :], gap[:, :], gap[:, :], ALU.mult))
                link(nc.vector.tensor_scalar(dev[:, :], dev[:, :], 1.0 / width, eps, ALU.mult, ALU.add))
                nc.vector.tensor_scalar(mean[:, :], mean[:, :], 0.5, None, ALU.mult)
                nc.vector.scalar_tensor_tensor(dev[:, :], gap[:, :], 0.25, dev[:, :], ALU.mult,
                                               ALU.add).then_inc(var_ready, 1)
                dve.wait_ge(root, 1)
                link(nc.vector.reciprocal(dev[:, :], dev[:, :]))
                with dve.Fori(0, NB) as b:
                    nc.vector.tensor_scalar(dst[:, ds(b * width, width)], src[:, ds(b * width, width)],
                                            mean[:, ds(b, 1)], dev[:, ds(b, 1)],
                                            ALU.subtract, ALU.mult).then_inc(normed, 1)
                if scale is not None:
                    dve.wait_ge(normed, NB)
                    d3 = dst[:, :].rearrange("p (b d) -> p b d", d=width)
                    link(nc.vector.tensor_tensor(d3, d3, scale.unsqueeze(1).to_broadcast([P, NB, width]), ALU.mult))
                    link(nc.vector.tensor_tensor(d3, d3, shift.unsqueeze(1).to_broadcast([P, NB, width]), ALU.add))

            @block.scalar
            def _(act):
                act.wait_ge(var_ready, 1)
                nc.scalar.activation(dev[:, :], dev[:, :], ACT.Sqrt).then_inc(root, 1)


MUL = 64


def equivariant_layer(nc, C, S, a, E, block_of, x, table):
    KT = E.plan.out
    with Scope(nc, "eq") as L:
        z = L.sb("z", [P, NB])
        z8 = L.sb("z8", [P, NB])
        own = L.sb("own", [P, NB * D])
        with Scope(nc, "eqn") as M:
            xn = M.sb("xn", [P, NB * D])
            layer_norm(nc, "eq", x, xn)
            w = M.sb("w", [MUL, 4 * MUL])
            xs = M.sb("xs", [P, D])
            xT = M.sb("xT", [MUL, 4 * P])
            row = [M.sb(f"row{s}", [P, D]) for s in range(2)]
            xT_ps = M.ps("xT_ps", [P, 512])
            o_ps = M.ps("o_ps", [P, 512])
            gate, ld, zed, split, turned, copied, made, owned, rowed, chain = (
                M.sem(n) for n in ("gate", "ld", "zed", "split", "turned", "copied", "made", "owned", "rowed", "chain"))
            stored = M.sems("stored", 2)
            with nc.Block() as block:
                @block.sync
                def _(sp):
                    loads(sp, ld, [(w[:, 0:64], a["L0_gnn_W_sc0"]), (w[:, 64:128], a["L0_gnn_W_lin1_0"]),
                                   (w[:, 128:192], a["L0_gnn_W_sc1"]), (w[:, 192:256], a["L0_gnn_W_lin1_1"]),
                                   (z[:, :], a["node_vec1"])])

                @block.vector
                def _(dve):
                    link = serial(dve, chain)
                    dve.wait_ge(ld, 80)
                    w3 = w[:, :].rearrange("p (g k v) -> p g k v", g=2, k=2)
                    link(nc.vector.tensor_scalar(w3[:, :, 0, :], w3[:, :, 0, :], float(np.float32(np.sin(np.pi / 8))),
                                                 None, ALU.mult))
                    nc.vector.tensor_scalar(z8[:, :], z[:, :], MUL ** -0.5, None, ALU.mult).then_inc(zed, 1)
                    dve.wait_ge(zed, 1)

                    def node(b, s, n, before):
                        dve.wait_ge(made, n + 1)
                        o3 = o_ps[:, :].rearrange("p (j k v) -> p j k v", j=4, k=2)
                        nc.vector.tensor_scalar(own[:, ds(b * D, D)].rearrange("p (j v) -> p j v", j=4),
                                                o3[:, :, 0, :], z8[:, ds(b, 1)], None, ALU.mult).then_inc(owned, 1)
                        dve.wait_ge(stored[s], before)
                        nc.vector.tensor_scalar(row[s][:, :].rearrange("p (j v) -> p j v", j=4),
                                                o3[:, :, 1, :], z8[:, ds(b, 1)], None, ALU.mult).then_inc(rowed, 1)

                    with dve.Fori(0, NB // 2) as i:
                        node(i * 2, 0, i * 2, i * 16)
                        node(i * 2 + 1, 1, i * 2 + 1, i * 16)
                    node(NB - 1, 0, NB - 1, 16 * (NB // 2))

                @block.scalar
                def _(act):
                    with act.Fori(0, NB) as b:
                        act.wait_ge(turned, b)
                        xb = xn[:, ds(b * D, D)]
                        nc.scalar.activation(xs[:, 0:MUL], xb[:, 0:MUL], ACT.Copy)
                        nc.scalar.activation(xs[:, MUL:D].rearrange("p (c u) -> p u c", c=3),
                                             xb[:, MUL:D].rearrange("p (u c) -> p u c", c=3), ACT.Copy).then_inc(split, 1)
                        act.wait_ge(turned, b + 1)
                        act.wait_ge(made, b)
                        nc.scalar.activation(xT[:, :], xT_ps[0:MUL, :], ACT.Copy).then_inc(copied, 1)

                @block.tensor
                def _(pe):
                    pe.wait_ge(ld, 80)
                    pe.wait_ge(zed, 1)
                    with pe.Fori(0, NB) as b:
                        pe.wait_ge(split, b + 1)
                        pe.wait_ge(copied, b)
                        pe.sem_inc(gate, 1)
                        for j in range(4):
                            mm = nc.tensor.transpose(xT_ps[0:MUL, j * P:(j + 1) * P], xs[:, j * MUL:(j + 1) * MUL],
                                                     C.ident[:, :])
                        mm.then_inc(turned, 1)
                        pe.wait_ge(copied, b + 1)
                        pe.wait_ge(rowed, b)
                        for j in range(4):
                            k = 0 if j == 0 else 2 * MUL
                            mm = nc.tensor.matmul(o_ps[:, j * P:(j + 1) * P], xT[:, j * P:(j + 1) * P],
                                                  w[:, k:k + 2 * MUL], start=True, stop=True)
                        mm.then_inc(made, 1)

                @block.gpsimd
                def _(pool):
                    def store(b, s, n):
                        pool.wait_ge(rowed, n + 1)
                        nc.gpsimd.dma_start(table[ds(b * P, P), 0:D], row[s][:, :]).then_inc(stored[s], 16)
                    with pool.Fori(0, NB // 2) as i:
                        store(i * 2, 0, i * 2)
                        store(i * 2 + 1, 1, i * 2 + 1)
                    store(NB - 1, 0, NB - 1)
                    pool.wait_ge(stored[0], 16 * (NB // 2 + 1))
                    pool.wait_ge(stored[1], 16 * (NB // 2))

        acc = L.sb("acc", [P, NB * 512])
        with Scope(nc, "eqe") as M:
            fc0 = M.sb("fc0", [G * 8, G * MUL])
            fc1 = M.sb("fc1", [MUL, 4 * MUL])
            idx = [M.sb(f"idx{s}", [P, G], I32) for s in range(2)]
            got = [M.sb(f"got{s}", [P, G * D]) for s in range(2)]
            attr = [M.sb(f"attr{s}", [P, G * 8]) for s in range(2)]
            attrT = M.sb("attrT", [G * 8, P])
            hid = M.sb("hid", [MUL, G * P])
            pick = M.sb("pick", [P, G * P])
            picks = [M.sb(f"picks{s}", [P, G * 4 * P]) for s in range(2)]
            msg = [M.sb(f"msg{s}", [P, G * 512]) for s in range(2)]
            small_ps = M.ps("small_ps", [P, 512])
            hid_ps = M.ps("hid_ps", [P, 512])
            w_ps = [M.ps(f"w_ps{s}", [P, 1024]) for s in range(2)]
            sum_ps = [M.ps(f"sum_ps{s}", [P, 512]) for s in range(2)]
            ld, ready, chain, idxed, attred, turned, copied, hidden, silued, weighted = (
                M.sem(n) for n in ("ld", "ready", "chain", "idxed", "attred", "turned", "copied", "hidden", "silued",
                                   "weighted"))
            picked, scaled, messaged, summed, added, gate, cleared = (
                M.sem(n) for n in ("picked", "scaled", "messaged", "summed", "added", "gate", "cleared"))
            arrived = M.sems("arrived", 2)
            n_it = KT // (2 * G)
            with nc.Block() as block:
                @block.sync
                def _(sp):
                    sp.wait_ge(cleared, 2)
                    loads(sp, ld, [(fc0[8 * t:8 * t + 8, MUL * t:MUL * t + MUL], a["L0_gnn_fc_w0"]) for t in range(G)]
                          + [(fc1[:, :], a["L0_gnn_fc_w1"])])

                @block.gpsimd
                def _(pool):
                    nc.gpsimd.memset(fc0[:, :], 0.0).then_inc(cleared, 1)
                    with pool.Fori(0, n_it) as i:
                        for s in range(2):
                            u = i * 2 + s
                            pool.wait_ge(messaged, u * G)
                            nc.gpsimd.tensor_copy(idx[s][:, :], E.src[:, ds(u * G, G)]).then_inc(idxed, 1)
                            pool.wait_ge(idxed, u + 1)
                            nc.gpsimd.sem_inc(gate, 1)
                            for t in range(G):
                                nc.gpsimd.indirect_dma_start(
                                    got[s][:, t * D:(t + 1) * D], None, table[:, 0:D],
                                    bass.IndirectOffsetOnAxis(ap=idx[s][:, t:t + 1], axis=0)).then_inc(arrived[s], 16)

                @block.vector
                def _(dve):
                    link = serial(dve, chain)
                    nc.vector.memset(acc[:, :], 0.0).then_inc(cleared, 1)
                    dve.sem_inc(messaged, G)
                    dve.wait_ge(cleared, 2)
                    dve.wait_ge(ld, 16 * (G + 1))
                    link(nc.vector.tensor_scalar(fc1[:, :], fc1[:, :], MUL ** -0.5, None, ALU.mult))
                    nc.vector.tensor_scalar(fc1[:, 3 * MUL:], fc1[:, 3 * MUL:], 3 ** -0.5, None,
                                            ALU.mult).then_inc(ready, 1)
                    dve.wait_ge(ready, 1)
                    with dve.Fori(0, n_it) as i:
                        for s in range(2):
                            u = i * 2 + s
                            blks = [dve.value_load(block_of[0:1, ds(u * G + t, 1)], min_val=0, max_val=NB - 1)
                                    for t in range(G)]
                            dve.wait_ge(scaled, u)
                            nc.vector.tensor_tensor(
                                pick[:, :].rearrange("p (t d) -> p t d", t=G),
                                C.ramp[:, :].unsqueeze(1).to_broadcast([P, G, P]),
                                E.low[:, ds(u * G, G)].unsqueeze(2).to_broadcast([P, G, P]),
                                ALU.is_equal).then_inc(picked, 1)
                            dve.wait_ge(arrived[s], (i + 1) * (16 * G))
                            dve.wait_ge(weighted, u + 1)
                            for t in range(G):
                                src = got[s][:, t * D:(t + 1) * D]
                                w = w_ps[s][:, t * D:(t + 1) * D]
                                out = msg[s][:, t * 512:(t + 1) * 512].rearrange("p (g f) -> p g f", g=2)
                                dve.wait_ge(summed, u * G)
                                nc.vector.tensor_tensor(out[:, :, 0:MUL], w[:, 0:2 * MUL].rearrange("p (g u) -> p g u", g=2),
                                                        src[:, 0:MUL].unsqueeze(1).to_broadcast([P, 2, MUL]), ALU.mult)
                                nc.vector.tensor_tensor(
                                    out[:, :, MUL:].rearrange("p g (c u) -> p g c u", c=3),
                                    w[:, 2 * MUL:].rearrange("p (g u) -> p g u", g=2).unsqueeze(2).to_broadcast([P, 2, 3, MUL]),
                                    src[:, MUL:].rearrange("p (c u) -> p c u", c=3).unsqueeze(1).to_broadcast([P, 2, 3, MUL]),
                                    ALU.mult).then_inc(messaged, 1)
                            for t in range(G):
                                dve.wait_ge(summed, u * G + t + 1 + G)
                                dve.wait_ge(added, u * G + t)
                                dst = acc[:, ds(blks[t] * 512, 512)]
                                nc.vector.tensor_tensor(dst, dst, sum_ps[t % 2][:, :], ALU.add).then_inc(added, 1)

                @block.scalar
                def _(act):
                    with act.Fori(0, n_it) as i:
                        for s in range(2):
                            u = i * 2 + s
                            act.wait_ge(turned, u)
                            nc.scalar.activation(attr[s][:, :].rearrange("p (t f) -> p t f", t=G),
                                                 E.rec3[:, ds(u * G, G), 6:14], ACT.Copy).then_inc(attred, 1)
                            act.wait_ge(turned, u + 1)
                            act.wait_ge(hidden, u)
                            nc.scalar.activation(attrT[:, :], small_ps[0:G * 8, 0:P], ACT.Copy).then_inc(copied, 1)
                            act.wait_ge(hidden, u + 1)
                            act.wait_ge(weighted, u)
                            nc.scalar.activation(hid[:, :], hid_ps[0:MUL, :], ACT.Silu, scale=8 ** -0.5).then_inc(silued, 1)
                            act.wait_ge(picked, u + 1)
                            act.wait_ge(summed, u * G)
                            for t in range(G):
                                for c in range(4):
                                    k = (t * 4 + c) * P
                                    last = nc.scalar.activation(picks[s][:, k:k + P], pick[:, t * P:(t + 1) * P], ACT.Copy,
                                                                scale=E.rec3[:, ds(u * G + t, 1), 2 + c])
                            last.then_inc(scaled, 1)

                @block.tensor
                def _(pe):
                    pe.sem_inc(summed, G)
                    pe.wait_ge(ready, 1)
                    pe.wait_ge(ld, 16 * (G + 1))
                    with pe.Fori(0, n_it) as i:
                        for s in range(2):
                            u = i * 2 + s
                            pe.wait_ge(attred, u + 1)
                            pe.wait_ge(copied, u)
                            nc.tensor.transpose(small_ps[0:G * 8, 0:P], attr[s][:, :], C.ident[:, :]).then_inc(turned, 1)
                            pe.wait_ge(copied, u + 1)
                            pe.wait_ge(silued, u)
                            for t in range(G):
                                mm = nc.tensor.matmul(hid_ps[0:MUL, t * P:(t + 1) * P], fc0[:, t * MUL:(t + 1) * MUL],
                                                      attrT[:, :], start=True, stop=True)
                            mm.then_inc(hidden, 1)
                            pe.wait_ge(silued, u + 1)
                            pe.wait_ge(messaged, u * G)
                            for t in range(G):
                                mm = nc.tensor.matmul(w_ps[s][:, t * D:(t + 1) * D], hid[:, t * P:(t + 1) * P], fc1[:, :],
                                                      start=True, stop=True)
                            mm.then_inc(weighted, 1)
                            pe.wait_ge(scaled, u + 1)
                            for t in range(G):
                                pe.wait_ge(messaged, u * G + t + 1 + G)
                                if s == 0 and t < 2:
                                    pe.wait_ge(added, i * (2 * G) + max(t - 1, 0))
                                else:
                                    pe.wait_ge(added, u * G + t - 1)
                                lhs = [picks[s][:, (t * 4 + c) * P:(t * 4 + c + 1) * P] for c in range(4)]
                                m = msg[s][:, t * 512:(t + 1) * 512]
                                o = sum_ps[t % 2]
                                nc.tensor.matmul(o[:, MUL:5 * MUL], lhs[0], m[:, 0:4 * MUL], start=True, stop=False)
                                for c in range(3):
                                    nc.tensor.matmul(o[:, (5 + c) * MUL:(6 + c) * MUL], lhs[1 + c], m[:, 4 * MUL:5 * MUL],
                                                     start=False, stop=False)
                                    mm = nc.tensor.matmul(o[:, 0:MUL], lhs[1 + c], m[:, (5 + c) * MUL:(6 + c) * MUL],
                                                          start=False, stop=c == 2)
                                mm.then_inc(summed, 1)

        with Scope(nc, "eqo") as M:
            w2 = M.sb("w2", [P, 2 * MUL])
            y = M.sb("y", [P, 512])
            yT = M.sb("yT", [P, 512])
            mixed = M.sb("mixed", [P, D])
            yT_ps = M.ps("yT_ps", [P, 512])
            o_ps = M.ps("o_ps", [P, 512])
            ld, ready, taken, turned, copied, made, mixed_s, outed = (
                M.sem(n) for n in ("ld", "ready", "taken", "turned", "copied", "made", "mixed_s", "outed"))
            with nc.Block() as block:
                @block.sync
                def _(sp):
                    w0, w1 = a["L0_gnn_W_lin2_0"], a["L0_gnn_W_lin2_1"]
                    loads(sp, ld, [(w2[0:64, 0:64], w0[64:128, :]), (w2[64:128, 0:64], w0[0:64, :]),
                                   (w2[0:64, 64:128], w1[64:128, :]), (w2[64:128, 64:128], w1[0:64, :])])

                @block.vector
                def _(dve):
                    dve.wait_ge(ld, 64)
                    k = float(np.float32(np.cos(np.pi / 8))) / np.sqrt(16.0) / np.sqrt(2.0 * MUL)
                    nc.vector.tensor_scalar(w2[:, :], w2[:, :], float(k), None, ALU.mult).then_inc(ready, 1)
                    with dve.Fori(0, NB) as b:
                        dve.wait_ge(made, b + 1)
                        nc.vector.scalar_tensor_tensor(mixed[:, :], o_ps[:, 0:D], z[:, ds(b, 1)], own[:, ds(b * D, D)],
                                                       ALU.mult, ALU.add).then_inc(mixed_s, 1)
                        dve.wait_ge(mixed_s, b + 1)
                        xb = x[:, ds(b * D, D)]
                        nc.vector.tensor_tensor(xb[:, 0:MUL], xb[:, 0:MUL], mixed[:, 0:MUL], ALU.add)
                        x3 = xb[:, MUL:].rearrange("p (u c) -> p u c", c=3)
                        nc.vector.tensor_tensor(x3, x3, mixed[:, MUL:].rearrange("p (c u) -> p u c", c=3),
                                                ALU.add).then_inc(outed, 1)
                        dve.wait_ge(outed, b + 1)

                @block.scalar
                def _(act):
                    with act.Fori(0, NB) as b:
                        act.wait_ge(turned, b)
                        sums = acc[:, ds(b * 512, 512)]
                        nc.scalar.activation(y[:, 0:2 * MUL], sums[:, 0:2 * MUL], ACT.Copy)
                        for g in range(2):
                            last = nc.scalar.activation(
                                y[:, 2 * MUL:].rearrange("p (c g u) -> p c g u", g=2, c=3)[:, :, g, :],
                                sums[:, (2 + 3 * g) * MUL:(5 + 3 * g) * MUL].rearrange("p (c u) -> p c u", c=3), ACT.Copy)
                        last.then_inc(taken, 1)
                        act.wait_ge(turned, b + 1)
                        act.wait_ge(made, b)
                        nc.scalar.activation(yT[:, :], yT_ps[:, :], ACT.Copy).then_inc(copied, 1)

                @block.tensor
                def _(pe):
                    pe.wait_ge(ready, 1)
                    pe.wait_ge(ld, 64)
                    with pe.Fori(0, NB) as b:
                        pe.wait_ge(taken, b + 1)
                        pe.wait_ge(copied, b)
                        for j in range(4):
                            mm = nc.tensor.transpose(yT_ps[:, j * P:(j + 1) * P], y[:, j * P:(j + 1) * P], C.ident[:, :])
                        mm.then_inc(turned, 1)
                        pe.wait_ge(copied, b + 1)
                        pe.wait_ge(mixed_s, b)
                        for j in range(4):
                            mm = nc.tensor.matmul(o_ps[:, j * MUL:(j + 1) * MUL], yT[:, j * P:(j + 1) * P],
                                                  w2[:, 0:MUL] if j == 0 else w2[:, MUL:], start=True, stop=True)
                        mm.then_inc(made, 1)


def broadcast_rows(ap):
    return ap.partition_broadcast(P)


def gating(nc, tag, logits, gates, n):
    with Scope(nc, f"gate{tag}") as L:
        above = L.sb("above", [P, NB * n * n])
        ties = L.sb("ties", [P, NB * n * n])
        early = L.sb("early", [P, n * n])
        rank = L.sb("rank", [P, NB * n])
        top = L.sb("top", [P, NB])
        ramp = L.sb("ramp", [P, n])
        chain, expd, ready, ramped = L.sem("chain"), L.sem("expd"), L.sem("ready"), L.sem("ramped")
        l3 = logits[:, :].rearrange("p (b e) -> p b e", e=n)
        g3 = gates[:, :].rearrange("p (b e) -> p b e", e=n)
        r3 = rank[:, :].rearrange("p (b e) -> p b e", e=n)
        with nc.Block() as block:
            @block.gpsimd
            def _(pool):
                nc.gpsimd.iota(ramp[:, :], [[1, n]], base=0, channel_multiplier=0,
                               allow_small_or_imprecise_dtypes=True).then_inc(ramped, 1)

            @block.vector
            def _(dve):
                link = serial(dve, chain)
                dve.wait_ge(ramped, 1)
                e3 = early[:, :].rearrange("p (e f) -> p e f", e=n)
                link(nc.vector.tensor_tensor(e3, ramp[:, :].unsqueeze(1).to_broadcast([P, n, n]),
                                             ramp[:, :].unsqueeze(2).to_broadcast([P, n, n]), ALU.is_lt))
                link(nc.vector.tensor_reduce(top[:, :], l3, AX.X, ALU.max))
                nc.vector.tensor_tensor(g3, l3, top[:, :].unsqueeze(2).to_broadcast([P, NB, n]),
                                        ALU.subtract).then_inc(ready, 1)
                for e in range(n):
                    for out, op in ((above, ALU.is_gt), (ties, ALU.is_equal)):
                        last = nc.vector.tensor_tensor(
                            out[:, :].rearrange("p (b e f) -> p b e f", e=n, f=n)[:, :, e, :], l3,
                            l3[:, :, e:e + 1].to_broadcast([P, NB, n]), op)
                link(last)
                t3 = ties[:, :].rearrange("p (b k) -> p b k", b=NB)
                link(nc.vector.tensor_tensor(t3, t3, early[:, :].unsqueeze(1).to_broadcast([P, NB, n * n]), ALU.mult))
                link(nc.vector.tensor_tensor(above[:, :], above[:, :], ties[:, :], ALU.add))
                link(nc.vector.tensor_reduce(rank[:, :], above[:, :].rearrange("p (k f) -> p k f", f=n), AX.X, ALU.add))
                dve.wait_ge(expd, 1)
                link(nc.vector.scalar_tensor_tensor(gates[:, :], rank[:, :], 1.5, gates[:, :], ALU.is_lt, ALU.mult))
                link(nc.vector.tensor_reduce(top[:, :], g3, AX.X, ALU.add))
                link(nc.vector.reciprocal(top[:, :], top[:, :]))
                link(nc.vector.tensor_tensor(g3, g3, top[:, :].unsqueeze(2).to_broadcast([P, NB, n]), ALU.mult))

            @block.scalar
            def _(act):
                act.wait_ge(ready, 1)
                nc.scalar.activation(gates[:, :], gates[:, :], ACT.Exp).then_inc(expd, 1)


HID = 512


def experts(nc, C, tag, xn, x, n, a, w1, b1, w2, b2, wr=None, br=None, gates=None):
    KD, KH = D // P, HID // P
    with Scope(nc, f"moe{tag}") as L:
        xnT = L.sb("xnT", [P, KD * NPAD])
        xnT3 = xnT[:, :].rearrange("p (k n) -> p k n", k=KD)
        if gates is None:
            gates = L.sb("gates", [P, NB * n])
            logits = L.sb("logits", [P, NB * n])
        with Scope(nc, f"moet{tag}") as M:
            block_in = M.sb("block_in", [P, D])
            turned = M.sb("turned", [P, D])
            wr_s = M.sb("wr", [P, KD * n])
            br_s = M.sb("br", [P, n])
            t_ps = M.ps("t_ps", [P, 512])
            l_ps = M.ps("l_ps", [P, 512])
            ld, taken, flipped, copied, kept, routed, logged = (
                M.sem(s) for s in ("ld", "taken", "flipped", "copied", "kept", "routed", "logged"))
            with nc.Block() as block:
                @block.sync
                def _(sp):
                    if wr is not None:
                        loads(sp, ld, [(wr_s[:, k * n:(k + 1) * n], a[wr][k * P:(k + 1) * P, :]) for k in range(KD)]
                              + [(br_s[:, :], broadcast_rows(a[br]))])

                @block.scalar
                def _(act):
                    with act.Fori(0, NB) as b:
                        act.wait_ge(flipped, b)
                        nc.scalar.activation(block_in[:, :], xn[:, ds(b * D, D)], ACT.Copy).then_inc(taken, 1)
                        act.wait_ge(flipped, b + 1)
                        act.wait_ge(kept, b)
                        act.wait_ge(routed, b)
                        nc.scalar.activation(turned[:, :], t_ps[:, 0:D], ACT.Copy).then_inc(copied, 1)

                @block.vector
                def _(dve):
                    with dve.Fori(0, NB) as b:
                        dve.wait_ge(copied, b + 1)
                        nc.vector.tensor_copy(xnT3[:, :, ds(b * P, P)],
                                              turned[:, :].rearrange("p (k n) -> p k n", k=KD)).then_inc(kept, 1)
                        if wr is not None:
                            dve.wait_ge(routed, b + 1)
                            nc.vector.tensor_tensor(logits[:, ds(b * n, n)], l_ps[:, 0:n], br_s[:, :],
                                                    ALU.add).then_inc(logged, 1)

                @block.tensor
                def _(pe):
                    if wr is not None:
                        pe.wait_ge(ld, 16 * (KD + 1))
                    with pe.Fori(0, NB) as b:
                        pe.wait_ge(taken, b + 1)
                        pe.wait_ge(copied, b)
                        for k in range(KD):
                            mm = nc.tensor.transpose(t_ps[:, k * P:(k + 1) * P], block_in[:, k * P:(k + 1) * P], C.ident[:, :])
                        mm.then_inc(flipped, 1)
                        pe.wait_ge(copied, b + 1)
                        if wr is not None:
                            pe.wait_ge(logged, b)
                            for k in range(KD):
                                mm = nc.tensor.matmul(l_ps[:, 0:n], turned[:, k * P:(k + 1) * P],
                                                      wr_s[:, k * n:(k + 1) * n], start=k == 0, stop=k == KD - 1)
                            mm.then_inc(routed, 1)
                        else:
                            pe.sem_inc(routed, 1)
        if wr is not None:
            gating(nc, tag, logits, gates, n)
        with Scope(nc, f"moeb{tag}") as M:
            g_in = M.sb("g_in", [P, n])
            gT = M.sb("gT", [n, P])
            b2_s = M.sb("b2", [n, D])
            t_ps = M.ps("t_ps", [P, 512])
            o_ps = M.ps("o_ps", [P, 512])
            ld, gate, taken, flipped, copied, made, added = (
                M.sem(s) for s in ("ld", "gate", "taken", "flipped", "copied", "made", "added"))
            with nc.Block() as block:
                @block.sync
                def _(sp):
                    sp.dma_start(b2_s[:, :], a[b2]).then_inc(ld, 16)

                @block.scalar
                def _(act):
                    with act.Fori(0, NB) as b:
                        act.wait_ge(flipped, b)
                        nc.scalar.activation(g_in[:, :], gates[:, ds(b * n, n)], ACT.Copy).then_inc(taken, 1)
                        act.wait_ge(flipped, b + 1)
                        act.wait_ge(made, b)
                        nc.scalar.activation(gT[:, :], t_ps[0:n, 0:P], ACT.Copy).then_inc(copied, 1)

                @block.vector
                def _(dve):
                    with dve.Fori(0, NB) as b:
                        dve.wait_ge(made, b + 1)
                        xb = x[:, ds(b * D, D)]
                        nc.vector.tensor_tensor(xb, xb, o_ps[:, 0:D], ALU.add).then_inc(added, 1)

                @block.tensor
                def _(pe):
                    pe.wait_ge(ld, 16)
                    with pe.Fori(0, NB) as b:
                        pe.wait_ge(taken, b + 1)
                        pe.wait_ge(copied, b)
                        pe.sem_inc(gate, 1)
                        nc.tensor.transpose(t_ps[0:n, 0:P], g_in[:, :], C.ident[:, :]).then_inc(flipped, 1)
                        pe.wait_ge(copied, b + 1)
                        pe.wait_ge(added, b)
                        pe.sem_inc(gate, 1)
                        nc.tensor.matmul(o_ps[:, 0:D], gT[:, :], b2_s[:, :], start=True, stop=True).then_inc(made, 1)
        BG = 5
        NG = BG * P
        groups = NB // BG
        half = NG // 2
        with Scope(nc, f"moee{tag}") as M:
            w1_s = [M.sb(f"w1_{s}", [P, KD * HID]) for s in range(2)]
            w2_s = [M.sb(f"w2_{s}", [P, KH * D]) for s in range(2)]
            b1_s = [M.sb(f"b1_{s}", [P, KH]) for s in range(2)]
            h = [M.sb(f"h{s}", [P, KH * NG]) for s in range(2)]
            h_ps = [M.ps(f"h_ps{s}", [P, 512]) for s in range(4)]
            y_ps = [M.ps(f"y_ps{s}", [P, 512]) for s in range(2)]
            gelued, up, down, added, done = (
                M.sem(s) for s in ("gelued", "up", "down", "added", "done"))
            ld = M.sems("ld", 2)
            per = groups * KH * 2
            with nc.Block() as block:
                @block.sync
                def _(sp):
                    with sp.Fori(0, n // 2) as i:
                        for s in range(2):
                            sp.wait_ge(done, i * 2 + s)
                            e = i * 2 + s
                            sp.dma_start(b1_s[s][:, :], a[b1][:, ds(e * KH, KH)]).then_inc(ld[s], 16)
                            sp.dma_start(w1_s[s][:, :].rearrange("p (k h) -> p k h", k=KD),
                                         a[w1][ds(e, 1), :, :].rearrange("o (k p) h -> p (o k) h", p=P)).then_inc(ld[s], 16)
                            sp.dma_start(w2_s[s][:, :].rearrange("p (k d) -> p k d", k=KH),
                                         a[w2][ds(e, 1), :, :].rearrange("o (k p) d -> p (o k) d", p=P)).then_inc(ld[s], 16)

                @block.tensor
                def _(pe):
                    pe.sem_inc(done, 1)
                    with pe.Fori(0, n // 2) as i:
                        for s in range(2):
                            pe.wait_ge(ld[s], i * 48 + 48)

                            def first_layer(gr):
                                for m in range(KH):
                                    for r in range(2):
                                        c = s * per + gr * KH * 2 + m * 2 + r
                                        pe.wait_ge(gelued, i * (2 * per) + c + 1)
                                        for k in range(KD):
                                            mm = nc.tensor.matmul(
                                                h_ps[c % 4][:, 0:half],
                                                w1_s[s][:, k * HID + m * P:k * HID + (m + 1) * P],
                                                xnT[:, k * NPAD + gr * NG + r * half:k * NPAD + gr * NG + (r + 1) * half],
                                                start=k == 0, stop=k == KD - 1)
                                        mm.then_inc(up, 1)

                            def second_layer(gr):
                                v = s * groups + gr
                                pe.wait_ge(gelued, i * (2 * per) + (v + 1) * KH * 2 + 4)
                                for j in range(BG):
                                    c = v * BG + j
                                    pe.wait_ge(added, i * (2 * groups * BG) + c)
                                    for m in range(KH):
                                        mm = nc.tensor.matmul(
                                            y_ps[c % 2][:, 0:D], h[v % 2][:, m * NG + j * P:m * NG + (j + 1) * P],
                                            w2_s[s][:, m * D:(m + 1) * D], start=m == 0, stop=m == KH - 1)
                                    mm.then_inc(down, 1)

                            first_layer(0)
                            for gr in range(1, groups):
                                first_layer(gr)
                                second_layer(gr - 1)
                            second_layer(groups - 1)
                            pe.wait_ge(down, i * (2 * groups * BG) + (s + 1) * groups * BG)
                            pe.sem_inc(done, 1)

                @block.scalar
                def _(act):
                    act.sem_inc(gelued, 4)
                    with act.Fori(0, n // 2) as i:
                        for s in range(2):
                            act.wait_ge(ld[s], i * 48 + 48)
                            for gr in range(groups):
                                v = s * groups + gr
                                if v >= 2:
                                    act.wait_ge(down, i * (2 * groups * BG) + (v - 1) * BG)
                                elif v == 1:
                                    act.wait_ge(down, i * (2 * groups * BG))
                                for m in range(KH):
                                    for r in range(2):
                                        c = v * KH * 2 + m * 2 + r
                                        act.wait_ge(up, i * (2 * per) + c + 1)
                                        nc.scalar.activation(
                                            h[v % 2][:, m * NG + r * half:m * NG + (r + 1) * half],
                                            h_ps[c % 4][:, 0:half], ACT.Gelu,
                                            bias=b1_s[s][:, m:m + 1]).then_inc(gelued, 1)

                @block.vector
                def _(dve):
                    dve.sem_inc(added, 1)
                    with dve.Fori(0, n // 2) as i:
                        for s in range(2):
                            for b in range(NB):
                                c = s * NB + b
                                dve.wait_ge(down, i * (2 * NB) + c + 1)
                                if b == 0:
                                    dve.wait_ge(added, i * (2 * NB) + c + 1)
                                xb = x[:, b * D:(b + 1) * D]
                                nc.vector.scalar_tensor_tensor(
                                    xb, y_ps[c % 2][:, 0:D], gates[:, ds(i * 2 + (b * n + s), 1)], xb,
                                    ALU.mult, ALU.add).then_inc(added, 1)


def turned_one_hots(nc, C, tag, E, columns, out_dram):
    KT = E.plan.out
    with Scope(nc, f"oht{tag}") as L:
        ps = [L.ps(f"ps{s}", [P, 512]) for s in range(2)]
        oh = [L.sb(f"oh{s}", [P, G * P], BF16) for s in range(2)]
        rows, compared = L.sem("rows"), L.sem("compared")
        put = L.sems("put", 2)
        n_it = KT // (2 * G)
        with nc.Block() as block:
            @block.tensor
            def _(pe):
                with pe.Fori(0, n_it) as i:
                    for s in range(2):
                        u = i * 2 + s
                        pe.wait_ge(compared, u)
                        for t in range(G):
                            mm = nc.tensor.matmul(ps[s][:, t * P:(t + 1) * P],
                                                  columns[:, ds(u * G + t, 1)].to_broadcast([P, P]), C.ident_b[:, :],
                                                  start=True, stop=True)
                        mm.then_inc(rows, 1)

            @block.vector
            def _(dve):
                dve.sem_inc(compared, 1)
                with dve.Fori(0, n_it) as i:
                    for s in range(2):
                        u = i * 2 + s
                        dve.wait_ge(rows, u + 1)
                        dve.wait_ge(put[s], i * 16)
                        nc.vector.tensor_scalar(oh[s][:, :], ps[s][:, :], C.part[:, :], None,
                                                ALU.is_equal).then_inc(compared, 1)

            @block.sync
            def _(sp):
                with sp.Fori(0, n_it) as i:
                    for s in range(2):
                        u = i * 2 + s
                        sp.wait_ge(compared, u + 2)
                        sp.dma_start(out_dram[:, ds(u * (G * P), G * P)], oh[s][:, :]).then_inc(put[s], 16)
                for s in range(2):
                    sp.wait_ge(put[s], 16 * n_it)


def split_bf16(nc, link, src, parts, rest):
    for j, part in enumerate(parts):
        link(nc.vector.tensor_copy(part, src if j == 0 else rest))
        if j < 2:
            link(nc.vector.tensor_tensor(rest, src if j == 0 else rest, part, ALU.subtract))


def segment_softmax(nc, C, tag, E, scores):
    KT, R = E.plan.out, E.plan.rows
    with Scope(nc, f"seg{tag}") as L:
        upto = L.sb("upto", [P, 2048])
        peak = L.sb("peak", [P, 2048])
        chain, leaky, flipped, ends, ended, carried, carry_t, spread, shifted, back, expd = (
            L.sem(n) for n in ("chain", "leaky", "flipped", "ends", "ended", "carried", "carry_t", "spread",
                               "shifted", "back", "expd"))
        s3 = scores[:, :].rearrange("p (k h) -> p k h", h=4)
        rows = L.sb("rows", [4, 2 * P])
        runs = L.sb("runs", [4, 2 * P])
        carry = L.sb("carry", [P, 8])
        with Scope(nc, f"sega{tag}") as M:
            e_ps = M.ps("e_ps", [P, 2048])
            small = M.ps("small", [P, 512])
            with nc.Block() as block:
                @block.vector
                def _(dve):
                    link = serial(dve, chain)
                    nc.vector.scalar_tensor_tensor(scores[:, :], scores[:, :], 0.2, scores[:, :], ALU.mult,
                                                   ALU.max).then_inc(leaky, 1)
                    dve.wait_ge(flipped, 1)
                    link(nc.vector.tensor_tensor_scan(upto[0:R, :], E.cut[0:R, :], e_ps[0:R, :], FAR, ALU.add, ALU.max))
                    nc.vector.tensor_tensor_scan(peak[0:R, ::-1], E.cut_back[0:R, ::-1], upto[0:R, ::-1], FAR,
                                                 ALU.add, ALU.max).then_inc(ends, 1)
                    dve.wait_ge(ended, 1)
                    link(nc.vector.tensor_copy(rows[:, 0:2 * R], small[0:4, 0:2 * R]))
                    nc.vector.memset(runs[:, 0:1], FAR)
                    link(nc.vector.memset(runs[:, 2 * R - 1:2 * R], FAR))
                    link(nc.vector.tensor_tensor_scan(runs[:, 1:R], E.carry_on[:, 0:R - 1], rows[:, R:2 * R - 1], FAR,
                                                      ALU.add, ALU.max))
                    link(nc.vector.tensor_tensor_scan(runs[:, 2 * R - 2:R - 1:-1], E.carry_back[:, R - 1:0:-1],
                                                      rows[:, R - 1:0:-1], FAR, ALU.add, ALU.max))
                    link(nc.vector.tensor_tensor(runs[:, 0:R], runs[:, 0:R], E.joins[:, 0:R], ALU.add))
                    nc.vector.tensor_tensor(runs[:, R:2 * R], runs[:, R:2 * R], E.joins[:, 1:R + 1],
                                            ALU.add).then_inc(carried, 1)
                    dve.wait_ge(carry_t, 1)
                    link(nc.vector.tensor_copy(carry[0:R, :], small[0:R, 384:392]))
                    for k, out in ((0, E.out_first), (4, E.out_last)):
                        for h in range(4):
                            part = peak[0:R, h * 512:(h + 1) * 512]
                            last = nc.vector.scalar_tensor_tensor(part, out[0:R, :], carry[0:R, k + h:k + h + 1], part,
                                                                  ALU.add, ALU.max)
                        link(last)
                    nc.vector.tensor_tensor(upto[0:R, :], e_ps[0:R, :], peak[0:R, :], ALU.subtract).then_inc(shifted, 1)

                @block.tensor
                def _(pe):
                    pe.wait_ge(leaky, 1)
                    for h in range(4):
                        for q in range(G):
                            mm = nc.tensor.transpose(e_ps[0:R, h * 512 + q * P:h * 512 + (q + 1) * P], s3[:, q::G, h],
                                                     C.ident[:, :])
                    mm.then_inc(flipped, 1)
                    pe.wait_ge(ends, 1)
                    p3 = peak[0:R, :].rearrange("p (h j) -> p h j", h=4)
                    nc.tensor.transpose(small[0:4, 0:R], p3[:, :, 0], C.ident[0:R, 0:R])
                    nc.tensor.transpose(small[0:4, R:2 * R], p3[:, :, 511], C.ident[0:R, 0:R]).then_inc(ended, 1)
                    pe.wait_ge(carried, 1)
                    nc.tensor.transpose(small[0:R, 384:388], runs[:, 0:R], C.ident[0:4, 0:4])
                    nc.tensor.transpose(small[0:R, 388:392], runs[:, R:2 * R], C.ident[0:4, 0:4]).then_inc(carry_t, 1)
        with Scope(nc, f"segb{tag}") as M:
            b_ps = M.ps("b_ps", [P, 2048])
            with nc.Block() as block:
                @block.tensor
                def _(pe):
                    for h in range(4):
                        for q in range(G):
                            mm = nc.tensor.transpose(b_ps[:, (q * 4 + h) * P:(q * 4 + h) * P + R],
                                                     upto[0:R, h * 512 + q * P:h * 512 + (q + 1) * P], C.ident[0:R, 0:R])
                    mm.then_inc(back, 1)

                @block.scalar
                def _(act):
                    act.wait_ge(back, 1)
                    for q in range(G):
                        nc.scalar.activation(
                            s3[:, q::G, :].rearrange("p r h -> p h r"),
                            b_ps[:, q * 512:(q + 1) * 512].rearrange("p (h r) -> p h r", h=4)[:, :, 0:R], ACT.Exp)


def gat_layer(nc, C, S, a, n, E, block_of, h_in, acc, table, oht_src, oht_dst):
    KT, DW = E.plan.out, D + 4
    with Scope(nc, f"gat{n}") as L:
        score = L.sb("score", [P, NB * 8])
        src3 = L.sb("src3", [P, 3 * NB * 4], BF16)
        dst3 = L.sb("dst3", [P, 3 * NB * 4], BF16)
        with Scope(nc, f"gatn{n}") as M:
            w = M.sb("w", [P, 2 * (D + 8)])
            w3 = w[:, :].rearrange("p (k f) -> p k f", k=2)
            att = M.sb("att", [P, 2 * D])
            prod = M.sb("prod", [P, 4 * D])
            block_in = M.sb("block_in", [P, D])
            hT = M.sb("hT", [P, D])
            row = [M.sb(f"row{s}", [P, D]) for s in range(2)]
            rest = M.sb("rest", [P, NB * 4])
            t_ps = M.ps("t_ps", [P, 512])
            o_ps = M.ps("o_ps", [P, 512])
            ld, chain, ready, taken, flipped, copied, made, rowed = (
                M.sem(s) for s in ("ld", "chain", "ready", "taken", "flipped", "copied", "made", "rowed"))
            stored = M.sems("stored", 2)
            with nc.Block() as block:
                @block.sync
                def _(sp):
                    loads(sp, ld, [(w3[:, k, 0:D], a[f"L1_gnn_W{n}"][k * P:(k + 1) * P, :]) for k in range(2)]
                          + [(att[:, 0:D], broadcast_rows(a[f"L1_gnn_a_src{n}"].rearrange("h c -> (h c)"))),
                             (att[:, D:], broadcast_rows(a[f"L1_gnn_a_dst{n}"].rearrange("h c -> (h c)")))])

                    def store(b, s, k):
                        sp.wait_ge(rowed, k + 1)
                        sp.dma_start(table[ds(b * P, P), 0:D], row[s][:, :]).then_inc(stored[s], 16)
                    with sp.Fori(0, NB // 2) as i:
                        store(i * 2, 0, i * 2)
                        store(i * 2 + 1, 1, i * 2 + 1)
                    store(NB - 1, 0, NB - 1)
                    sp.wait_ge(stored[0], 16 * (NB // 2 + 1))
                    sp.wait_ge(stored[1], 16 * (NB // 2))

                @block.vector
                def _(dve):
                    link = serial(dve, chain)
                    dve.wait_ge(ld, 64)
                    p4 = prod[:, :].rearrange("p (k g f) -> p k g f", k=2, g=2)
                    for k in range(2):
                        last = nc.vector.tensor_tensor(p4[:, k, :, :], w3[:, k, 0:D].unsqueeze(1).to_broadcast([P, 2, D]),
                                                       att[:, :].rearrange("p (g f) -> p g f", g=2), ALU.mult)
                    link(last)
                    for k in range(2):
                        last = nc.vector.tensor_reduce(
                            w3[:, k, D:D + 8], prod[:, k * 2 * D:(k + 1) * 2 * D].rearrange("p (g c) -> p g c", c=64),
                            AX.X, ALU.add)
                    last.then_inc(ready, 1)

                    def node(b, s, k, before):
                        dve.wait_ge(made, k + 1)
                        dve.wait_ge(stored[s], before)
                        nc.vector.tensor_copy(row[s][:, :], o_ps[:, 0:D])
                        nc.vector.tensor_copy(score[:, ds(b * 8, 8)], o_ps[:, D:D + 8]).then_inc(rowed, 1)
                    with dve.Fori(0, NB // 2) as i:
                        node(i * 2, 0, i * 2, i * 16)
                        node(i * 2 + 1, 1, i * 2 + 1, i * 16)
                    node(NB - 1, 0, NB - 1, 16 * (NB // 2))
                    dve.wait_ge(rowed, NB)
                    sc3 = score[:, :].rearrange("p (b k) -> p b k", k=8)
                    for k, out in ((0, src3), (4, dst3)):
                        parts = [out[:, j * NB * 4:(j + 1) * NB * 4].rearrange("p (b h) -> p b h", h=4) for j in range(3)]
                        split_bf16(nc, link, sc3[:, :, k:k + 4], parts, rest[:, :].rearrange("p (b h) -> p b h", h=4))

                @block.scalar
                def _(act):
                    with act.Fori(0, NB) as b:
                        act.wait_ge(flipped, b)
                        nc.scalar.activation(block_in[:, :], h_in[:, ds(b * D, D)], ACT.Copy).then_inc(taken, 1)
                        act.wait_ge(flipped, b + 1)
                        act.wait_ge(made, b)
                        nc.scalar.activation(hT[:, :], t_ps[:, 0:D], ACT.Copy).then_inc(copied, 1)

                @block.tensor
                def _(pe):
                    pe.wait_ge(ready, 1)
                    pe.wait_ge(ld, 64)
                    with pe.Fori(0, NB) as b:
                        pe.wait_ge(taken, b + 1)
                        pe.wait_ge(copied, b)
                        for k in range(2):
                            mm = nc.tensor.transpose(t_ps[:, k * P:(k + 1) * P], block_in[:, k * P:(k + 1) * P], C.ident[:, :])
                        mm.then_inc(flipped, 1)
                        pe.wait_ge(copied, b + 1)
                        pe.wait_ge(rowed, b)
                        for k in range(2):
                            mm = nc.tensor.matmul(o_ps[:, 0:D + 8], hT[:, k * P:(k + 1) * P], w3[:, k, :],
                                                  start=k == 0, stop=k == 1)
                        mm.then_inc(made, 1)

        edge = L.sb("edge", [P, KT * 4])
        with Scope(nc, f"gats{n}") as M:
            os_ = [M.sb(f"os{s}", [P, G * P], BF16) for s in range(2)]
            od_ = [M.sb(f"od{s}", [P, G * P], BF16) for s in range(2)]
            ohb = M.sb("ohb", [P, G * NB])
            prod = M.sb("prod", [P, G * NB * 4])
            part = M.sb("part", [P, G * 4])
            r_ps = [M.ps(f"r_ps{s}", [P, 512]) for s in range(2)]
            d_ps = [M.ps(f"d_ps{s}", [P, 512]) for s in range(2)]
            looked, chosen, multed, reduced, summed = (
                M.sem(s) for s in ("looked", "chosen", "multed", "reduced", "summed"))
            came = M.sems("came", 2)
            n_it = KT // (2 * G)
            with nc.Block() as block:
                @block.sync
                def _(sp):
                    with sp.Fori(0, n_it) as i:
                        for s in range(2):
                            u = i * 2 + s
                            sp.wait_ge(looked, u)
                            sp.dma_start(os_[s][:, :], oht_src[:, ds(u * (G * P), G * P)]).then_inc(came[s], 16)
                            sp.dma_start(od_[s][:, :], oht_dst[:, ds(u * (G * P), G * P)]).then_inc(came[s], 16)

                @block.tensor
                def _(pe):
                    pe.sem_inc(looked, 1)
                    with pe.Fori(0, n_it) as i:
                        for s in range(2):
                            u = i * 2 + s
                            pe.wait_ge(came[s], i * 32 + 32)
                            pe.wait_ge(summed, u)
                            for t in range(G):
                                for j in range(3):
                                    nc.tensor.matmul(r_ps[s][:, t * NB * 4:(t + 1) * NB * 4], os_[s][:, t * P:(t + 1) * P],
                                                     src3[:, j * NB * 4:(j + 1) * NB * 4], start=j == 0, stop=j == 2)
                            for t in range(G):
                                blk = pe.value_load(block_of[0:1, ds(u * G + t, 1)], min_val=0, max_val=NB - 1)
                                for j in range(3):
                                    mm = nc.tensor.matmul(d_ps[s][:, t * 4:(t + 1) * 4], od_[s][:, t * P:(t + 1) * P],
                                                          dst3[:, ds(blk * 4 + j * NB * 4, 4)], start=j == 0, stop=j == 2)
                            mm.then_inc(looked, 1)

                @block.vector
                def _(dve):
                    dve.sem_inc(summed, 1)
                    with dve.Fori(0, n_it) as i:
                        for s in range(2):
                            u = i * 2 + s
                            dve.wait_ge(multed, u)
                            nc.vector.tensor_tensor(
                                ohb[:, :].rearrange("p (t b) -> p t b", t=G),
                                C.ramp[:, 0:NB].unsqueeze(1).to_broadcast([P, G, NB]),
                                E.src_blk[:, ds(u * G, G)].unsqueeze(2).to_broadcast([P, G, NB]),
                                ALU.is_equal).then_inc(chosen, 1)
                            dve.wait_ge(chosen, u + 1)
                            dve.wait_ge(looked, u + 2)
                            dve.wait_ge(reduced, u)
                            nc.vector.tensor_tensor(
                                prod[:, :].rearrange("p (b h) -> p b h", h=4),
                                r_ps[s][:, 0:G * NB * 4].rearrange("p (b h) -> p b h", h=4),
                                ohb[:, :].unsqueeze(2).to_broadcast([P, G * NB, 4]), ALU.mult).then_inc(multed, 1)
                            dve.wait_ge(multed, u + 1)
                            nc.vector.tensor_reduce(part[:, :].rearrange("p (t h) -> p t h", t=G),
                                                    prod[:, :].rearrange("p (t b h) -> p t h b", t=G, h=4),
                                                    AX.X, ALU.add).then_inc(reduced, 1)
                            dve.wait_ge(reduced, u + 1)
                            nc.vector.tensor_tensor(edge[:, ds(u * (G * 4), G * 4)], part[:, :], d_ps[s][:, 0:G * 4],
                                                    ALU.add).then_inc(summed, 1)

        segment_softmax(nc, C, f"{n}", E, edge)

        with Scope(nc, f"gata{n}") as M:
            idx = [M.sb(f"idx{s}", [P, G], I32) for s in range(2)]
            got = [M.sb(f"got{s}", [P, G * D]) for s in range(2)]
            msg = [M.sb(f"msg{s}", [P, G * DW]) for s in range(2)]
            pick = [M.sb(f"pick{s}", [P, G * P]) for s in range(2)]
            sum_ps = [M.ps(f"sum_ps{s}", [P, 512]) for s in range(4)]
            idxed, gate, weighed, copied, picked, summed, added, cleared = (
                M.sem(s) for s in ("idxed", "gate", "weighed", "copied", "picked", "summed", "added", "cleared"))
            arrived = M.sems("arrived", 2)
            n_it = KT // (2 * G)
            with nc.Block() as block:
                @block.gpsimd
                def _(pool):
                    with pool.Fori(0, n_it) as i:
                        for s in range(2):
                            u = i * 2 + s
                            pool.wait_ge(weighed, u)
                            nc.gpsimd.tensor_copy(idx[s][:, :], E.src[:, ds(u * G, G)]).then_inc(idxed, 1)
                            pool.wait_ge(idxed, u + 1)
                            nc.gpsimd.sem_inc(gate, 1)
                            for t in range(G):
                                nc.gpsimd.indirect_dma_start(
                                    got[s][:, t * D:(t + 1) * D], None, table[:, 0:D],
                                    bass.IndirectOffsetOnAxis(ap=idx[s][:, t:t + 1], axis=0)).then_inc(arrived[s], 16)

                @block.scalar
                def _(act):
                    with act.Fori(0, n_it) as i:
                        for s in range(2):
                            u = i * 2 + s
                            act.wait_ge(summed, u)
                            nc.scalar.activation(
                                msg[s][:, :].rearrange("p (t f) -> p t f", t=G)[:, :, D:DW],
                                edge[:, ds(u * (G * 4), G * 4)].rearrange("p (t h) -> p t h", t=G),
                                ACT.Copy).then_inc(copied, 1)

                @block.vector
                def _(dve):
                    nc.vector.memset(acc[:, :], 0.0).then_inc(cleared, 1)
                    dve.sem_inc(weighed, 1)
                    dve.wait_ge(cleared, 1)
                    with dve.Fori(0, n_it) as i:
                        for s in range(2):
                            u = i * 2 + s
                            blks = [dve.value_load(block_of[0:1, ds(u * G + t, 1)], min_val=0, max_val=NB - 1)
                                    for t in range(G)]
                            dve.wait_ge(summed, u)
                            nc.vector.tensor_tensor(
                                pick[s][:, :].rearrange("p (t d) -> p t d", t=G),
                                C.ramp[:, :].unsqueeze(1).to_broadcast([P, G, P]),
                                E.low[:, ds(u * G, G)].unsqueeze(2).to_broadcast([P, G, P]),
                                ALU.is_equal).then_inc(picked, 1)
                            dve.wait_ge(arrived[s], (i + 1) * (16 * G))
                            m3 = msg[s][:, :].rearrange("p (t f) -> p t f", t=G)
                            for t in range(G):
                                last = nc.vector.tensor_tensor(
                                    m3[:, t, 0:D].rearrange("p (h c) -> p h c", h=4),
                                    got[s][:, t * D:(t + 1) * D].rearrange("p (h c) -> p h c", h=4),
                                    edge[:, ds(u * (G * 4) + t * 4, 4)].unsqueeze(2).to_broadcast([P, 4, 64]), ALU.mult)
                            last.then_inc(weighed, 1)
                            dve.wait_ge(summed, u + 2)
                            for t in range(G):
                                dve.wait_ge(added, u * G + t)
                                dst = acc[:, ds(blks[t] * DW, DW)]
                                nc.vector.tensor_tensor(dst, dst, sum_ps[t][:, 0:DW], ALU.add).then_inc(added, 1)

                @block.tensor
                def _(pe):
                    pe.sem_inc(summed, 1)
                    with pe.Fori(0, n_it) as i:
                        for s in range(2):
                            u = i * 2 + s
                            pe.wait_ge(picked, u + 1)
                            pe.wait_ge(copied, u + 1)
                            pe.wait_ge(weighed, u + 2)
                            pe.wait_ge(added, u * G)
                            for t in range(G):
                                mm = nc.tensor.matmul(sum_ps[t][:, 0:DW], pick[s][:, t * P:(t + 1) * P],
                                                      msg[s][:, t * DW:(t + 1) * DW], start=True, stop=True)
                            mm.then_inc(summed, 1)


def gat_output(nc, a, n, acc, h, x):
    DW = D + 4
    with Scope(nc, f"gato{n}") as L:
        bias = L.sb("bias", [P, D])
        inv = L.sb("inv", [P, NB * 4])
        norm = L.sb("norm", [P, NB])
        ld, chain, squares, root = L.sem("ld"), L.sem("chain"), L.sem("squares"), L.sem("root")
        a3 = acc[:, :].rearrange("p (b f) -> p b f", f=DW)
        h3 = h[:, :].rearrange("p (b d) -> p b d", d=D)
        i3 = inv[:, :].rearrange("p (b h) -> p b h", h=4)
        with nc.Block() as block:
            @block.sync
            def _(sp):
                sp.dma_start(bias[:, :], broadcast_rows(a[f"L1_gnn_b{n}"])).then_inc(ld, 16)

            @block.vector
            def _(dve):
                link = serial(dve, chain)
                link(nc.vector.tensor_scalar(i3, a3[:, :, D:DW], 1e-16, None, ALU.add))
                link(nc.vector.reciprocal(inv[:, :], inv[:, :]))
                for hd in range(4):
                    c = slice(hd * 64, (hd + 1) * 64)
                    last = nc.vector.tensor_tensor(h3[:, :, c], a3[:, :, c], i3[:, :, hd:hd + 1].to_broadcast([P, NB, 64]),
                                                   ALU.mult)
                link(last)
                dve.wait_ge(ld, 16)
                link(nc.vector.tensor_tensor(h3, h3, bias[:, :].unsqueeze(1).to_broadcast([P, NB, D]), ALU.add))
                if n < 3:
                    link(nc.vector.tensor_scalar(h[:, :], h[:, :], 0.0, None, ALU.max))
                else:
                    sq = acc[:, 0:NB * D]
                    link(nc.vector.tensor_tensor(sq, h[:, :], h[:, :], ALU.mult))
                    nc.vector.tensor_reduce(norm[:, :], sq.rearrange("p (b d) -> p b d", d=D), AX.X,
                                            ALU.add).then_inc(squares, 1)
                    dve.wait_ge(root, 1)
                    link(nc.vector.tensor_scalar(norm[:, :], norm[:, :], 1e-12, None, ALU.max))
                    link(nc.vector.reciprocal(norm[:, :], norm[:, :]))
                    link(nc.vector.tensor_tensor(h3, h3, norm[:, :].unsqueeze(2).to_broadcast([P, NB, D]), ALU.mult))
                    link(nc.vector.tensor_tensor(x[:, :], x[:, :], h[:, :], ALU.add))

            if n == 3:
                @block.scalar
                def _(act):
                    act.wait_ge(squares, 1)
                    nc.scalar.activation(norm[:, :], norm[:, :], ACT.Sqrt).then_inc(root, 1)


def router(nc, C, S, a, E, block_of, xn, table, oht_dst, gates):
    KT, F = E.plan.out, 20
    with Scope(nc, "rt") as L:
        dst3 = L.sb("dst3", [P, 3 * NB * 4], BF16)
        with Scope(nc, "rtn") as M:
            w = M.sb("w", [P, 2 * 16])
            att = M.sb("att", [P, 32])
            all_in = M.sb("all_in", [P, NB * 24])
            prod = M.sb("prod", [P, NB * 16])
            rest = M.sb("rest", [P, NB * 4])
            block_in = M.sb("block_in", [P, D])
            hT = M.sb("hT", [P, D])
            t_ps = M.ps("t_ps", [P, 512])
            o_ps = M.ps("o_ps", [P, 512])
            ld, chain, taken, flipped, copied, made, kept, ready, stored = (
                M.sem(s) for s in ("ld", "chain", "taken", "flipped", "copied", "made", "kept", "ready", "stored"))
            a3 = all_in[:, :].rearrange("p (b f) -> p b f", f=24)
            with nc.Block() as block:
                @block.sync
                def _(sp):
                    loads(sp, ld, [(w[:, k * 16:(k + 1) * 16], a["L1_ffn_W_gat"][k * P:(k + 1) * P, :]) for k in range(2)]
                          + [(att[:, 0:16], broadcast_rows(a["L1_ffn_att_src"].rearrange("h c -> (h c)"))),
                             (att[:, 16:], broadcast_rows(a["L1_ffn_att_dst"].rearrange("h c -> (h c)")))])
                    sp.wait_ge(ready, 1)
                    sp.dma_start(table.rearrange("(b p) f -> p b f", p=P), a3[:, :, 0:F]).then_inc(stored, 16)
                    sp.wait_ge(stored, 16)

                @block.scalar
                def _(act):
                    with act.Fori(0, NB) as b:
                        act.wait_ge(flipped, b)
                        nc.scalar.activation(block_in[:, :], xn[:, ds(b * D, D)], ACT.Copy).then_inc(taken, 1)
                        act.wait_ge(flipped, b + 1)
                        act.wait_ge(made, b)
                        nc.scalar.activation(hT[:, :], t_ps[:, 0:D], ACT.Copy).then_inc(copied, 1)

                @block.tensor
                def _(pe):
                    pe.wait_ge(ld, 64)
                    with pe.Fori(0, NB) as b:
                        pe.wait_ge(taken, b + 1)
                        pe.wait_ge(copied, b)
                        for k in range(2):
                            mm = nc.tensor.transpose(t_ps[:, k * P:(k + 1) * P], block_in[:, k * P:(k + 1) * P], C.ident[:, :])
                        mm.then_inc(flipped, 1)
                        pe.wait_ge(copied, b + 1)
                        pe.wait_ge(kept, b)
                        for k in range(2):
                            mm = nc.tensor.matmul(o_ps[:, 0:16], hT[:, k * P:(k + 1) * P], w[:, k * 16:(k + 1) * 16],
                                                  start=k == 0, stop=k == 1)
                        mm.then_inc(made, 1)

                @block.vector
                def _(dve):
                    link = serial(dve, chain)
                    with dve.Fori(0, NB) as b:
                        dve.wait_ge(made, b + 1)
                        nc.vector.tensor_copy(all_in[:, ds(b * 24, 16)], o_ps[:, 0:16]).then_inc(kept, 1)
                    dve.wait_ge(kept, NB)
                    dve.wait_ge(ld, 64)
                    p3 = prod[:, :].rearrange("p (b f) -> p b f", f=16)
                    for g in range(2):
                        link(nc.vector.tensor_tensor(p3, a3[:, :, 0:16], att[:, g * 16:(g + 1) * 16].unsqueeze(1)
                                                     .to_broadcast([P, NB, 16]), ALU.mult))
                        link(nc.vector.tensor_reduce(a3[:, :, 16 + 4 * g:20 + 4 * g],
                                                     prod[:, :].rearrange("p (b h c) -> p b h c", h=4, c=4), AX.X, ALU.add))
                    dve.sem_inc(ready, 1)
                    parts = [dst3[:, j * NB * 4:(j + 1) * NB * 4].rearrange("p (b h) -> p b h", h=4) for j in range(3)]
                    split_bf16(nc, link, a3[:, :, 20:24], parts, rest[:, :].rearrange("p (b h) -> p b h", h=4))

        msg = L.sb("msg", [P, KT * F])
        edge = L.sb("edge", [P, KT * 4])
        with Scope(nc, "rts") as M:
            idx = [M.sb(f"idx{s}", [P, G], I32) for s in range(2)]
            got = [M.sb(f"got{s}", [P, G * F]) for s in range(2)]
            od_ = [M.sb(f"od{s}", [P, G * P], BF16) for s in range(2)]
            d_ps = [M.ps(f"d_ps{s}", [P, 512]) for s in range(2)]
            idxed, gate, looked, taken = (M.sem(s) for s in ("idxed", "gate", "looked", "taken"))
            arrived, came = M.sems("arrived", 2), M.sems("came", 2)
            n_it = KT // (2 * G)
            with nc.Block() as block:
                @block.gpsimd
                def _(pool):
                    with pool.Fori(0, n_it) as i:
                        for s in range(2):
                            u = i * 2 + s
                            pool.wait_ge(taken, u)
                            nc.gpsimd.tensor_copy(idx[s][:, :], E.src[:, ds(u * G, G)]).then_inc(idxed, 1)
                            pool.wait_ge(idxed, u + 1)
                            nc.gpsimd.sem_inc(gate, 1)
                            for t in range(G):
                                nc.gpsimd.indirect_dma_start(
                                    got[s][:, t * F:(t + 1) * F], None, table,
                                    bass.IndirectOffsetOnAxis(ap=idx[s][:, t:t + 1], axis=0)).then_inc(arrived[s], 16)

                @block.sync
                def _(sp):
                    with sp.Fori(0, n_it) as i:
                        for s in range(2):
                            u = i * 2 + s
                            sp.wait_ge(looked, u)
                            sp.dma_start(od_[s][:, :], oht_dst[:, ds(u * (G * P), G * P)]).then_inc(came[s], 16)

                @block.tensor
                def _(pe):
                    pe.sem_inc(looked, 1)
                    with pe.Fori(0, n_it) as i:
                        for s in range(2):
                            u = i * 2 + s
                            pe.wait_ge(came[s], i * 16 + 16)
                            pe.wait_ge(taken, u)
                            for t in range(G):
                                blk = pe.value_load(block_of[0:1, ds(u * G + t, 1)], min_val=0, max_val=NB - 1)
                                for j in range(3):
                                    mm = nc.tensor.matmul(d_ps[s][:, t * 4:(t + 1) * 4], od_[s][:, t * P:(t + 1) * P],
                                                          dst3[:, ds(blk * 4 + j * NB * 4, 4)], start=j == 0, stop=j == 2)
                            mm.then_inc(looked, 1)

                @block.vector
                def _(dve):
                    dve.sem_inc(taken, 1)
                    with dve.Fori(0, n_it) as i:
                        for s in range(2):
                            u = i * 2 + s
                            dve.wait_ge(arrived[s], (i + 1) * (16 * G))
                            nc.vector.tensor_copy(msg[:, ds(u * (G * F), G * F)], got[s][:, :])
                            dve.wait_ge(looked, u + 2)
                            nc.vector.tensor_tensor(
                                edge[:, ds(u * (G * 4), G * 4)].rearrange("p (t h) -> p t h", t=G),
                                got[s][:, :].rearrange("p (t f) -> p t f", t=G)[:, :, 16:20],
                                d_ps[s][:, 0:G * 4].rearrange("p (t h) -> p t h", t=G), ALU.add).then_inc(taken, 1)

        segment_softmax(nc, C, "r", E, edge)

        acc = L.sb("acc", [P, NB * F])
        with Scope(nc, "rta") as M:
            pick = [M.sb(f"pick{s}", [P, G * P]) for s in range(2)]
            sum_ps = [M.ps(f"sum_ps{s}", [P, 512]) for s in range(2)]
            chain, ready, picked, summed, added = (M.sem(s) for s in ("chain", "ready", "picked", "summed", "added"))
            m3 = msg[:, :].rearrange("p (k f) -> p k f", f=F)
            e3 = edge[:, :].rearrange("p (k h) -> p k h", h=4)
            n_it = KT // (2 * G)
            with nc.Block() as block:
                @block.vector
                def _(dve):
                    link = serial(dve, chain)
                    nc.vector.memset(acc[:, :], 0.0)
                    for hd in range(4):
                        c = slice(hd * 4, hd * 4 + 4)
                        nc.vector.tensor_tensor(m3[:, :, c], m3[:, :, c], e3[:, :, hd:hd + 1].to_broadcast([P, KT, 4]),
                                                ALU.mult)
                    link(nc.vector.tensor_copy(m3[:, :, 16:20], e3))
                    dve.sem_inc(ready, 1)
                    with dve.Fori(0, n_it) as i:
                        for s in range(2):
                            u = i * 2 + s
                            blks = [dve.value_load(block_of[0:1, ds(u * G + t, 1)], min_val=0, max_val=NB - 1)
                                    for t in range(G)]
                            dve.wait_ge(summed, u)
                            nc.vector.tensor_tensor(
                                pick[s][:, :].rearrange("p (t d) -> p t d", t=G),
                                C.ramp[:, :].unsqueeze(1).to_broadcast([P, G, P]),
                                E.low[:, ds(u * G, G)].unsqueeze(2).to_broadcast([P, G, P]),
                                ALU.is_equal).then_inc(picked, 1)
                            dve.wait_ge(summed, u + 2)
                            for t in range(G):
                                dve.wait_ge(added, u * G + t)
                                dst = acc[:, ds(blks[t] * F, F)]
                                nc.vector.tensor_tensor(dst, dst, sum_ps[s][:, t * F:(t + 1) * F], ALU.add).then_inc(added, 1)

                @block.tensor
                def _(pe):
                    pe.sem_inc(summed, 1)
                    pe.wait_ge(ready, 1)
                    with pe.Fori(0, n_it) as i:
                        for s in range(2):
                            u = i * 2 + s
                            pe.wait_ge(picked, u + 1)
                            if s == 0:
                                pe.wait_ge(added, u * G)
                            else:
                                pe.wait_ge(added, i * (2 * G))
                            for t in range(G):
                                mm = nc.tensor.matmul(sum_ps[s][:, t * F:(t + 1) * F], pick[s][:, t * P:(t + 1) * P],
                                                      msg[:, ds((u * G + t) * F, F)], start=True, stop=True)
                            mm.then_inc(summed, 1)
        with Scope(nc, "rto") as M:
            rows = M.sb("rows", [P, 48])
            inv = M.sb("inv", [P, NB * 4])
            agg = M.sb("agg", [P, NB * 16])
            norm = M.sb("norm", [P, NB * 16])
            logits = M.sb("logits", [P, NB * 4])
            ld, chain = M.sem("ld"), M.sem("chain")
            a3 = acc[:, :].rearrange("p (b f) -> p b f", f=F)
            g3 = agg[:, :].rearrange("p (b f) -> p b f", f=16)
            i3 = inv[:, :].rearrange("p (b h) -> p b h", h=4)
            with nc.Block() as block:
                @block.sync
                def _(sp):
                    loads(sp, ld, [(rows[:, 0:16], broadcast_rows(a["L1_ffn_b_gat"])),
                                   (rows[:, 16:32], broadcast_rows(a["L1_ffn_ln_gamma"])),
                                   (rows[:, 32:48], broadcast_rows(a["L1_ffn_ln_beta"]))])
                    sp.wait_ge(ld, 48)

                @block.vector
                def _(dve):
                    link = serial(dve, chain)
                    link(nc.vector.tensor_scalar(i3, a3[:, :, 16:20], 1e-16, None, ALU.add))
                    link(nc.vector.reciprocal(inv[:, :], inv[:, :]))
                    for hd in range(4):
                        c = slice(hd * 4, hd * 4 + 4)
                        last = nc.vector.tensor_tensor(g3[:, :, c], a3[:, :, c], i3[:, :, hd:hd + 1].to_broadcast([P, NB, 4]),
                                                       ALU.mult)
                    link(last)
                    dve.wait_ge(ld, 48)
                    link(nc.vector.tensor_tensor(g3, g3, rows[:, 0:16].unsqueeze(1).to_broadcast([P, NB, 16]), ALU.add))
            layer_norm(nc, "rt", agg, norm, width=16, scale=rows[:, 16:32], shift=rows[:, 32:48])
            with nc.Block() as block:
                @block.vector
                def _(dve):
                    link = serial(dve, chain, 7 - 7 + 4)
                    link(nc.vector.tensor_reduce(logits[:, :].rearrange("p (b e) -> p b e", e=4),
                                                 norm[:, :].rearrange("p (b h e) -> p b e h", h=4, e=4), AX.X, ALU.add))
                    link(nc.vector.tensor_scalar(logits[:, :], logits[:, :], 0.25, None, ALU.mult))
            gating(nc, "rt", logits, gates, 4)


def load_nodes(nc, x_in, x):
    full = N // P
    with Scope(nc, "nodes") as L:
        zeroed, got = L.sem("zeroed"), L.sem("got")
        with nc.Block() as block:
            @block.vector
            def _(dve):
                nc.vector.memset(x[:, full * D:], 0.0).then_inc(zeroed, 1)

            @block.sync
            def _(sp):
                sp.dma_start(x[:, 0:full * D].rearrange("p (b d) -> p b d", d=D),
                             x_in[0:full * P, :].rearrange("(b p) d -> p b d", p=P)).then_inc(got, 16)
                sp.wait_ge(zeroed, 1)
                sp.dma_start(x[0:N - full * P, full * D:], x_in[full * P:N, :]).then_inc(got, 16)
                sp.wait_ge(got, 32)


def store_nodes(nc, x, out):
    full = N // P
    with Scope(nc, "out") as L:
        put = L.sem("put")
        with nc.Block() as block:
            @block.sync
            def _(sp):
                sp.dma_start(out[0:full * P, :].rearrange("(b p) d -> p b d", p=P),
                             x[:, 0:full * D].rearrange("p (b d) -> p b d", d=D)).then_inc(put, 16)
                sp.dma_start(out[full * P:N, :], x[0:N - full * P, full * D:]).then_inc(put, 16)
                sp.wait_ge(put, 32)


GNN = edge_plan(53125 + 625, 16)
ROUTE = edge_plan(32768 + N, 2)


def program(nc, a, out, stop=9):
    with Scope(nc, "all") as S:
        C = make_constants(nc, S)
        x = S.sb("x", [P, NB * D])
        load_nodes(nc, a["x"], x)
        gnn_sorted = nc.dram_tensor("gnn_sorted", [GNN.out * P, GNN.width], F32).ap()
        route_sorted = nc.dram_tensor("route_sorted", [ROUTE.out * P, ROUTE.width], F32).ap()
        table = nc.dram_tensor("table", [NPAD, D], F32).ap()
        route_table = nc.dram_tensor("route_table", [NPAD, 20], F32).ap()
        oht_src = nc.dram_tensor("oht_src", [P, GNN.out * P], BF16).ap()
        oht_dst = nc.dram_tensor("oht_dst", [P, GNN.out * P], BF16).ap()
        block_of = S.sb("block_of", [1, GNN.out], I32)
        if stop in (0, 1, 2, 9):
            sort_edges(nc, C, GNN, "g", a["gnn_src"], a["gnn_dst"], a["gnn_attr"], gnn_sorted, block_of)
            with Scope(nc, "gnn") as T:
                E = Edges(T, "g", GNN)
                with Scope(nc, "recs") as U:
                    rec = U.sb("rec", [P, GNN.out * GNN.width])
                    prepare_edges(nc, C, E, "g", gnn_sorted, rec)
                    equivariant_layer(nc, C, T, a, E, block_of, x, table)
                if stop >= 1:
                    with Scope(nc, "ffn0") as U:
                        xn = U.sb("xn", [P, NB * D])
                        rows = U.sb("rows", [P, 2 * D])
                        load_rows(nc, "ffn0", rows, [a["L0_ffn_gamma"], a["L0_ffn_beta"]])
                        layer_norm(nc, "f0", x, xn)
                        layer_norm(nc, "f1", xn, xn, scale=rows[:, 0:D], shift=rows[:, D:])
                        experts(nc, C, "0", xn, x, 8, a, "L0_ffn_W1", "L0_ffn_b1", "L0_ffn_W2", "L0_ffn_b2",
                                wr="L0_ffn_Wr", br="L0_ffn_br")
                if stop >= 2:
                    with Scope(nc, "gats") as U:
                        h = U.sb("h", [P, NB * D])
                        acc = U.sb("acc", [P, NB * (D + 4)])
                        layer_norm(nc, "g", x, h)
                        turned_one_hots(nc, C, "s", E, E.src_low, oht_src)
                        turned_one_hots(nc, C, "d", E, E.low_b, oht_dst)
                        for n in (1, 2, 3):
                            gat_layer(nc, C, U, a, n, E, block_of, h, acc, table, oht_src, oht_dst)
                            gat_output(nc, a, n, acc, h, x)
        if stop >= 3:
            with Scope(nc, "route") as T:
                xn = T.sb("xn", [P, NB * D])
                gates = T.sb("gates", [P, NB * 4])
                layer_norm(nc, "r", x, xn)
                with Scope(nc, "routes") as U:
                    sort_edges(nc, C, ROUTE, "r", a["route_src"], a["route_dst"], None, route_sorted, block_of)
                    E = Edges(U, "r", ROUTE)
                    rec = U.sb("rec", [P, ROUTE.out * ROUTE.width])
                    prepare_edges(nc, C, E, "r", route_sorted, rec)
                    turned_one_hots(nc, C, "r", E, E.low_b, oht_dst)
                    router(nc, C, U, a, E, block_of, xn, route_table, oht_dst, gates)
                experts(nc, C, "1", xn, x, 4, a, "L1_ffn_W1", "L1_ffn_b1", "L1_ffn_W2", "L1_ffn_b2", gates=gates)
        store_nodes(nc, x, out)


def load_rows(nc, tag, rows, vectors):
    with Scope(nc, f"rows{tag}") as L:
        ld = L.sem("ld")
        with nc.Block() as block:
            @block.sync
            def _(sp):
                sp.wait_ge(ld, loads(sp, ld, [(rows[:, k * D:(k + 1) * D], broadcast_rows(v))
                                              for k, v in enumerate(vectors)]))


def cut_edges(plan, src, dst, loops):
    fill = plan.tiles * P - plan.edges
    loops = np.arange(loops, dtype=np.int32)
    return (np.concatenate([src, loops, np.zeros(fill, np.int32)]).reshape(P, -1),
            np.concatenate([dst, loops, np.full(fill, KEY_PAD, np.int32)]).reshape(P, -1))


def layout(inputs):
    a = {k: np.ascontiguousarray(v) for k, v in inputs.items()}
    src, dst = a.pop("src"), a.pop("dst")
    e4, e8 = a.pop("edge_attr_4"), a.pop("edge_attr_8")
    a["gnn_src"], a["gnn_dst"] = cut_edges(GNN, src, dst, 625)
    route = a.pop("L1_ffn_edge_index")
    a["route_src"], a["route_dst"] = cut_edges(ROUTE, route[0], route[1], N)
    attr = np.zeros((GNN.tiles * P, GNN.width), np.float32)
    attr[:len(src), 2:6] = e4
    attr[:len(src), 6:14] = e8
    a["gnn_attr"] = attr.reshape(P, -1)
    z = np.zeros((NPAD, 1), np.float32)
    z[:N] = a["node_vec1"]
    a["node_vec1"] = np.ascontiguousarray(z.reshape(NB, P).T)
    for b in ("L0_ffn_b1", "L1_ffn_b1"):
        a[b] = np.ascontiguousarray(a[b].reshape(-1, P).T)
    return a


def kernel(**inputs):
    import concourse.bacc as _bacc
    from concourse.bass_utils import run_bass_kernel_spmd as _run

    arrays = {f"in_{k}": v for k, v in layout(inputs).items()}
    nc = _bacc.Bacc("TRN2", target_bir_lowering=False, num_devices=1)
    a = {k[3:]: nc.dram_tensor(k, v.shape, mybir.dt.from_np(v.dtype), kind="ExternalInput").ap()
         for k, v in arrays.items()}
    out = nc.dram_tensor("out_0", (N, D), F32, kind="ExternalOutput").ap()
    program(nc, a, out)
    r = _run(nc, [arrays], core_ids=[0])
    return r.results[0]["out_0"]
```

```python
import numpy as np
from contextlib import ExitStack
from collections import namedtuple

import concourse.bass as bass
from concourse import mybir

F32 = mybir.dt.float32
BF16 = mybir.dt.bfloat16
I32 = mybir.dt.int32
ALU = mybir.AluOpType
ACT = mybir.ActivationFunctionType
AX = mybir.AxisListType
ds = bass.ds

P = 128
N = 3125
D = 256
NB = -(-N // P)
NPAD = NB * P
SORT_G = 3
G = 4
LAG = 2
RING = 4
FAR = -1.0e30
KEY_PAD = NPAD


Plan = namedtuple("Plan", "edges tiles out width rows")
Constants = namedtuple("Constants", "ident ident_b ramp ramp_b part before upper ones")


def edge_plan(edges, width):
    step = RING * SORT_G
    tiles = -(-(-(-edges // P)) // step) * step
    fill = tiles * P - edges
    worst = (edges + NB * (P - 1)) // P + -(-fill // P)
    out = -(-worst // (RING * G)) * RING * G
    return Plan(edges, tiles, out, width, out // G)


def serial(eng, sem, base=0):
    n = [0]

    def step(ins):
        ins.then_inc(sem, 1)
        n[0] += 1
        eng.wait_ge(sem, base + n[0])
    return step


def there(v, groups):
    return not isinstance(v, int) or 0 <= v < groups


def after(eng, sem, count):
    if not isinstance(count, int) or count > 0:
        eng.wait_ge(sem, count)


def run_steps(eng, step, groups, ahead):
    n_it = groups // RING
    for u in range(-ahead, RING):
        step(u, u % RING, u // RING)
    with eng.Fori(1, n_it - 1) as i:
        for s in range(RING):
            step(i * RING + s, s, i)
    for s in range(RING):
        step(groups - RING + s, s, n_it - 1)


def load_blocks(eng, regs, ap):
    eng.load(regs, ap)
    return [eng.snap(r, min_val=0, max_val=NB - 1) for r in regs]


class Scope:

    def __init__(self, nc, name):
        self.nc, self.name, self.ctx, self.used = nc, name, ExitStack(), []

    def __enter__(self):
        self.ctx.__enter__()
        return self

    def __exit__(self, *a):
        if self.used and a[0] is None:
            self.nc.clear_and_free_semaphores(self.used)
            self.nc.all_engine_barrier()
        return self.ctx.__exit__(*a)

    def sb(self, name, shape, dt=F32):
        return self.ctx.enter_context(self.nc.sbuf_tensor(f"{self.name}_{name}", shape, dt))

    def ps(self, name, shape, dt=F32):
        return self.ctx.enter_context(self.nc.psum_tensor(f"{self.name}_{name}", shape, dt))

    def sem(self, name):
        self.used.append(self.nc.alloc_semaphore(f"{self.name}_{name}"))
        return self.used[-1]

    def sems(self, name, n):
        return [self.sem(f"{name}{i}") for i in range(n)]


def make_constants(nc, S):
    c = Constants(
        ident=S.sb("ident", [P, P]), ident_b=S.sb("ident_b", [P, P], BF16),
        ramp=S.sb("ramp", [P, P]), ramp_b=S.sb("ramp_b", [P, P], BF16),
        part=S.sb("part", [P, 1]), before=S.sb("before", [P, P]), upper=S.sb("upper", [P, P]),
        ones=S.sb("ones", [P, 1]))
    with Scope(nc, "const") as L:
        ramp_i = L.sb("ramp_i", [P, P], I32)
        part_i = L.sb("part_i", [P, 1], I32)
        made = L.sem("made")
        chain = L.sem("chain")
        with nc.Block() as block:
            @block.gpsimd
            def _(pool):
                nc.gpsimd.iota(ramp_i[:, :], [[1, P]], base=0, channel_multiplier=0).then_inc(made, 1)
                nc.gpsimd.iota(part_i[:, :], [[0, 1]], base=0, channel_multiplier=1).then_inc(made, 1)

            @block.vector
            def _(dve):
                link = serial(dve, chain)
                dve.wait_ge(made, 2)
                nc.vector.memset(c.ones[:, :], 1.0)
                link(nc.vector.tensor_copy(c.ramp[:, :], ramp_i[:, :]))
                link(nc.vector.tensor_copy(c.ramp_b[:, :], ramp_i[:, :]))
                link(nc.vector.tensor_copy(c.part[:, :], part_i[:, :]))
                link(nc.vector.tensor_scalar(c.ident[:, :], c.ramp[:, :], c.part[:, :], None, ALU.is_equal))
                link(nc.vector.tensor_scalar(c.before[:, :], c.ramp[:, :], c.part[:, :], None, ALU.is_lt))
                link(nc.vector.tensor_scalar(c.upper[:, :], c.ramp[:, :], c.part[:, :], None, ALU.is_gt))
                link(nc.vector.tensor_copy(c.ident_b[:, :], c.ident[:, :]))
    return c


def sort_edges(nc, C, plan, tag, src, dst, attr, sorted_dram, block_of):
    T, KT, W, g = plan.tiles, plan.out, plan.width, SORT_G
    H = NB + 1
    with Scope(nc, f"sort{tag}") as L:
        src_i = L.sb("src_i", [P, T], I32)
        dst_i = L.sb("dst_i", [P, T], I32)
        blk_i = L.sb("blk_i", [P, T], I32)
        low_i = L.sb("low_i", [P, T], I32)
        key = L.sb("key", [P, T])
        key1 = L.sb("key1", [P, T])
        blk = L.sb("blk", [P, T], BF16)
        blk128 = L.sb("blk128", [P, T], BF16)
        low = L.sb("low", [P, T], BF16)
        rec = L.sb("rec", [P, T * W])
        rec3 = rec[:, :].rearrange("p (t w) -> p t w", w=W)
        empty = L.sb("empty", [P, 16 * W])
        oh_low = [L.sb(f"oh_low{s}", [P, g * P], BF16) for s in range(RING)]
        oh_blk = [L.sb(f"oh_blk{s}", [P, g * H], BF16) for s in range(RING)]
        zero_b = L.sb("zero_b", [P, P], BF16)
        hist_ps = L.ps("hist_ps", [P, 512])
        loaded, chain, blank, chain2 = L.sem("loaded"), L.sem("chain"), L.sem("blank"), L.sem("chain2")
        oh_made, hist_done = L.sem("oh_made"), L.sem("hist_done")

        def one_hots(s, t):
            nc.vector.tensor_tensor(
                oh_low[s][:, :].rearrange("p (t d) -> p t d", t=g),
                C.ramp_b[:, :].unsqueeze(1).to_broadcast([P, g, P]),
                low[:, ds(t, g)].unsqueeze(2).to_broadcast([P, g, P]), ALU.is_equal)
            return nc.vector.tensor_tensor(
                oh_blk[s][:, :].rearrange("p (t d) -> p t d", t=g),
                C.ramp_b[:, 0:H].unsqueeze(1).to_broadcast([P, g, H]),
                blk[:, ds(t, g)].unsqueeze(2).to_broadcast([P, g, H]), ALU.is_equal)

        with nc.Block() as block:
            @block.sync
            def _(sp):
                sp.dma_start(src_i[:, :], src).then_inc(loaded, 16)
                sp.dma_start(dst_i[:, :], dst).then_inc(loaded, 16)
                if attr is not None:
                    sp.dma_start(rec[:, :], attr).then_inc(loaded, 16)

            @block.gpsimd
            def _(pool):
                nc.gpsimd.memset(zero_b[:, :], 0.0)

            @block.vector
            def _(dve):
                link = serial(dve, chain)
                e3 = empty[:, :].rearrange("p (t w) -> p t w", w=W)
                link(nc.vector.memset(empty[:, :], 0.0))
                link(nc.vector.memset(e3[:, :, 1:2], -1.0))
                dve.wait_ge(loaded, 48 if attr is not None else 32)
                nc.vector.tensor_copy(key[:, :], dst_i[:, :])
                nc.vector.tensor_scalar(blk_i[:, :], dst_i[:, :], 7, None, ALU.arith_shift_right)
                nc.vector.tensor_scalar(low_i[:, :], dst_i[:, :], P - 1, None, ALU.bitwise_and)
                link(nc.vector.tensor_copy(rec3[:, :, 0], src_i[:, :]))
                nc.vector.tensor_copy(blk[:, :], blk_i[:, :])
                nc.vector.tensor_scalar(blk128[:, :], blk_i[:, :], float(P), None, ALU.mult)
                nc.vector.tensor_copy(low[:, :], low_i[:, :])
                link(nc.vector.tensor_scalar(key1[:, :], key[:, :], 1.0, None, ALU.add))
                link(nc.vector.scalar_tensor_tensor(key1[:, :], key[:, :], float(KEY_PAD), key1[:, :],
                                                    ALU.is_lt, ALU.mult))
                link(nc.vector.tensor_scalar(rec3[:, :, 1], key1[:, :], -1.0, None, ALU.add))

        with nc.Block() as block:
            @block.sync
            def _(sp):
                flat = sorted_dram.rearrange("(p k) w -> p (k w)", p=P)
                for k in range(0, KT, 16):
                    n = min(16, KT - k)
                    sp.dma_start(flat[:, k * W:(k + n) * W], empty[:, 0:n * W]).then_inc(blank, 16)
                sp.wait_ge(blank, 16 * -(-KT // 16))

            @block.vector
            def _(dve):
                with dve.Fori(0, T // (RING * g)) as i:
                    for s in range(RING):
                        dve.wait_ge(hist_done, i * RING + s + 1)
                        one_hots(s, i * (RING * g) + s * g).then_inc(oh_made, 1)

            @block.tensor
            def _(pe):
                nc.tensor.matmul(hist_ps[0:H, 0:P], zero_b[:, 0:H], zero_b[:, :], start=True, stop=False)
                pe.sem_inc(hist_done, RING)
                with pe.Fori(0, T // (RING * g)) as i:
                    for s in range(RING):
                        pe.wait_ge(oh_made, i * RING + s + 1)
                        for q in range(g):
                            mm = nc.tensor.matmul(hist_ps[0:H, 0:P], oh_blk[s][:, q * H:(q + 1) * H],
                                                  oh_low[s][:, q * P:(q + 1) * P], start=False, stop=False)
                        mm.then_inc(hist_done, 1)
                nc.tensor.matmul(hist_ps[0:H, 0:P], zero_b[:, 0:H], zero_b[:, :], start=False, stop=True)

        first = L.sb("first", [P, P])
        with Scope(nc, f"base{tag}") as B:
            hist = B.sb("hist", [P, P])
            run = B.sb("run", [P, P])
            zero = B.sb("zero", [P, P])
            room = B.sb("room", [P, 2])
            room_i = B.sb("room_i", [P, 2], I32)
            start_blk = B.sb("start_blk", [P, 1])
            tile_i = B.sb("tile_i", [P, KT], I32)
            tile_f = B.sb("tile_f", [P, KT])
            begun = B.sb("begun", [P, KT])
            ps = B.ps("ps", [P, 512])
            ps2 = B.ps("ps2", [P, 512])
            bchain, tiles_made, roomy, excl, cmp, summed = (
                B.sem(n) for n in ("chain", "tiles_made", "roomy", "excl", "cmp", "summed"))
            with nc.Block() as block:
                @block.gpsimd
                def _(pool):
                    nc.gpsimd.iota(tile_i[:, :], [[P, KT]], base=0, channel_multiplier=0).then_inc(tiles_made, 1)

                @block.vector
                def _(dve):
                    link = serial(dve, bchain)
                    nc.vector.memset(zero[:, :], 0.0)
                    link(nc.vector.tensor_copy(hist[0:H, :], hist_ps[0:H, 0:P]))
                    link(nc.vector.tensor_tensor_scan(run[0:H, :], zero[0:H, :], hist[0:H, :], 0.0,
                                                      ALU.add, ALU.add))
                    link(nc.vector.tensor_scalar(room[0:H, 0:1], run[0:H, P - 1:P], float(P - 1), None, ALU.add))
                    link(nc.vector.tensor_copy(room_i[0:H, 0:1], room[0:H, 0:1]))
                    link(nc.vector.tensor_scalar(room_i[0:H, 1:2], room_i[0:H, 0:1], -P, None, ALU.bitwise_and))
                    nc.vector.tensor_copy(room[0:H, 1:2], room_i[0:H, 1:2]).then_inc(roomy, 1)
                    dve.wait_ge(excl, 1)
                    link(nc.vector.tensor_copy(start_blk[0:H, :], ps[0:H, 0:1]))
                    link(nc.vector.tensor_tensor(run[0:H, :], run[0:H, :], hist[0:H, :], ALU.subtract))
                    link(nc.vector.tensor_scalar(first[0:H, :], run[0:H, :], start_blk[0:H, :], None, ALU.add))
                    dve.wait_ge(tiles_made, 1)
                    link(nc.vector.tensor_copy(tile_f[:, :], tile_i[:, :]))
                    nc.vector.tensor_scalar(begun[0:NB, :], tile_f[0:NB, :], start_blk[0:NB, :], None,
                                            ALU.is_ge).then_inc(cmp, 1)
                    dve.wait_ge(summed, 1)
                    link(nc.vector.tensor_scalar(block_of[0:1, 0:KT], ps2[0:1, 0:KT], -1.0, None, ALU.add))

                @block.tensor
                def _(pe):
                    pe.wait_ge(roomy, 1)
                    nc.tensor.matmul(ps[0:H, 0:1], C.upper[0:H, 0:H], room[0:H, 1:2],
                                     start=True, stop=True).then_inc(excl, 1)
                    pe.wait_ge(cmp, 1)
                    nc.tensor.matmul(ps2[0:1, 0:KT], C.ones[0:NB, 0:1], begun[0:NB, :],
                                     start=True, stop=True).then_inc(summed, 1)

        blkT_ps = [L.ps(f"blkT_ps{s}", [P, 1024], BF16) for s in range(2)]
        row_ps = [L.ps(f"row_ps{s}", [P, 512]) for s in range(2)]
        at_ps = [L.ps(f"at_ps{s}", [P, 512]) for s in range(2)]
        blkT = [L.sb(f"blkT{s}", [P, g * P]) for s in range(2)]
        snap = [L.sb(f"snap{s}", [P, g * P]) for s in range(2)]
        scrap = L.sb("scrap", [P, 2 * g * P])
        place = [L.sb(f"place{s}", [P, 2 * g]) for s in range(2)]
        place_i = [L.sb(f"place_i{s}", [P, g], I32) for s in range(RING)]
        rec_out = [L.sb(f"rec_out{s}", [P, g * W]) for s in range(RING)]
        oh2, blkT_made, blkT_copied, rows_made, compared, snapped, counted, looked, added, placed, rec_ready, gate = (
            L.sem(n) for n in ("oh2", "blkT_made", "blkT_copied", "rows_made", "compared", "snapped", "counted",
                               "looked", "added", "placed", "rec_ready", "gate"))
        sent = L.sems("sent", RING)
        V = T // g
        with nc.Block() as block:
            @block.vector
            def _(dve):
                def step(u, s, i):
                    if there(u + 1, V):
                        dve.wait_ge(rows_made, u + 2)
                        after(dve, placed, u)
                        for q in range(g):
                            last = nc.vector.scalar_tensor_tensor(
                                scrap[:, q * P:(q + 1) * P], row_ps[(s + 1) % 2][:, q * P:(q + 1) * P],
                                key[:, ds((u + 1) * g + q, 1)], C.before[:, :], ALU.is_equal, ALU.mult,
                                accum_out=place[(s + 1) % 2][:, q:q + 1])
                        last.then_inc(compared, 1)
                    if there(u + 2, V):
                        one_hots((s + 2) % RING, (u + 2) * g).then_inc(oh2, 1)
                    if there(u, V):
                        dve.wait_ge(looked, u * g + 3 * g)
                        for q in range(g):
                            last = nc.vector.scalar_tensor_tensor(
                                scrap[:, (g + q) * P:(g + q + 1) * P], at_ps[s % 2][:, q * P:(q + 1) * P], 1.0,
                                oh_low[s][:, q * P:(q + 1) * P], ALU.mult, ALU.mult,
                                accum_out=place[s % 2][:, g + q:g + q + 1])
                        last.then_inc(added, 1)
                        dve.wait_ge(added, u + 3)
                        after(dve, sent[s], i * (16 * g))
                        nc.vector.tensor_tensor(place_i[s][:, :], place[s % 2][:, 0:g], place[s % 2][:, g:2 * g],
                                                ALU.add).then_inc(placed, 1)
                dve.sem_inc(added, 2)
                dve.sem_inc(compared, 2)
                run_steps(dve, step, V, 2)

            @block.scalar
            def _(act):
                def snapshot(u, s, q):
                    act.wait_ge(counted, u * g + (q + g))
                    if q == 0:
                        act.wait_ge(looked, u * g + g)
                    nc.scalar.activation(snap[s % 2][0:H, q * P:(q + 1) * P], hist_ps[0:H, 0:P],
                                         ACT.Copy).then_inc(snapped, 1)

                def step(u, s, i):
                    if there(u, V):
                        snapshot(u, s, 0)
                        after(act, sent[s], i * (16 * g))
                        nc.scalar.activation(rec_out[s][:, :], rec[:, ds(u * (g * W), g * W)],
                                             ACT.Copy).then_inc(rec_ready, 1)
                        snapshot(u, s, 1)
                    if there(u + 1, V):
                        act.wait_ge(blkT_made, u + 2)
                        act.wait_ge(looked, u * g + 2 * g)
                        nc.scalar.activation(blkT[(s + 1) % 2][0:H, :], blkT_ps[(s + 1) % 2][0:H, 0:g * P],
                                             ACT.Copy).then_inc(blkT_copied, 1)
                    if there(u, V):
                        snapshot(u, s, 2)
                run_steps(act, step, V, 1)

            @block.tensor
            def _(pe):
                def count(u, s, q):
                    pe.wait_ge(snapped, u * g + (q + 1))
                    nc.tensor.matmul(hist_ps[0:H, 0:P], oh_blk[s][:, q * H:(q + 1) * H],
                                     oh_low[s][:, q * P:(q + 1) * P], start=False, stop=False,
                                     skip_group_check=True).then_inc(counted, 1)
                    nc.tensor.matmul(at_ps[s % 2][:, q * P:(q + 1) * P], blkT[s % 2][0:H, q * P:(q + 1) * P],
                                     snap[s % 2][0:H, q * P:(q + 1) * P], start=True, stop=True).then_inc(looked, 1)

                def step(u, s, i):
                    s1 = (s + 1) % RING
                    if there(u, V):
                        pe.wait_ge(blkT_copied, u + 1)
                        pe.wait_ge(added, u + 1)
                        count(u, s, 0)
                    if there(u + 1, V):
                        pe.wait_ge(oh2, u + 2)
                        for q in range(g):
                            mm = nc.tensor.transpose(blkT_ps[s1 % 2][0:H, q * P:(q + 1) * P],
                                                     oh_blk[s1][:, q * H:(q + 1) * H], C.ident_b[:, :])
                        mm.then_inc(blkT_made, 1)
                    if there(u, V):
                        count(u, s, 1)
                    if there(u + 1, V):
                        pe.wait_ge(compared, u + 2)
                        for q in range(g):
                            out = row_ps[s1 % 2][:, q * P:(q + 1) * P]
                            nc.tensor.matmul(out, blk128[:, ds((u + 1) * g + q, 1)].to_broadcast([P, P]),
                                             C.ident_b[:, :], start=True, stop=False)
                            mm = nc.tensor.matmul(out, low[:, ds((u + 1) * g + q, 1)].to_broadcast([P, P]),
                                                  C.ident_b[:, :], start=False, stop=True)
                        mm.then_inc(rows_made, 1)
                    if there(u, V):
                        count(u, s, 2)

                nc.tensor.matmul(hist_ps[0:H, 0:P], C.ident[0:H, 0:H], first[0:H, :],
                                 start=True, stop=False, skip_group_check=True).then_inc(counted, g)
                pe.sem_inc(looked, 2 * g)
                run_steps(pe, step, V, 1)
                nc.tensor.matmul(hist_ps[0:H, 0:P], zero_b[:, 0:H], zero_b[:, :], start=False, stop=True,
                                 skip_group_check=True)

            @block.gpsimd
            def _(pool):
                with pool.Fori(0, V // RING) as i:
                    for s in range(RING):
                        u = i * RING + s
                        pool.wait_ge(placed, u + 1)
                        nc.gpsimd.sem_inc(gate, 1)
                        pool.wait_ge(rec_ready, u + 1)
                        nc.gpsimd.sem_inc(gate, 1)
                        for q in range(g):
                            nc.gpsimd.indirect_dma_start(
                                sorted_dram, bass.IndirectOffsetOnAxis(ap=place_i[s][:, q:q + 1], axis=0),
                                rec_out[s][:, q * W:(q + 1) * W], None).then_inc(sent[s], 16)
                for s in range(RING):
                    pool.wait_ge(sent[s], V // RING * 16 * g)


def loads(eng, sem, pairs):
    for dst, src in pairs:
        eng.dma_start(dst, src).then_inc(sem, 16)
    return 16 * len(pairs)


class Edges:

    def __init__(self, S, tag, plan):
        KT, R = plan.out, plan.rows
        self.plan = plan
        self.src = S.sb(f"{tag}src", [P, KT], I32)
        self.low = S.sb(f"{tag}low", [P, KT])
        self.low_b = S.sb(f"{tag}low_b", [P, KT], BF16)
        self.src_low = S.sb(f"{tag}src_low", [P, KT], BF16)
        self.src_blk = S.sb(f"{tag}src_blk", [P, KT], BF16)
        self.cut = S.sb(f"{tag}cut", [P, 4 * 512])
        self.cut_back = S.sb(f"{tag}cut_back", [P, 4 * 512])
        self.out_first = S.sb(f"{tag}out_first", [P, 512])
        self.out_last = S.sb(f"{tag}out_last", [P, 512])
        self.joins = S.sb(f"{tag}joins", [4, R + 1])
        self.carry_on = S.sb(f"{tag}carry_on", [4, R])
        self.carry_back = S.sb(f"{tag}carry_back", [4, R])
        self.rec3 = None


def prepare_edges(nc, C, E, tag, rec_dram, rec):
    KT, W, R = E.plan.out, E.plan.width, E.plan.rows
    E.rec3 = rec[:, :].rearrange("p (k w) -> p k w", w=W)
    with Scope(nc, f"prep{tag}") as L:
        a_i = L.sb("a_i", [P, KT], I32)
        b_i = L.sb("b_i", [P, KT], I32)
        b_f = L.sb("b_f", [P, KT])
        dst_s = L.sb("dst_s", [P, 512])
        dst_ps = L.ps("dst_ps", [P, 512])
        ends_ps = L.ps("ends_ps", [4, 512])
        ends = L.sb("ends", [4, 2 * R])
        whole = L.sb("whole", [4, R])
        got, chain, turned, copied, ended = (L.sem(n) for n in ("got", "chain", "turned", "copied", "ended"))
        with nc.Block() as block:
            @block.sync
            def _(sp):
                by_tile = rec_dram.rearrange("(k r) w -> r k w", r=P)
                for k in range(0, KT, 8 * G):
                    n = min(8 * G, KT - k)
                    sp.dma_start(E.rec3[:, k:k + n, :], by_tile[:, k:k + n, :]).then_inc(got, 16)

            @block.tensor
            def _(pe):
                pe.wait_ge(got, 16 * -(-KT // (8 * G)))
                for q in range(G):
                    mm = nc.tensor.transpose(dst_ps[0:R, q * P:(q + 1) * P], E.rec3[:, q::G, 1], C.ident[:, :])
                mm.then_inc(turned, 1)
                pe.wait_ge(copied, 1)
                nc.tensor.transpose(ends_ps[0:4, 0:R], dst_s[0:R, 0:1].to_broadcast([R, 4]), C.ident[0:R, 0:R])
                nc.tensor.transpose(ends_ps[0:4, R:2 * R], dst_s[0:R, 511:512].to_broadcast([R, 4]),
                                    C.ident[0:R, 0:R]).then_inc(ended, 1)

            @block.vector
            def _(dve):
                link = serial(dve, chain)
                dve.wait_ge(got, 16 * -(-KT // (8 * G)))
                nc.vector.tensor_copy(E.src[:, :], E.rec3[:, :, 0])
                link(nc.vector.tensor_copy(a_i[:, :], E.rec3[:, :, 0]))
                link(nc.vector.tensor_scalar(b_i[:, :], a_i[:, :], 7, None, ALU.arith_shift_right))
                link(nc.vector.tensor_copy(E.src_blk[:, :], b_i[:, :]))
                link(nc.vector.tensor_scalar(b_i[:, :], a_i[:, :], P - 1, None, ALU.bitwise_and))
                link(nc.vector.tensor_copy(E.src_low[:, :], b_i[:, :]))
                link(nc.vector.tensor_copy(a_i[:, :], E.rec3[:, :, 1]))
                link(nc.vector.tensor_scalar(b_i[:, :], a_i[:, :], P - 1, None, ALU.bitwise_and))
                link(nc.vector.tensor_copy(E.low[:, :], b_i[:, :]))
                link(nc.vector.tensor_scalar(b_f[:, :], E.rec3[:, :, 1], 0.0, 1024.0, ALU.min, ALU.mult))
                link(nc.vector.tensor_tensor(E.low[:, :], E.low[:, :], b_f[:, :], ALU.add))
                link(nc.vector.tensor_copy(E.low_b[:, :], E.low[:, :]))
                dve.wait_ge(turned, 1)
                nc.vector.tensor_copy(dst_s[0:R, :], dst_ps[0:R, :]).then_inc(copied, 1)
                dve.wait_ge(copied, 1)
                cut = E.cut[0:R, :].rearrange("p (h j) -> p h j", h=4)
                back = E.cut_back[0:R, :].rearrange("p (h j) -> p h j", h=4)
                nc.vector.memset(cut[:, :, 0:1], FAR)
                nc.vector.memset(back[:, :, 511:512], FAR)
                for h in range(4):
                    nc.vector.tensor_tensor(cut[:, h, 1:512], dst_s[0:R, 1:512], dst_s[0:R, 0:511], ALU.not_equal)
                    nc.vector.tensor_tensor(back[:, h, 0:511], dst_s[0:R, 1:512], dst_s[0:R, 0:511], ALU.not_equal)
                nc.vector.tensor_scalar(E.out_first[0:R, :], dst_s[0:R, :], dst_s[0:R, 0:1], FAR,
                                        ALU.not_equal, ALU.mult)
                link(nc.vector.tensor_scalar(E.out_last[0:R, :], dst_s[0:R, :], dst_s[0:R, 511:512], FAR,
                                             ALU.not_equal, ALU.mult))
                nc.vector.tensor_scalar(cut[:, :, 1:512], cut[:, :, 1:512], FAR, None, ALU.mult)
                link(nc.vector.tensor_scalar(back[:, :, 0:511], back[:, :, 0:511], FAR, None, ALU.mult))
                dve.wait_ge(ended, 1)
                link(nc.vector.tensor_copy(ends[:, :], ends_ps[0:4, 0:2 * R]))
                link(nc.vector.memset(E.joins[:, :], FAR))
                link(nc.vector.tensor_tensor(E.joins[:, 1:R], ends[:, 1:R], ends[:, R:2 * R - 1], ALU.not_equal))
                link(nc.vector.tensor_scalar(E.joins[:, 1:R], E.joins[:, 1:R], FAR, None, ALU.mult))
                link(nc.vector.tensor_tensor(whole[:, :], ends[:, 0:R], ends[:, R:2 * R], ALU.not_equal))
                link(nc.vector.tensor_scalar(whole[:, :], whole[:, :], FAR, None, ALU.mult))
                link(nc.vector.tensor_tensor(E.carry_on[:, :], whole[:, :], E.joins[:, 0:R], ALU.add))
                link(nc.vector.tensor_tensor(E.carry_back[:, :], whole[:, :], E.joins[:, 1:R + 1], ALU.add))


def layer_norm(nc, tag, src, dst, width=D, eps=1e-5, scale=None, shift=None):
    with Scope(nc, f"ln{tag}") as L:
        stats = L.sb("stats", [P, NB * 6])
        mean = L.sb("mean", [P, NB])
        gap = L.sb("gap", [P, NB])
        dev = L.sb("dev", [P, NB])
        counted, var_ready, root, chain, normed = (
            L.sem(n) for n in ("counted", "var_ready", "root", "chain", "normed"))
        s6 = stats[:, :].rearrange("p (b t) -> p b t", t=6)
        with nc.Block() as block:
            @block.vector
            def _(dve):
                link = serial(dve, chain)
                with dve.Fori(0, NB) as b:
                    nc.vector.bn_stats(stats[:, ds(b * 6, 6)], src[:, ds(b * width, width)]).then_inc(counted, 1)
                dve.wait_ge(counted, NB)
                nc.vector.tensor_tensor(mean[:, :], s6[:, :, 1], s6[:, :, 4], ALU.add)
                nc.vector.tensor_tensor(dev[:, :], s6[:, :, 2], s6[:, :, 5], ALU.add)
                link(nc.vector.tensor_tensor(gap[:, :], s6[:, :, 1], s6[:, :, 4], ALU.subtract))
                link(nc.vector.tensor_tensor(gap[:, :], gap[:, :], gap[:, :], ALU.mult))
                link(nc.vector.tensor_scalar(dev[:, :], dev[:, :], 1.0 / width, eps, ALU.mult, ALU.add))
                nc.vector.tensor_scalar(mean[:, :], mean[:, :], 0.5, None, ALU.mult)
                nc.vector.scalar_tensor_tensor(dev[:, :], gap[:, :], 0.25, dev[:, :], ALU.mult,
                                               ALU.add).then_inc(var_ready, 1)
                dve.wait_ge(root, 1)
                link(nc.vector.reciprocal(dev[:, :], dev[:, :]))
                with dve.Fori(0, NB) as b:
                    nc.vector.tensor_scalar(dst[:, ds(b * width, width)], src[:, ds(b * width, width)],
                                            mean[:, ds(b, 1)], dev[:, ds(b, 1)],
                                            ALU.subtract, ALU.mult).then_inc(normed, 1)
                if scale is not None:
                    dve.wait_ge(normed, NB)
                    d3 = dst[:, :].rearrange("p (b d) -> p b d", d=width)
                    link(nc.vector.tensor_tensor(d3, d3, scale.unsqueeze(1).to_broadcast([P, NB, width]), ALU.mult))
                    link(nc.vector.tensor_tensor(d3, d3, shift.unsqueeze(1).to_broadcast([P, NB, width]), ALU.add))

            @block.scalar
            def _(act):
                act.wait_ge(var_ready, 1)
                nc.scalar.activation(dev[:, :], dev[:, :], ACT.Sqrt).then_inc(root, 1)


MUL = 64
MSG = 10 * MUL


def equivariant_layer(nc, C, S, a, E, block_of, x, table):
    KT = E.plan.out
    with Scope(nc, "eq") as L:
        z = L.sb("z", [P, NB])
        z8 = L.sb("z8", [P, NB])
        with Scope(nc, "eqn") as M:
            xn = M.sb("xn", [P, NB * D])
            layer_norm(nc, "eq", x, xn)
            w = M.sb("w", [MUL, 4 * MUL])
            xs = M.sb("xs", [P, D])
            xT = M.sb("xT", [MUL, 4 * P])
            row = [M.sb(f"row{s}", [P, D]) for s in range(2)]
            xT_ps = M.ps("xT_ps", [P, 512])
            o_ps = M.ps("o_ps", [P, 512])
            gate, ld, zed, split, turned, copied, made, owned, rowed, chain = (
                M.sem(n) for n in ("gate", "ld", "zed", "split", "turned", "copied", "made", "owned", "rowed", "chain"))
            stored = M.sems("stored", 2)
            with nc.Block() as block:
                @block.sync
                def _(sp):
                    loads(sp, ld, [(w[:, 0:64], a["L0_gnn_W_sc0"]), (w[:, 64:128], a["L0_gnn_W_lin1_0"]),
                                   (w[:, 128:192], a["L0_gnn_W_sc1"]), (w[:, 192:256], a["L0_gnn_W_lin1_1"]),
                                   (z[:, :], a["node_vec1"])])

                @block.vector
                def _(dve):
                    link = serial(dve, chain)
                    dve.wait_ge(ld, 80)
                    w3 = w[:, :].rearrange("p (g k v) -> p g k v", g=2, k=2)
                    link(nc.vector.tensor_scalar(w3[:, :, 0, :], w3[:, :, 0, :], float(np.float32(np.sin(np.pi / 8))),
                                                 None, ALU.mult))
                    nc.vector.tensor_scalar(z8[:, :], z[:, :], MUL ** -0.5, None, ALU.mult).then_inc(zed, 1)
                    dve.wait_ge(zed, 1)

                    def node(b, s, n, before):
                        dve.wait_ge(made, n + 1)
                        o3 = o_ps[:, :].rearrange("p (j k v) -> p j k v", j=4, k=2)
                        xb = x[:, ds(b * D, D)]
                        nc.vector.scalar_tensor_tensor(xb[:, 0:MUL], o3[:, 0, 0, :], z8[:, ds(b, 1)], xb[:, 0:MUL],
                                                       ALU.mult, ALU.add)
                        x3 = xb[:, MUL:].rearrange("p (u c) -> p c u", c=3)
                        nc.vector.scalar_tensor_tensor(x3, o3[:, 1:4, 0, :], z8[:, ds(b, 1)], x3, ALU.mult,
                                                       ALU.add).then_inc(owned, 1)
                        dve.wait_ge(stored[s], before)
                        nc.vector.tensor_scalar(row[s][:, :].rearrange("p (j v) -> p j v", j=4),
                                                o3[:, :, 1, :], z8[:, ds(b, 1)], None, ALU.mult).then_inc(rowed, 1)

                    with dve.Fori(0, NB // 2) as i:
                        node(i * 2, 0, i * 2, i * 16)
                        node(i * 2 + 1, 1, i * 2 + 1, i * 16)
                    node(NB - 1, 0, NB - 1, 16 * (NB // 2))

                @block.scalar
                def _(act):
                    with act.Fori(0, NB) as b:
                        act.wait_ge(turned, b)
                        xb = xn[:, ds(b * D, D)]
                        nc.scalar.activation(xs[:, 0:MUL], xb[:, 0:MUL], ACT.Copy)
                        nc.scalar.activation(xs[:, MUL:D].rearrange("p (c u) -> p u c", c=3),
                                             xb[:, MUL:D].rearrange("p (u c) -> p u c", c=3), ACT.Copy).then_inc(split, 1)
                        act.wait_ge(turned, b + 1)
                        act.wait_ge(made, b)
                        nc.scalar.activation(xT[:, :], xT_ps[0:MUL, :], ACT.Copy).then_inc(copied, 1)

                @block.tensor
                def _(pe):
                    pe.wait_ge(ld, 80)
                    pe.wait_ge(zed, 1)
                    with pe.Fori(0, NB) as b:
                        pe.wait_ge(split, b + 1)
                        pe.wait_ge(copied, b)
                        pe.sem_inc(gate, 1)
                        for j in range(4):
                            mm = nc.tensor.transpose(xT_ps[0:MUL, j * P:(j + 1) * P], xs[:, j * MUL:(j + 1) * MUL],
                                                     C.ident[:, :])
                        mm.then_inc(turned, 1)
                        pe.wait_ge(copied, b + 1)
                        pe.wait_ge(rowed, b)
                        for j in range(4):
                            k = 0 if j == 0 else 2 * MUL
                            mm = nc.tensor.matmul(o_ps[:, j * P:(j + 1) * P], xT[:, j * P:(j + 1) * P],
                                                  w[:, k:k + 2 * MUL], start=True, stop=True)
                        mm.then_inc(made, 1)

                @block.gpsimd
                def _(pool):
                    def store(b, s, n):
                        pool.wait_ge(rowed, n + 1)
                        nc.gpsimd.dma_start(table[ds(b * P, P), 0:D], row[s][:, :]).then_inc(stored[s], 16)
                    with pool.Fori(0, NB // 2) as i:
                        store(i * 2, 0, i * 2)
                        store(i * 2 + 1, 1, i * 2 + 1)
                    store(NB - 1, 0, NB - 1)
                    pool.wait_ge(stored[0], 16 * (NB // 2 + 1))
                    pool.wait_ge(stored[1], 16 * (NB // 2))

        acc = L.sb("acc", [P, NB * 512])
        with Scope(nc, "eqe") as M:
            fc0 = M.sb("fc0", [G * 8, G * MUL])
            fc1 = M.sb("fc1", [2 * MUL, 4 * MUL])
            idx = [M.sb(f"idx{s}", [P, G], I32) for s in range(RING)]
            got = [M.sb(f"got{s}", [P, G * D]) for s in range(RING)]
            attr = [M.sb(f"attr{s}", [P, G * 8]) for s in range(2)]
            attrT = M.sb("attrT", [G * 8, P])
            hid = [M.sb(f"hid{s}", [2 * MUL, G * MUL]) for s in range(2)]
            pick = [M.sb(f"pick{s}", [P, G * P]) for s in range(2)]
            sized = [M.sb(f"sized{s}", [P, G * MSG]) for s in range(2)]
            msg = [M.sb(f"msg{s}", [P, G * MSG]) for s in range(2)]
            small_ps = M.ps("small_ps", [P, 512])
            hid_ps = M.ps("hid_ps", [P, 512])
            w_ps = [M.ps(f"w_ps{s}", [P, 1024]) for s in range(2)]
            sum_ps = [M.ps(f"sum_ps{s}", [P, 512]) for s in range(2)]
            ld, ready, chain, idxed, attred, turned, copied, hidden, silued, weighted = (
                M.sem(n) for n in ("ld", "ready", "chain", "idxed", "attred", "turned", "copied", "hidden", "silued",
                                   "weighted"))
            sized_act, sized_dve, messaged, summed, added, gate, cleared = (
                M.sem(n) for n in ("sized_act", "sized_dve", "messaged", "summed", "added", "gate", "cleared"))
            arrived = M.sems("arrived", RING)
            V = KT // G
            n_it = V // RING

            AHEAD = 4

            with nc.Block() as block:
                @block.sync
                def _(sp):
                    sp.wait_ge(cleared, 2)
                    loads(sp, ld, [(fc0[8 * t:8 * t + 8, MUL * k:MUL * k + MUL], a["L0_gnn_fc_w0"])
                                   for t, k in enumerate((0, 2, 1, 3))]
                          + [(fc1[k * MUL:(k + 1) * MUL, to * MUL:(to + 1) * MUL],
                              a["L0_gnn_fc_w1"][:, w * MUL:(w + 1) * MUL])
                             for k in range(2) for to, w in enumerate((0, 2, 1, 3))])

                @block.gpsimd
                def _(pool):
                    nc.gpsimd.memset(fc0[:, :], 0.0).then_inc(cleared, 1)
                    with pool.Fori(0, n_it) as i:
                        for s in range(RING):
                            pool.wait_ge(idxed, i * RING + s + 1)
                            nc.gpsimd.sem_inc(gate, 1)
                            for t in range(G):
                                nc.gpsimd.indirect_dma_start(
                                    got[s][:, t * D:(t + 1) * D], None, table[:, 0:D],
                                    bass.IndirectOffsetOnAxis(ap=idx[s][:, t:t + 1], axis=0)).then_inc(arrived[s], 16)

                @block.vector
                def _(dve):
                    blk_regs = [dve.alloc_register(f"eqe_blk{t}") for t in range(G)]
                    link = serial(dve, chain)
                    nc.vector.memset(acc[:, :], 0.0).then_inc(cleared, 1)
                    dve.wait_ge(cleared, 2)
                    dve.wait_ge(ld, 16 * (G + 8))
                    link(nc.vector.tensor_scalar(fc1[:, :], fc1[:, :], MUL ** -0.5, None, ALU.mult))
                    nc.vector.tensor_scalar(fc1[:, 3 * MUL:], fc1[:, 3 * MUL:], 3 ** -0.5, None,
                                            ALU.mult).then_inc(ready, 1)
                    dve.wait_ge(ready, 1)

                    def size(v, s):
                        nc.vector.tensor_tensor(
                            sized[s % 2][:, :].rearrange("p (t f) -> p t f", t=G)[:, :, 7 * MUL:].rearrange(
                                "p t (c u) -> p t c u", c=3),
                            got[s][:, :].rearrange("p (t f) -> p t f", t=G)[:, :, MUL:].rearrange(
                                "p t (c u) -> p t c u", c=3),
                            E.rec3[:, ds(v * G, G), 3:6].unsqueeze(3).to_broadcast([P, G, 3, MUL]),
                            ALU.mult).then_inc(sized_dve, 1)

                    def message_a(s):
                        nc.vector.tensor_tensor(
                            msg[s % 2][:, :].rearrange("p (t f) -> p t f", t=G)[:, :, 0:MUL],
                            w_ps[s % 2][:, :].rearrange("p (t f) -> p t f", t=G)[:, :, 0:MUL],
                            sized[s % 2][:, :].rearrange("p (t f) -> p t f", t=G)[:, :, 0:MUL], ALU.mult)

                    def message(s, t):
                        part = slice(t * MSG + MUL, (t + 1) * MSG)
                        nc.vector.tensor_tensor(
                            msg[s % 2][:, part].rearrange("p (g c u) -> p g c u", g=3, c=3),
                            w_ps[s % 2][:, t * D + MUL:(t + 1) * D].rearrange("p (g u) -> p g u", g=3).unsqueeze(2)
                            .to_broadcast([P, 3, 3, MUL]),
                            sized[s % 2][:, part].rearrange("p (g c u) -> p g c u", g=3, c=3),
                            ALU.mult).then_inc(messaged, 1)

                    def step(u, s, i):
                        if there(u, V):
                            blks = load_blocks(dve, blk_regs, block_of[0:1, ds(u * G, G)])
                        if there(u + 1, V):
                            dve.wait_ge(weighted, u + 2)
                            dve.wait_ge(sized_act, u + 2)
                            dve.wait_ge(sized_dve, u + 2)
                            after(dve, summed, (u + 1) * G)
                            nc.vector.tensor_tensor(
                                pick[(s + 1) % 2][:, :].rearrange("p (t d) -> p t d", t=G),
                                C.ramp[:, :].unsqueeze(1).to_broadcast([P, G, P]),
                                E.low[:, ds((u + 1) * G, G)].unsqueeze(2).to_broadcast([P, G, P]), ALU.is_equal)
                            message_a(s + 1)
                        for t in range(G):
                            if there(u + 1, V):
                                message(s + 1, t)
                            if there(u, V):
                                dve.wait_ge(summed, u * G + (t + 1 + G))
                                dve.wait_ge(added, u * G + (t + 2))
                                dst = acc[:, ds(blks[t] * 512, 512)]
                                nc.vector.tensor_tensor(dst, dst, sum_ps[t % 2][:, :], ALU.add).then_inc(added, 1)
                        if there(u + 2, V):
                            s2 = (s + 2) % RING
                            dve.wait_ge(arrived[s2], (i + (1 + (s + 2) // RING)) * (16 * G))
                            after(dve, messaged, (u + 1) * G)
                            size(u + 2, s2)

                    dve.sem_inc(added, 2)
                    run_steps(dve, step, V, AHEAD)

                @block.scalar
                def _(act):
                    def step(u, s, i):
                        if there(u + 2, V):
                            act.wait_ge(hidden, u + 3)
                            after(act, weighted, u + 1)
                            nc.scalar.activation(hid[s % 2][:, :], hid_ps[:, 0:G * MUL], ACT.Silu,
                                                 scale=8 ** -0.5).then_inc(silued, 1)
                        if there(u + 3, V):
                            act.wait_ge(turned, u + 4)
                            after(act, hidden, u + 3)
                            nc.scalar.activation(attrT[:, :], small_ps[0:G * 8, 0:P], ACT.Copy).then_inc(copied, 1)
                        if there(u + 2, V):
                            s2 = (s + 2) % RING
                            act.wait_ge(arrived[s2], (i + (1 + (s + 2) // RING)) * (16 * G))
                            after(act, messaged, (u + 1) * G)
                            for t in range(G):
                                row = got[s2][:, t * D:(t + 1) * D]
                                to = sized[s % 2][:, t * MSG:(t + 1) * MSG]
                                of = [E.rec3[:, ds((u + 2) * G + t, 1), 2 + c] for c in range(4)]
                                last = nc.scalar.activation(to[:, 0:D], row, ACT.Copy, scale=of[0])
                                for c in range(3):
                                    last = nc.scalar.activation(to[:, (4 + c) * MUL:(5 + c) * MUL], row[:, 0:MUL], ACT.Copy,
                                                                scale=of[1 + c])
                            last.then_inc(sized_act, 1)
                        if there(u + 4, V):
                            after(act, turned, u + 3)
                            nc.scalar.activation(attr[s % 2][:, :].rearrange("p (t f) -> p t f", t=G),
                                                 E.rec3[:, ds((u + 4) * G, G), 6:14], ACT.Copy).then_inc(attred, 1)
                            after(act, sized_dve, u + 1)
                            after(act, sized_act, u + 1)
                            nc.scalar.activation(idx[s][:, :], E.src[:, ds((u + 4) * G, G)], ACT.Copy).then_inc(idxed, 1)

                    run_steps(act, step, V, AHEAD)

                @block.tensor
                def _(pe):
                    def step(u, s, i):
                        if there(u + 3, V):
                            pe.wait_ge(attred, u + 4)
                            after(pe, copied, u + 3)
                            nc.tensor.transpose(small_ps[0:G * 8, 0:P], attr[(s + 3) % 2][:, :],
                                                C.ident[:, :]).then_inc(turned, 1)
                        for t in range(G):
                            if there(u, V):
                                pe.wait_ge(messaged, u * G + (t + 1))
                                pe.wait_ge(added, u * G + (t + 1))
                                lhs = pick[s % 2][:, t * P:(t + 1) * P]
                                m = msg[s % 2][:, t * MSG:(t + 1) * MSG]
                                o = sum_ps[t % 2]
                                nc.tensor.matmul(o[:, :], lhs, m[:, 0:512], start=True, stop=False)
                                nc.tensor.matmul(o[:, 7 * MUL:], lhs, m[:, 8 * MUL:9 * MUL], start=False, stop=False)
                                mm = nc.tensor.matmul(o[:, 7 * MUL:], lhs, m[:, 9 * MUL:], start=False, stop=True)
                                mm.then_inc(summed, 1)
                            if there(u + 2, V):
                                if t == 0:
                                    pe.wait_ge(silued, u + 3)
                                if t % 2 == 0:
                                    after(pe, messaged, u * G + (t + 2))
                                half = slice(t // 2 * MUL, (t // 2 + 1) * MUL)
                                mm = nc.tensor.matmul(w_ps[s % 2][:, t * D:(t + 1) * D],
                                                      hid[s % 2][half, t % 2 * P:(t % 2 + 1) * P], fc1[half, :],
                                                      start=True, stop=True)
                        if there(u + 2, V):
                            mm.then_inc(weighted, 1)
                        if there(u + 3, V):
                            pe.wait_ge(copied, u + 4)
                            after(pe, silued, u + 3)
                            for k in range(2):
                                mm = nc.tensor.matmul(hid_ps[:, k * P:(k + 1) * P], fc0[:, k * P:(k + 1) * P],
                                                      attrT[:, :], start=True, stop=True)
                            mm.then_inc(hidden, 1)

                    pe.sem_inc(summed, G)
                    pe.wait_ge(ready, 1)
                    pe.wait_ge(ld, 16 * (G + 8))
                    run_steps(pe, step, V, AHEAD)

        with Scope(nc, "eqo") as M:
            w2 = M.sb("w2", [P, 2 * MUL])
            y = M.sb("y", [P, 512])
            yT = M.sb("yT", [P, 512])
            yT_ps = M.ps("yT_ps", [P, 512])
            o_ps = M.ps("o_ps", [P, 512])
            ld, ready, taken, turned, copied, made, mixed_s = (
                M.sem(n) for n in ("ld", "ready", "taken", "turned", "copied", "made", "mixed_s"))
            with nc.Block() as block:
                @block.sync
                def _(sp):
                    w0, w1 = a["L0_gnn_W_lin2_0"], a["L0_gnn_W_lin2_1"]
                    loads(sp, ld, [(w2[:, 0:64], w0),
                                   (w2[0:64, 64:128], w1[64:128, :]), (w2[64:128, 64:128], w1[0:64, :])])

                @block.vector
                def _(dve):
                    dve.wait_ge(ld, 48)
                    k = float(np.float32(np.cos(np.pi / 8))) / np.sqrt(16.0) / np.sqrt(2.0 * MUL)
                    nc.vector.tensor_scalar(w2[:, :], w2[:, :], float(k), None, ALU.mult).then_inc(ready, 1)
                    with dve.Fori(0, NB) as b:
                        dve.wait_ge(made, b + 1)
                        xb = x[:, ds(b * D, D)]
                        nc.vector.scalar_tensor_tensor(xb[:, 0:MUL], o_ps[:, 0:MUL], z[:, ds(b, 1)], xb[:, 0:MUL],
                                                       ALU.mult, ALU.add)
                        x3 = xb[:, MUL:].rearrange("p (u c) -> p c u", c=3)
                        nc.vector.scalar_tensor_tensor(x3, o_ps[:, MUL:D].rearrange("p (c u) -> p c u", c=3),
                                                       z[:, ds(b, 1)], x3, ALU.mult, ALU.add).then_inc(mixed_s, 1)

                @block.scalar
                def _(act):
                    with act.Fori(0, NB) as b:
                        act.wait_ge(turned, b)
                        sums = acc[:, ds(b * 512, 512)]
                        nc.scalar.activation(y[:, 0:MUL], sums[:, 0:MUL], ACT.Copy)
                        nc.scalar.activation(y[:, MUL:2 * MUL], sums[:, 7 * MUL:], ACT.Copy)
                        for g in range(2):
                            last = nc.scalar.activation(
                                y[:, 2 * MUL:].rearrange("p (c g u) -> p c g u", g=2, c=3)[:, :, g, :],
                                sums[:, (1 + 3 * g) * MUL:(4 + 3 * g) * MUL].rearrange("p (c u) -> p c u", c=3), ACT.Copy)
                        last.then_inc(taken, 1)
                        act.wait_ge(turned, b + 1)
                        act.wait_ge(made, b)
                        nc.scalar.activation(yT[:, :], yT_ps[:, :], ACT.Copy).then_inc(copied, 1)

                @block.tensor
                def _(pe):
                    pe.wait_ge(ready, 1)
                    pe.wait_ge(ld, 48)
                    with pe.Fori(0, NB) as b:
                        pe.wait_ge(taken, b + 1)
                        pe.wait_ge(copied, b)
                        for j in range(4):
                            mm = nc.tensor.transpose(yT_ps[:, j * P:(j + 1) * P], y[:, j * P:(j + 1) * P], C.ident[:, :])
                        mm.then_inc(turned, 1)
                        pe.wait_ge(copied, b + 1)
                        pe.wait_ge(mixed_s, b)
                        for j in range(4):
                            mm = nc.tensor.matmul(o_ps[:, j * MUL:(j + 1) * MUL], yT[:, j * P:(j + 1) * P],
                                                  w2[:, 0:MUL] if j == 0 else w2[:, MUL:], start=True, stop=True)
                        mm.then_inc(made, 1)


def broadcast_rows(ap):
    return ap.partition_broadcast(P)


def gating(nc, tag, logits, gates, n):
    with Scope(nc, f"gate{tag}") as L:
        above = L.sb("above", [P, NB * n * n])
        ties = L.sb("ties", [P, NB * n * n])
        early = L.sb("early", [P, n * n])
        rank = L.sb("rank", [P, NB * n])
        top = L.sb("top", [P, NB])
        ramp = L.sb("ramp", [P, n])
        chain, expd, ready, ramped = L.sem("chain"), L.sem("expd"), L.sem("ready"), L.sem("ramped")
        l3 = logits[:, :].rearrange("p (b e) -> p b e", e=n)
        g3 = gates[:, :].rearrange("p (b e) -> p b e", e=n)
        r3 = rank[:, :].rearrange("p (b e) -> p b e", e=n)
        with nc.Block() as block:
            @block.gpsimd
            def _(pool):
                nc.gpsimd.iota(ramp[:, :], [[1, n]], base=0, channel_multiplier=0,
                               allow_small_or_imprecise_dtypes=True).then_inc(ramped, 1)

            @block.vector
            def _(dve):
                link = serial(dve, chain)
                dve.wait_ge(ramped, 1)
                e3 = early[:, :].rearrange("p (e f) -> p e f", e=n)
                link(nc.vector.tensor_tensor(e3, ramp[:, :].unsqueeze(1).to_broadcast([P, n, n]),
                                             ramp[:, :].unsqueeze(2).to_broadcast([P, n, n]), ALU.is_lt))
                link(nc.vector.tensor_reduce(top[:, :], l3, AX.X, ALU.max))
                nc.vector.tensor_tensor(g3, l3, top[:, :].unsqueeze(2).to_broadcast([P, NB, n]),
                                        ALU.subtract).then_inc(ready, 1)
                for e in range(n):
                    for out, op in ((above, ALU.is_gt), (ties, ALU.is_equal)):
                        last = nc.vector.tensor_tensor(
                            out[:, :].rearrange("p (b e f) -> p b e f", e=n, f=n)[:, :, e, :], l3,
                            l3[:, :, e:e + 1].to_broadcast([P, NB, n]), op)
                link(last)
                t3 = ties[:, :].rearrange("p (b k) -> p b k", b=NB)
                link(nc.vector.tensor_tensor(t3, t3, early[:, :].unsqueeze(1).to_broadcast([P, NB, n * n]), ALU.mult))
                link(nc.vector.tensor_tensor(above[:, :], above[:, :], ties[:, :], ALU.add))
                link(nc.vector.tensor_reduce(rank[:, :], above[:, :].rearrange("p (k f) -> p k f", f=n), AX.X, ALU.add))
                dve.wait_ge(expd, 1)
                link(nc.vector.scalar_tensor_tensor(gates[:, :], rank[:, :], 1.5, gates[:, :], ALU.is_lt, ALU.mult))
                link(nc.vector.tensor_reduce(top[:, :], g3, AX.X, ALU.add))
                link(nc.vector.reciprocal(top[:, :], top[:, :]))
                link(nc.vector.tensor_tensor(g3, g3, top[:, :].unsqueeze(2).to_broadcast([P, NB, n]), ALU.mult))

            @block.scalar
            def _(act):
                act.wait_ge(ready, 1)
                nc.scalar.activation(gates[:, :], gates[:, :], ACT.Exp).then_inc(expd, 1)


HID = 512


def experts(nc, C, tag, xn, x, n, a, w1, b1, w2, b2, wr=None, br=None, gates=None):
    KD, KH = D // P, HID // P
    with Scope(nc, f"moe{tag}") as L:
        xnT = L.sb("xnT", [P, KD * NPAD])
        xnT3 = xnT[:, :].rearrange("p (k n) -> p k n", k=KD)
        if gates is None:
            gates = L.sb("gates", [P, NB * n])
            logits = L.sb("logits", [P, NB * n])
        with Scope(nc, f"moet{tag}") as M:
            block_in = M.sb("block_in", [P, D])
            turned = M.sb("turned", [P, D])
            wr_s = M.sb("wr", [P, KD * n])
            br_s = M.sb("br", [P, n])
            t_ps = M.ps("t_ps", [P, 512])
            l_ps = M.ps("l_ps", [P, 512])
            ld, taken, flipped, copied, kept, routed, logged = (
                M.sem(s) for s in ("ld", "taken", "flipped", "copied", "kept", "routed", "logged"))
            with nc.Block() as block:
                @block.sync
                def _(sp):
                    if wr is not None:
                        loads(sp, ld, [(wr_s[:, k * n:(k + 1) * n], a[wr][k * P:(k + 1) * P, :]) for k in range(KD)]
                              + [(br_s[:, :], broadcast_rows(a[br]))])

                @block.scalar
                def _(act):
                    with act.Fori(0, NB) as b:
                        act.wait_ge(flipped, b)
                        nc.scalar.activation(block_in[:, :], xn[:, ds(b * D, D)], ACT.Copy).then_inc(taken, 1)
                        act.wait_ge(flipped, b + 1)
                        act.wait_ge(kept, b)
                        act.wait_ge(routed, b)
                        nc.scalar.activation(turned[:, :], t_ps[:, 0:D], ACT.Copy).then_inc(copied, 1)

                @block.vector
                def _(dve):
                    with dve.Fori(0, NB) as b:
                        dve.wait_ge(copied, b + 1)
                        nc.vector.tensor_copy(xnT3[:, :, ds(b * P, P)],
                                              turned[:, :].rearrange("p (k n) -> p k n", k=KD)).then_inc(kept, 1)
                        if wr is not None:
                            dve.wait_ge(routed, b + 1)
                            nc.vector.tensor_tensor(logits[:, ds(b * n, n)], l_ps[:, 0:n], br_s[:, :],
                                                    ALU.add).then_inc(logged, 1)

                @block.tensor
                def _(pe):
                    if wr is not None:
                        pe.wait_ge(ld, 16 * (KD + 1))
                    with pe.Fori(0, NB) as b:
                        pe.wait_ge(taken, b + 1)
                        pe.wait_ge(copied, b)
                        for k in range(KD):
                            mm = nc.tensor.transpose(t_ps[:, k * P:(k + 1) * P], block_in[:, k * P:(k + 1) * P], C.ident[:, :])
                        mm.then_inc(flipped, 1)
                        pe.wait_ge(copied, b + 1)
                        if wr is not None:
                            pe.wait_ge(logged, b)
                            for k in range(KD):
                                mm = nc.tensor.matmul(l_ps[:, 0:n], turned[:, k * P:(k + 1) * P],
                                                      wr_s[:, k * n:(k + 1) * n], start=k == 0, stop=k == KD - 1)
                            mm.then_inc(routed, 1)
                        else:
                            pe.sem_inc(routed, 1)
        if wr is not None:
            gating(nc, tag, logits, gates, n)
        with Scope(nc, f"moeb{tag}") as M:
            g_in = M.sb("g_in", [P, n])
            gT = M.sb("gT", [n, P])
            b2_s = M.sb("b2", [n, D])
            t_ps = M.ps("t_ps", [P, 512])
            o_ps = M.ps("o_ps", [P, 512])
            ld, gate, taken, flipped, copied, made, added = (
                M.sem(s) for s in ("ld", "gate", "taken", "flipped", "copied", "made", "added"))
            with nc.Block() as block:
                @block.sync
                def _(sp):
                    sp.dma_start(b2_s[:, :], a[b2]).then_inc(ld, 16)

                @block.scalar
                def _(act):
                    with act.Fori(0, NB) as b:
                        act.wait_ge(flipped, b)
                        nc.scalar.activation(g_in[:, :], gates[:, ds(b * n, n)], ACT.Copy).then_inc(taken, 1)
                        act.wait_ge(flipped, b + 1)
                        act.wait_ge(made, b)
                        nc.scalar.activation(gT[:, :], t_ps[0:n, 0:P], ACT.Copy).then_inc(copied, 1)

                @block.vector
                def _(dve):
                    with dve.Fori(0, NB) as b:
                        dve.wait_ge(made, b + 1)
                        xb = x[:, ds(b * D, D)]
                        nc.vector.tensor_tensor(xb, xb, o_ps[:, 0:D], ALU.add).then_inc(added, 1)

                @block.tensor
                def _(pe):
                    pe.wait_ge(ld, 16)
                    with pe.Fori(0, NB) as b:
                        pe.wait_ge(taken, b + 1)
                        pe.wait_ge(copied, b)
                        pe.sem_inc(gate, 1)
                        nc.tensor.transpose(t_ps[0:n, 0:P], g_in[:, :], C.ident[:, :]).then_inc(flipped, 1)
                        pe.wait_ge(copied, b + 1)
                        pe.wait_ge(added, b)
                        pe.sem_inc(gate, 1)
                        nc.tensor.matmul(o_ps[:, 0:D], gT[:, :], b2_s[:, :], start=True, stop=True).then_inc(made, 1)
        BG = 5
        NG = BG * P
        groups = NB // BG
        half = NG // 2
        with Scope(nc, f"moee{tag}") as M:
            w1_s = [M.sb(f"w1_{s}", [P, KD * HID]) for s in range(2)]
            w2_s = [M.sb(f"w2_{s}", [P, KH * D]) for s in range(2)]
            b1_s = [M.sb(f"b1_{s}", [P, KH]) for s in range(2)]
            h = [M.sb(f"h{s}", [P, KH * NG]) for s in range(2)]
            h_ps = [M.ps(f"h_ps{s}", [P, 512]) for s in range(4)]
            y_ps = [M.ps(f"y_ps{s}", [P, 512]) for s in range(2)]
            gelued, up, down, added, done = (
                M.sem(s) for s in ("gelued", "up", "down", "added", "done"))
            ld = M.sems("ld", 2)
            per = groups * KH * 2
            with nc.Block() as block:
                @block.sync
                def _(sp):
                    with sp.Fori(0, n // 2) as i:
                        for s in range(2):
                            sp.wait_ge(done, i * 2 + s)
                            e = i * 2 + s
                            sp.dma_start(b1_s[s][:, :], a[b1][:, ds(e * KH, KH)]).then_inc(ld[s], 16)
                            sp.dma_start(w1_s[s][:, :].rearrange("p (k h) -> p k h", k=KD),
                                         a[w1][ds(e, 1), :, :].rearrange("o (k p) h -> p (o k) h", p=P)).then_inc(ld[s], 16)
                            sp.dma_start(w2_s[s][:, :].rearrange("p (k d) -> p k d", k=KH),
                                         a[w2][ds(e, 1), :, :].rearrange("o (k p) d -> p (o k) d", p=P)).then_inc(ld[s], 16)

                @block.tensor
                def _(pe):
                    pe.sem_inc(done, 1)
                    with pe.Fori(0, n // 2) as i:
                        for s in range(2):
                            pe.wait_ge(ld[s], i * 48 + 48)

                            def first_layer(gr):
                                for m in range(KH):
                                    for r in range(2):
                                        c = s * per + gr * KH * 2 + m * 2 + r
                                        pe.wait_ge(gelued, i * (2 * per) + c + 1)
                                        for k in range(KD):
                                            mm = nc.tensor.matmul(
                                                h_ps[c % 4][:, 0:half],
                                                w1_s[s][:, k * HID + m * P:k * HID + (m + 1) * P],
                                                xnT[:, k * NPAD + gr * NG + r * half:k * NPAD + gr * NG + (r + 1) * half],
                                                start=k == 0, stop=k == KD - 1)
                                        mm.then_inc(up, 1)

                            def second_layer(gr):
                                v = s * groups + gr
                                pe.wait_ge(gelued, i * (2 * per) + (v + 1) * KH * 2 + 4)
                                for j in range(BG):
                                    c = v * BG + j
                                    pe.wait_ge(added, i * (2 * groups * BG) + c)
                                    for m in range(KH):
                                        mm = nc.tensor.matmul(
                                            y_ps[c % 2][:, 0:D], h[v % 2][:, m * NG + j * P:m * NG + (j + 1) * P],
                                            w2_s[s][:, m * D:(m + 1) * D], start=m == 0, stop=m == KH - 1)
                                    mm.then_inc(down, 1)

                            first_layer(0)
                            for gr in range(1, groups):
                                first_layer(gr)
                                second_layer(gr - 1)
                            second_layer(groups - 1)
                            pe.wait_ge(down, i * (2 * groups * BG) + (s + 1) * groups * BG)
                            pe.sem_inc(done, 1)

                @block.scalar
                def _(act):
                    act.sem_inc(gelued, 4)
                    with act.Fori(0, n // 2) as i:
                        for s in range(2):
                            act.wait_ge(ld[s], i * 48 + 48)
                            for gr in range(groups):
                                v = s * groups + gr
                                if v >= 2:
                                    act.wait_ge(down, i * (2 * groups * BG) + (v - 1) * BG)
                                elif v == 1:
                                    act.wait_ge(down, i * (2 * groups * BG))
                                for m in range(KH):
                                    for r in range(2):
                                        c = v * KH * 2 + m * 2 + r
                                        act.wait_ge(up, i * (2 * per) + c + 1)
                                        nc.scalar.activation(
                                            h[v % 2][:, m * NG + r * half:m * NG + (r + 1) * half],
                                            h_ps[c % 4][:, 0:half], ACT.Gelu,
                                            bias=b1_s[s][:, m:m + 1]).then_inc(gelued, 1)

                @block.vector
                def _(dve):
                    dve.sem_inc(added, 1)
                    with dve.Fori(0, n // 2) as i:
                        for s in range(2):
                            for b in range(NB):
                                c = s * NB + b
                                dve.wait_ge(down, i * (2 * NB) + c + 1)
                                if b == 0:
                                    dve.wait_ge(added, i * (2 * NB) + c + 1)
                                xb = x[:, b * D:(b + 1) * D]
                                nc.vector.scalar_tensor_tensor(
                                    xb, y_ps[c % 2][:, 0:D], gates[:, ds(i * 2 + (b * n + s), 1)], xb,
                                    ALU.mult, ALU.add).then_inc(added, 1)


def turned_one_hots(nc, C, tag, E, lists):
    KT, K = E.plan.out, len(lists)
    with Scope(nc, f"oht{tag}") as L:
        ps = [L.ps(f"ps{s}", [P, 512]) for s in range(RING)]
        row = [L.sb(f"row{s}", [P, G * P], BF16) for s in range(RING)]
        oh = [L.sb(f"oh{s}", [P, G * P], BF16) for s in range(RING)]
        rows, copied, compared = L.sem("rows"), L.sem("copied"), L.sem("compared")
        put = L.sems("put", RING)
        n_it = KT * K // (RING * G)
        with nc.Block() as block:
            @block.tensor
            def _(pe):
                pe.sem_inc(copied, RING)
                with pe.Fori(0, n_it) as i:
                    for s in range(RING):
                        u = i * RING + s
                        columns = lists[s % K][0]
                        pe.wait_ge(copied, u + 1)
                        for t in range(G):
                            mm = nc.tensor.matmul(ps[s][:, t * P:(t + 1) * P],
                                                  columns[:, ds(i * (RING // K * G) + (s // K * G + t), 1)]
                                                  .to_broadcast([P, P]), C.ident_b[:, :], start=True, stop=True)
                        mm.then_inc(rows, 1)

            @block.scalar
            def _(act):
                act.sem_inc(compared, RING)
                with act.Fori(0, n_it) as i:
                    for s in range(RING):
                        u = i * RING + s
                        act.wait_ge(rows, u + 1)
                        act.wait_ge(compared, u + 1)
                        nc.scalar.activation(row[s][:, :], ps[s][:, :], ACT.Copy).then_inc(copied, 1)

            @block.vector
            def _(dve):
                for p in put:
                    dve.sem_inc(p, 16)
                with dve.Fori(0, n_it) as i:
                    for s in range(RING):
                        u = i * RING + s
                        dve.wait_ge(copied, u + RING + 1)
                        dve.wait_ge(put[s], i * 16 + 16)
                        nc.vector.tensor_scalar(oh[s][:, :], row[s][:, :], C.part[:, :], None,
                                                ALU.is_equal).then_inc(compared, 1)

            @block.sync
            def _(sp):
                with sp.Fori(0, n_it) as i:
                    for s in range(RING):
                        u = i * RING + s
                        out = lists[s % K][1]
                        sp.wait_ge(compared, u + RING + 1)
                        sp.dma_start(out[:, ds(i * (RING // K * G * P) + s // K * G * P, G * P)],
                                     oh[s][:, :]).then_inc(put[s], 16)
                for s in range(RING):
                    sp.wait_ge(put[s], 16 * (n_it + 1))


def split_bf16(nc, link, src, parts, rest):
    for j, part in enumerate(parts):
        link(nc.vector.tensor_copy(part, src if j == 0 else rest))
        if j < 2:
            link(nc.vector.tensor_tensor(rest, src if j == 0 else rest, part, ALU.subtract))


def segment_softmax(nc, C, tag, E, scores):
    KT, R = E.plan.out, E.plan.rows
    with Scope(nc, f"seg{tag}") as L:
        upto = L.sb("upto", [P, 2048])
        peak = L.sb("peak", [P, 2048])
        chain, leaky, flipped, ends, ended, carried, carry_t, spread, shifted, back, expd = (
            L.sem(n) for n in ("chain", "leaky", "flipped", "ends", "ended", "carried", "carry_t", "spread",
                               "shifted", "back", "expd"))
        s3 = scores[:, :].rearrange("p (k h) -> p k h", h=4)
        rows = L.sb("rows", [4, 2 * P])
        runs = L.sb("runs", [4, 2 * P])
        carry = L.sb("carry", [P, 8])
        with Scope(nc, f"sega{tag}") as M:
            e_ps = M.ps("e_ps", [P, 2048])
            small = M.ps("small", [P, 512])
            with nc.Block() as block:
                @block.vector
                def _(dve):
                    link = serial(dve, chain)
                    nc.vector.scalar_tensor_tensor(scores[:, :], scores[:, :], 0.2, scores[:, :], ALU.mult,
                                                   ALU.max).then_inc(leaky, 1)
                    dve.wait_ge(flipped, 1)
                    link(nc.vector.tensor_tensor_scan(upto[0:R, :], E.cut[0:R, :], e_ps[0:R, :], FAR, ALU.add, ALU.max))
                    nc.vector.tensor_tensor_scan(peak[0:R, ::-1], E.cut_back[0:R, ::-1], upto[0:R, ::-1], FAR,
                                                 ALU.add, ALU.max).then_inc(ends, 1)
                    dve.wait_ge(ended, 1)
                    link(nc.vector.tensor_copy(rows[:, 0:2 * R], small[0:4, 0:2 * R]))
                    nc.vector.memset(runs[:, 0:1], FAR)
                    link(nc.vector.memset(runs[:, 2 * R - 1:2 * R], FAR))
                    link(nc.vector.tensor_tensor_scan(runs[:, 1:R], E.carry_on[:, 0:R - 1], rows[:, R:2 * R - 1], FAR,
                                                      ALU.add, ALU.max))
                    link(nc.vector.tensor_tensor_scan(runs[:, 2 * R - 2:R - 1:-1], E.carry_back[:, R - 1:0:-1],
                                                      rows[:, R - 1:0:-1], FAR, ALU.add, ALU.max))
                    link(nc.vector.tensor_tensor(runs[:, 0:R], runs[:, 0:R], E.joins[:, 0:R], ALU.add))
                    nc.vector.tensor_tensor(runs[:, R:2 * R], runs[:, R:2 * R], E.joins[:, 1:R + 1],
                                            ALU.add).then_inc(carried, 1)
                    dve.wait_ge(carry_t, 1)
                    link(nc.vector.tensor_copy(carry[0:R, :], small[0:R, 384:392]))
                    for k, out in ((0, E.out_first), (4, E.out_last)):
                        for h in range(4):
                            part = peak[0:R, h * 512:(h + 1) * 512]
                            last = nc.vector.scalar_tensor_tensor(part, out[0:R, :], carry[0:R, k + h:k + h + 1], part,
                                                                  ALU.add, ALU.max)
                        link(last)
                    nc.vector.tensor_tensor(upto[0:R, :], e_ps[0:R, :], peak[0:R, :], ALU.subtract).then_inc(shifted, 1)

                @block.tensor
                def _(pe):
                    pe.wait_ge(leaky, 1)
                    for h in range(4):
                        for q in range(G):
                            mm = nc.tensor.transpose(e_ps[0:R, h * 512 + q * P:h * 512 + (q + 1) * P], s3[:, q::G, h],
                                                     C.ident[:, :])
                    mm.then_inc(flipped, 1)
                    pe.wait_ge(ends, 1)
                    p3 = peak[0:R, :].rearrange("p (h j) -> p h j", h=4)
                    nc.tensor.transpose(small[0:4, 0:R], p3[:, :, 0], C.ident[0:R, 0:R])
                    nc.tensor.transpose(small[0:4, R:2 * R], p3[:, :, 511], C.ident[0:R, 0:R]).then_inc(ended, 1)
                    pe.wait_ge(carried, 1)
                    nc.tensor.transpose(small[0:R, 384:388], runs[:, 0:R], C.ident[0:4, 0:4])
                    nc.tensor.transpose(small[0:R, 388:392], runs[:, R:2 * R], C.ident[0:4, 0:4]).then_inc(carry_t, 1)
        with Scope(nc, f"segb{tag}") as M:
            b_ps = M.ps("b_ps", [P, 2048])
            with nc.Block() as block:
                @block.tensor
                def _(pe):
                    for h in range(4):
                        for q in range(G):
                            mm = nc.tensor.transpose(b_ps[:, (q * 4 + h) * P:(q * 4 + h) * P + R],
                                                     upto[0:R, h * 512 + q * P:h * 512 + (q + 1) * P], C.ident[0:R, 0:R])
                    mm.then_inc(back, 1)

                @block.scalar
                def _(act):
                    act.wait_ge(back, 1)
                    for q in range(G):
                        nc.scalar.activation(
                            s3[:, q::G, :].rearrange("p r h -> p h r"),
                            b_ps[:, q * 512:(q + 1) * 512].rearrange("p (h r) -> p h r", h=4)[:, :, 0:R], ACT.Exp)


def gat_layer(nc, C, S, a, n, E, block_of, h_in, acc, table, oht_src, oht_dst):
    KT, DW = E.plan.out, D + 4
    with Scope(nc, f"gat{n}") as L:
        score = L.sb("score", [P, NB * 8])
        src3 = L.sb("src3", [P, 3 * NB * 4], BF16)
        dst3 = L.sb("dst3", [P, NB * 3 * 4], BF16)
        with Scope(nc, f"gatn{n}") as M:
            w = M.sb("w", [P, 2 * (D + 8)])
            w3 = w[:, :].rearrange("p (k f) -> p k f", k=2)
            att = M.sb("att", [P, 2 * D])
            prod = M.sb("prod", [P, 4 * D])
            block_in = M.sb("block_in", [P, D])
            hT = M.sb("hT", [P, D])
            row = [M.sb(f"row{s}", [P, D]) for s in range(2)]
            rest = M.sb("rest", [P, NB * 4])
            t_ps = M.ps("t_ps", [P, 512])
            o_ps = M.ps("o_ps", [P, 512])
            ld, chain, ready, taken, flipped, copied, made, rowed = (
                M.sem(s) for s in ("ld", "chain", "ready", "taken", "flipped", "copied", "made", "rowed"))
            stored = M.sems("stored", 2)
            with nc.Block() as block:
                @block.sync
                def _(sp):
                    loads(sp, ld, [(w3[:, k, 0:D], a[f"L1_gnn_W{n}"][k * P:(k + 1) * P, :]) for k in range(2)]
                          + [(att[:, 0:D], broadcast_rows(a[f"L1_gnn_a_src{n}"].rearrange("h c -> (h c)"))),
                             (att[:, D:], broadcast_rows(a[f"L1_gnn_a_dst{n}"].rearrange("h c -> (h c)")))])

                    def store(b, s, k):
                        sp.wait_ge(rowed, k + 1)
                        sp.dma_start(table[ds(b * P, P), 0:D], row[s][:, :]).then_inc(stored[s], 16)
                    with sp.Fori(0, NB // 2) as i:
                        store(i * 2, 0, i * 2)
                        store(i * 2 + 1, 1, i * 2 + 1)
                    store(NB - 1, 0, NB - 1)
                    sp.wait_ge(stored[0], 16 * (NB // 2 + 1))
                    sp.wait_ge(stored[1], 16 * (NB // 2))

                @block.vector
                def _(dve):
                    link = serial(dve, chain)
                    dve.wait_ge(ld, 64)
                    p4 = prod[:, :].rearrange("p (k g f) -> p k g f", k=2, g=2)
                    for k in range(2):
                        last = nc.vector.tensor_tensor(p4[:, k, :, :], w3[:, k, 0:D].unsqueeze(1).to_broadcast([P, 2, D]),
                                                       att[:, :].rearrange("p (g f) -> p g f", g=2), ALU.mult)
                    link(last)
                    for k in range(2):
                        last = nc.vector.tensor_reduce(
                            w3[:, k, D:D + 8], prod[:, k * 2 * D:(k + 1) * 2 * D].rearrange("p (g c) -> p g c", c=64),
                            AX.X, ALU.add)
                    last.then_inc(ready, 1)

                    def node(b, s, k, before):
                        dve.wait_ge(made, k + 1)
                        dve.wait_ge(stored[s], before)
                        nc.vector.tensor_copy(row[s][:, :], o_ps[:, 0:D])
                        nc.vector.tensor_copy(score[:, ds(b * 8, 8)], o_ps[:, D:D + 8]).then_inc(rowed, 1)
                    with dve.Fori(0, NB // 2) as i:
                        node(i * 2, 0, i * 2, i * 16)
                        node(i * 2 + 1, 1, i * 2 + 1, i * 16)
                    node(NB - 1, 0, NB - 1, 16 * (NB // 2))
                    dve.wait_ge(rowed, NB)
                    sc3 = score[:, :].rearrange("p (b k) -> p b k", k=8)
                    part_rest = rest[:, :].rearrange("p (b h) -> p b h", h=4)
                    split_bf16(nc, link, sc3[:, :, 0:4],
                               [src3[:, :].rearrange("p (j b h) -> p j b h", j=3, h=4)[:, j] for j in range(3)], part_rest)
                    split_bf16(nc, link, sc3[:, :, 4:8],
                               [dst3[:, :].rearrange("p (b j h) -> p j b h", j=3, h=4)[:, j] for j in range(3)], part_rest)

                @block.scalar
                def _(act):
                    with act.Fori(0, NB) as b:
                        act.wait_ge(flipped, b)
                        nc.scalar.activation(block_in[:, :], h_in[:, ds(b * D, D)], ACT.Copy).then_inc(taken, 1)
                        act.wait_ge(flipped, b + 1)
                        act.wait_ge(made, b)
                        nc.scalar.activation(hT[:, :], t_ps[:, 0:D], ACT.Copy).then_inc(copied, 1)

                @block.tensor
                def _(pe):
                    pe.wait_ge(ready, 1)
                    pe.wait_ge(ld, 64)
                    with pe.Fori(0, NB) as b:
                        pe.wait_ge(taken, b + 1)
                        pe.wait_ge(copied, b)
                        for k in range(2):
                            mm = nc.tensor.transpose(t_ps[:, k * P:(k + 1) * P], block_in[:, k * P:(k + 1) * P], C.ident[:, :])
                        mm.then_inc(flipped, 1)
                        pe.wait_ge(copied, b + 1)
                        pe.wait_ge(rowed, b)
                        for k in range(2):
                            mm = nc.tensor.matmul(o_ps[:, 0:D + 8], hT[:, k * P:(k + 1) * P], w3[:, k, :],
                                                  start=k == 0, stop=k == 1)
                        mm.then_inc(made, 1)

        edge = L.sb("edge", [P, KT * 4])
        with Scope(nc, f"gats{n}") as M:
            W = (NB + 3) * 4
            os_ = [M.sb(f"os{s}", [P, G * P], BF16) for s in range(RING)]
            od_ = [M.sb(f"od{s}", [P, G * P], BF16) for s in range(RING)]
            ohb = [M.sb(f"ohb{s}", [P, G * (NB + 3)]) for s in range(2)]
            prod = [M.sb(f"prod{s}", [P, G * W]) for s in range(2)]
            r_ps = [M.ps(f"r_ps{s}", [P, 512]) for s in range(RING)]
            filled, looked, chosen, multed, reduced = (
                M.sem(s) for s in ("filled", "looked", "chosen", "multed", "reduced"))
            came = M.sems("came", RING)
            n_it = KT // (RING * G)
            with nc.Block() as block:
                @block.sync
                def _(sp):
                    with sp.Fori(0, n_it) as i:
                        for s in range(RING):
                            u = i * RING + s
                            sp.wait_ge(looked, u + 1)
                            sp.dma_start(os_[s][:, :], oht_src[:, ds(u * (G * P), G * P)]).then_inc(came[s], 16)
                            sp.dma_start(od_[s][:, :], oht_dst[:, ds(u * (G * P), G * P)]).then_inc(came[s], 16)

                @block.tensor
                def _(pe):
                    blk_regs = [pe.alloc_register(f"gats{n}_blk{t}") for t in range(RING * G)]
                    pe.sem_inc(looked, RING)
                    with pe.Fori(0, n_it) as i:
                        blks = load_blocks(pe, blk_regs, block_of[0:1, ds(i * (RING * G), RING * G)])
                        for s in range(RING):
                            u = i * RING + s
                            pe.wait_ge(came[s], i * 32 + 32)
                            pe.wait_ge(multed, u + 1)
                            for t in range(G):
                                for j in range(3):
                                    nc.tensor.matmul(r_ps[s][:, t * W:t * W + NB * 4], os_[s][:, t * P:(t + 1) * P],
                                                     src3[:, j * NB * 4:(j + 1) * NB * 4], start=j == 0, stop=j == 2)
                                mm = nc.tensor.matmul(r_ps[s][:, t * W + NB * 4:(t + 1) * W], od_[s][:, t * P:(t + 1) * P],
                                                      dst3[:, ds(blks[s * G + t] * 12, 12)], start=True, stop=True)
                            mm.then_inc(looked, 1)

                @block.vector
                def _(dve):
                    def choose(u, s):
                        nc.vector.tensor_tensor(
                            ohb[s % 2][:, :].rearrange("p (t b) -> p t b", t=G)[:, :, 0:NB],
                            C.ramp[:, 0:NB].unsqueeze(1).to_broadcast([P, G, NB]),
                            E.src_blk[:, ds(u * G, G)].unsqueeze(2).to_broadcast([P, G, NB]),
                            ALU.is_equal).then_inc(chosen, 1)

                    def step(u, s, more=True):
                        dve.wait_ge(chosen, u + 1)
                        dve.wait_ge(reduced, u + 1)
                        dve.wait_ge(looked, u + RING + 1)
                        nc.vector.tensor_tensor(
                            prod[s % 2][:, :].rearrange("p (b h) -> p b h", h=4),
                            r_ps[s][:, 0:G * W].rearrange("p (b h) -> p b h", h=4),
                            ohb[s % 2][:, :].unsqueeze(2).to_broadcast([P, G * (NB + 3), 4]), ALU.mult).then_inc(multed, 1)
                        if more:
                            choose(u + 1, s + 1)
                        dve.wait_ge(multed, u + RING + 1)
                        nc.vector.tensor_reduce(edge[:, ds(u * (G * 4), G * 4)].rearrange("p (t h) -> p t h", t=G),
                                                prod[s % 2][:, :].rearrange("p (t b h) -> p t h b", t=G, h=4),
                                                AX.X, ALU.add).then_inc(reduced, 1)

                    for o in ohb:
                        nc.vector.memset(o[:, :], 1.0).then_inc(filled, 1)
                    dve.wait_ge(filled, 2)
                    dve.sem_inc(multed, RING)
                    dve.sem_inc(reduced, 2)
                    choose(0, 0)
                    with dve.Fori(0, n_it - 1) as i:
                        for s in range(RING):
                            step(i * RING + s, s)
                    for s in range(RING):
                        step((n_it - 1) * RING + s, s, more=s + 1 < RING)

        segment_softmax(nc, C, f"{n}", E, edge)

        with Scope(nc, f"gata{n}") as M:
            idx = [M.sb(f"idx{s}", [P, G], I32) for s in range(RING)]
            got = [M.sb(f"got{s}", [P, G * D]) for s in range(RING)]
            msg = [M.sb(f"msg{s}", [P, G * DW]) for s in range(RING)]
            pick = [M.sb(f"pick{s}", [P, G * P]) for s in range(RING)]
            sum_ps = [M.ps(f"sum_ps{s}", [P, 512]) for s in range(LAG * G)]
            idxed, gate, weighed, copied, summed, added, cleared = (
                M.sem(s) for s in ("idxed", "gate", "weighed", "copied", "summed", "added", "cleared"))
            arrived = M.sems("arrived", RING)
            n_it = KT // (RING * G)
            with nc.Block() as block:
                @block.gpsimd
                def _(pool):
                    with pool.Fori(0, n_it) as i:
                        for s in range(RING):
                            pool.wait_ge(idxed, i * RING + s + 1)
                            nc.gpsimd.sem_inc(gate, 1)
                            for t in range(G):
                                nc.gpsimd.indirect_dma_start(
                                    got[s][:, t * D:(t + 1) * D], None, table[:, 0:D],
                                    bass.IndirectOffsetOnAxis(ap=idx[s][:, t:t + 1], axis=0)).then_inc(arrived[s], 16)

                @block.scalar
                def _(act):
                    with act.Fori(0, n_it) as i:
                        for s in range(RING):
                            u = i * RING + s
                            act.wait_ge(weighed, u + 1)
                            nc.scalar.activation(idx[s][:, :], E.src[:, ds(u * G, G)], ACT.Copy).then_inc(idxed, 1)
                            act.wait_ge(summed, u + 1)
                            nc.scalar.activation(
                                msg[s][:, :].rearrange("p (t f) -> p t f", t=G)[:, :, D:DW],
                                edge[:, ds(u * (G * 4), G * 4)].rearrange("p (t h) -> p t h", t=G),
                                ACT.Copy).then_inc(copied, 1)

                @block.vector
                def _(dve):
                    blk_regs = [dve.alloc_register(f"gata{n}_blk{t}") for t in range(G)]

                    def choose(u, s):
                        dve.wait_ge(summed, u + 1)
                        nc.vector.tensor_tensor(
                            pick[s][:, :].rearrange("p (t d) -> p t d", t=G),
                            C.ramp[:, :].unsqueeze(1).to_broadcast([P, G, P]),
                            E.low[:, ds(u * G, G)].unsqueeze(2).to_broadcast([P, G, P]), ALU.is_equal)

                    def weigh(u, s, t):
                        return nc.vector.tensor_tensor(
                            msg[s][:, t * DW:t * DW + D].rearrange("p (h c) -> p h c", h=4),
                            got[s][:, t * D:(t + 1) * D].rearrange("p (h c) -> p h c", h=4),
                            edge[:, ds(u * (G * 4) + t * 4, 4)].unsqueeze(2).to_broadcast([P, 4, 64]), ALU.mult)

                    def take(u, s, t, blk):
                        dve.wait_ge(added, u * G + (LAG * G + t))
                        dst = acc[:, ds(blk * DW, DW)]
                        nc.vector.tensor_tensor(dst, dst, sum_ps[(s % LAG) * G + t][:, 0:DW], ALU.add).then_inc(added, 1)

                    def step(u, s, arrivals, more=True):
                        blks = load_blocks(dve, blk_regs, block_of[0:1, ds(u * G, G)])
                        f = (s + LAG) % RING
                        if more:
                            choose(u + LAG, f)
                            dve.wait_ge(arrived[f], arrivals)
                        for t in range(G):
                            if more:
                                last = weigh(u + LAG, f, t)
                            if t == 0:
                                dve.wait_ge(summed, u + RING + 1)
                            take(u, s, t, blks[t])
                        if more:
                            last.then_inc(weighed, 1)

                    nc.vector.memset(acc[:, :], 0.0).then_inc(cleared, 1)
                    dve.sem_inc(weighed, RING)
                    dve.sem_inc(added, LAG * G)
                    dve.wait_ge(cleared, 1)
                    for u in range(LAG):
                        choose(u, u)
                        dve.wait_ge(arrived[u], 16 * G)
                        for t in range(G):
                            last = weigh(u, u, t)
                        last.then_inc(weighed, 1)
                    with dve.Fori(0, n_it - 1) as i:
                        for s in range(RING):
                            step(i * RING + s, s, (i + (1 + (s + LAG) // RING)) * (16 * G))
                    for s in range(RING):
                        step((n_it - 1) * RING + s, s, n_it * 16 * G, more=s + LAG < RING)

                @block.tensor
                def _(pe):
                    pe.sem_inc(summed, RING)
                    with pe.Fori(0, n_it) as i:
                        for s in range(RING):
                            u = i * RING + s
                            pe.wait_ge(copied, u + 1)
                            pe.wait_ge(weighed, u + RING + 1)
                            pe.wait_ge(added, u * G + G)
                            for t in range(G):
                                mm = nc.tensor.matmul(sum_ps[(s % LAG) * G + t][:, 0:DW], pick[s][:, t * P:(t + 1) * P],
                                                      msg[s][:, t * DW:(t + 1) * DW], start=True, stop=True)
                            mm.then_inc(summed, 1)


def gat_output(nc, a, n, acc, h, x):
    DW = D + 4
    with Scope(nc, f"gato{n}") as L:
        bias = L.sb("bias", [P, D])
        inv = L.sb("inv", [P, NB * 4])
        norm = L.sb("norm", [P, NB])
        ld, chain, squares, root = L.sem("ld"), L.sem("chain"), L.sem("squares"), L.sem("root")
        a3 = acc[:, :].rearrange("p (b f) -> p b f", f=DW)
        h3 = h[:, :].rearrange("p (b d) -> p b d", d=D)
        i3 = inv[:, :].rearrange("p (b h) -> p b h", h=4)
        with nc.Block() as block:
            @block.sync
            def _(sp):
                sp.dma_start(bias[:, :], broadcast_rows(a[f"L1_gnn_b{n}"])).then_inc(ld, 16)

            @block.vector
            def _(dve):
                link = serial(dve, chain)
                link(nc.vector.tensor_scalar(i3, a3[:, :, D:DW], 1e-16, None, ALU.add))
                link(nc.vector.reciprocal(inv[:, :], inv[:, :]))
                for hd in range(4):
                    c = slice(hd * 64, (hd + 1) * 64)
                    last = nc.vector.tensor_tensor(h3[:, :, c], a3[:, :, c], i3[:, :, hd:hd + 1].to_broadcast([P, NB, 64]),
                                                   ALU.mult)
                link(last)
                dve.wait_ge(ld, 16)
                link(nc.vector.tensor_tensor(h3, h3, bias[:, :].unsqueeze(1).to_broadcast([P, NB, D]), ALU.add))
                if n < 3:
                    link(nc.vector.tensor_scalar(h[:, :], h[:, :], 0.0, None, ALU.max))
                else:
                    sq = acc[:, 0:NB * D]
                    link(nc.vector.tensor_tensor(sq, h[:, :], h[:, :], ALU.mult))
                    nc.vector.tensor_reduce(norm[:, :], sq.rearrange("p (b d) -> p b d", d=D), AX.X,
                                            ALU.add).then_inc(squares, 1)
                    dve.wait_ge(root, 1)
                    link(nc.vector.tensor_scalar(norm[:, :], norm[:, :], 1e-12, None, ALU.max))
                    link(nc.vector.reciprocal(norm[:, :], norm[:, :]))
                    link(nc.vector.tensor_tensor(h3, h3, norm[:, :].unsqueeze(2).to_broadcast([P, NB, D]), ALU.mult))
                    link(nc.vector.tensor_tensor(x[:, :], x[:, :], h[:, :], ALU.add))

            if n == 3:
                @block.scalar
                def _(act):
                    act.wait_ge(squares, 1)
                    nc.scalar.activation(norm[:, :], norm[:, :], ACT.Sqrt).then_inc(root, 1)


def router(nc, C, S, a, E, block_of, xn, table, oht_dst, gates):
    KT, F = E.plan.out, 20
    with Scope(nc, "rt") as L:
        dst3 = L.sb("dst3", [P, 3 * NB * 4], BF16)
        with Scope(nc, "rtn") as M:
            w = M.sb("w", [P, 2 * 16])
            att = M.sb("att", [P, 32])
            all_in = M.sb("all_in", [P, NB * 24])
            prod = M.sb("prod", [P, NB * 16])
            rest = M.sb("rest", [P, NB * 4])
            block_in = M.sb("block_in", [P, D])
            hT = M.sb("hT", [P, D])
            t_ps = M.ps("t_ps", [P, 512])
            o_ps = M.ps("o_ps", [P, 512])
            ld, chain, taken, flipped, copied, made, kept, ready, stored = (
                M.sem(s) for s in ("ld", "chain", "taken", "flipped", "copied", "made", "kept", "ready", "stored"))
            a3 = all_in[:, :].rearrange("p (b f) -> p b f", f=24)
            with nc.Block() as block:
                @block.sync
                def _(sp):
                    loads(sp, ld, [(w[:, k * 16:(k + 1) * 16], a["L1_ffn_W_gat"][k * P:(k + 1) * P, :]) for k in range(2)]
                          + [(att[:, 0:16], broadcast_rows(a["L1_ffn_att_src"].rearrange("h c -> (h c)"))),
                             (att[:, 16:], broadcast_rows(a["L1_ffn_att_dst"].rearrange("h c -> (h c)")))])
                    sp.wait_ge(ready, 1)
                    sp.dma_start(table.rearrange("(b p) f -> p b f", p=P), a3[:, :, 0:F]).then_inc(stored, 16)
                    sp.wait_ge(stored, 16)

                @block.scalar
                def _(act):
                    with act.Fori(0, NB) as b:
                        act.wait_ge(flipped, b)
                        nc.scalar.activation(block_in[:, :], xn[:, ds(b * D, D)], ACT.Copy).then_inc(taken, 1)
                        act.wait_ge(flipped, b + 1)
                        act.wait_ge(made, b)
                        nc.scalar.activation(hT[:, :], t_ps[:, 0:D], ACT.Copy).then_inc(copied, 1)

                @block.tensor
                def _(pe):
                    pe.wait_ge(ld, 64)
                    with pe.Fori(0, NB) as b:
                        pe.wait_ge(taken, b + 1)
                        pe.wait_ge(copied, b)
                        for k in range(2):
                            mm = nc.tensor.transpose(t_ps[:, k * P:(k + 1) * P], block_in[:, k * P:(k + 1) * P], C.ident[:, :])
                        mm.then_inc(flipped, 1)
                        pe.wait_ge(copied, b + 1)
                        pe.wait_ge(kept, b)
                        for k in range(2):
                            mm = nc.tensor.matmul(o_ps[:, 0:16], hT[:, k * P:(k + 1) * P], w[:, k * 16:(k + 1) * 16],
                                                  start=k == 0, stop=k == 1)
                        mm.then_inc(made, 1)

                @block.vector
                def _(dve):
                    link = serial(dve, chain)
                    with dve.Fori(0, NB) as b:
                        dve.wait_ge(made, b + 1)
                        nc.vector.tensor_copy(all_in[:, ds(b * 24, 16)], o_ps[:, 0:16]).then_inc(kept, 1)
                    dve.wait_ge(kept, NB)
                    dve.wait_ge(ld, 64)
                    p3 = prod[:, :].rearrange("p (b f) -> p b f", f=16)
                    for g in range(2):
                        link(nc.vector.tensor_tensor(p3, a3[:, :, 0:16], att[:, g * 16:(g + 1) * 16].unsqueeze(1)
                                                     .to_broadcast([P, NB, 16]), ALU.mult))
                        link(nc.vector.tensor_reduce(a3[:, :, 16 + 4 * g:20 + 4 * g],
                                                     prod[:, :].rearrange("p (b h c) -> p b h c", h=4, c=4), AX.X, ALU.add))
                    dve.sem_inc(ready, 1)
                    parts = [dst3[:, :].rearrange("p (b j h) -> p j b h", j=3, h=4)[:, j] for j in range(3)]
                    split_bf16(nc, link, a3[:, :, 20:24], parts, rest[:, :].rearrange("p (b h) -> p b h", h=4))

        msg = L.sb("msg", [P, KT * F])
        edge = L.sb("edge", [P, KT * 4])
        with Scope(nc, "rts") as M:
            idx = [M.sb(f"idx{s}", [P, G], I32) for s in range(RING)]
            got = [M.sb(f"got{s}", [P, G * F]) for s in range(RING)]
            od_ = [M.sb(f"od{s}", [P, G * P], BF16) for s in range(RING)]
            d_ps = [M.ps(f"d_ps{s}", [P, 512]) for s in range(RING)]
            idxed, gate, looked, taken = (M.sem(s) for s in ("idxed", "gate", "looked", "taken"))
            arrived, came = M.sems("arrived", RING), M.sems("came", RING)
            n_it = KT // (RING * G)
            with nc.Block() as block:
                @block.gpsimd
                def _(pool):
                    with pool.Fori(0, n_it) as i:
                        for s in range(RING):
                            pool.wait_ge(idxed, i * RING + s + 1)
                            nc.gpsimd.sem_inc(gate, 1)
                            for t in range(G):
                                nc.gpsimd.indirect_dma_start(
                                    got[s][:, t * F:(t + 1) * F], None, table,
                                    bass.IndirectOffsetOnAxis(ap=idx[s][:, t:t + 1], axis=0)).then_inc(arrived[s], 16)

                @block.scalar
                def _(act):
                    with act.Fori(0, n_it) as i:
                        for s in range(RING):
                            u = i * RING + s
                            act.wait_ge(taken, u + 1)
                            nc.scalar.activation(idx[s][:, :], E.src[:, ds(u * G, G)], ACT.Copy).then_inc(idxed, 1)

                @block.sync
                def _(sp):
                    with sp.Fori(0, n_it) as i:
                        for s in range(RING):
                            u = i * RING + s
                            sp.wait_ge(looked, u + 1)
                            sp.dma_start(od_[s][:, :], oht_dst[:, ds(u * (G * P), G * P)]).then_inc(came[s], 16)

                @block.tensor
                def _(pe):
                    blk_regs = [pe.alloc_register(f"rts_blk{t}") for t in range(RING * G)]
                    pe.sem_inc(looked, RING)
                    with pe.Fori(0, n_it) as i:
                        blks = load_blocks(pe, blk_regs, block_of[0:1, ds(i * (RING * G), RING * G)])
                        for s in range(RING):
                            u = i * RING + s
                            pe.wait_ge(came[s], i * 16 + 16)
                            pe.wait_ge(taken, u + 1)
                            for t in range(G):
                                for j in range(3):
                                    mm = nc.tensor.matmul(d_ps[s][:, t * 4:(t + 1) * 4], od_[s][:, t * P:(t + 1) * P],
                                                          dst3[:, ds(blks[s * G + t] * 12 + j * 4, 4)],
                                                          start=j == 0, stop=j == 2)
                            mm.then_inc(looked, 1)

                @block.vector
                def _(dve):
                    dve.sem_inc(taken, RING)
                    with dve.Fori(0, n_it) as i:
                        for s in range(RING):
                            u = i * RING + s
                            dve.wait_ge(arrived[s], (i + 1) * (16 * G))
                            nc.vector.tensor_copy(msg[:, ds(u * (G * F), G * F)], got[s][:, :])
                            dve.wait_ge(looked, u + RING + 1)
                            nc.vector.tensor_tensor(
                                edge[:, ds(u * (G * 4), G * 4)].rearrange("p (t h) -> p t h", t=G),
                                got[s][:, :].rearrange("p (t f) -> p t f", t=G)[:, :, 16:20],
                                d_ps[s][:, 0:G * 4].rearrange("p (t h) -> p t h", t=G), ALU.add).then_inc(taken, 1)

        segment_softmax(nc, C, "r", E, edge)

        acc = L.sb("acc", [P, NB * F])
        with Scope(nc, "rta") as M:
            pick = [M.sb(f"pick{s}", [P, G * P]) for s in range(RING)]
            sum_ps = [M.ps(f"sum_ps{s}", [P, 512]) for s in range(RING)]
            chain, ready, picked, summed, added = (M.sem(s) for s in ("chain", "ready", "picked", "summed", "added"))
            m3 = msg[:, :].rearrange("p (k f) -> p k f", f=F)
            e3 = edge[:, :].rearrange("p (k h) -> p k h", h=4)
            n_it = KT // (RING * G)
            with nc.Block() as block:
                @block.vector
                def _(dve):
                    blk_regs = [dve.alloc_register(f"rta_blk{t}") for t in range(G)]
                    link = serial(dve, chain)
                    nc.vector.memset(acc[:, :], 0.0)
                    for hd in range(4):
                        c = slice(hd * 4, hd * 4 + 4)
                        nc.vector.tensor_tensor(m3[:, :, c], m3[:, :, c], e3[:, :, hd:hd + 1].to_broadcast([P, KT, 4]),
                                                ALU.mult)
                    link(nc.vector.tensor_copy(m3[:, :, 16:20], e3))
                    dve.sem_inc(ready, 1)

                    def choose(u, s):
                        nc.vector.tensor_tensor(
                            pick[s][:, :].rearrange("p (t d) -> p t d", t=G),
                            C.ramp[:, :].unsqueeze(1).to_broadcast([P, G, P]),
                            E.low[:, ds(u * G, G)].unsqueeze(2).to_broadcast([P, G, P]),
                            ALU.is_equal).then_inc(picked, 1)

                    def step(u, s, more=True):
                        blks = load_blocks(dve, blk_regs, block_of[0:1, ds(u * G, G)])
                        if more:
                            choose(u + LAG, (s + LAG) % RING)
                        dve.wait_ge(summed, u + 1)
                        for t in range(G):
                            dve.wait_ge(added, u * G + (t + LAG * G))
                            dst = acc[:, ds(blks[t] * F, F)]
                            nc.vector.tensor_tensor(dst, dst, sum_ps[s][:, t * F:(t + 1) * F], ALU.add).then_inc(added, 1)

                    dve.sem_inc(added, LAG * G)
                    for u in range(LAG):
                        choose(u, u)
                    with dve.Fori(0, n_it - 1) as i:
                        for s in range(RING):
                            step(i * RING + s, s)
                    for s in range(RING):
                        step((n_it - 1) * RING + s, s, more=s + LAG < RING)

                @block.tensor
                def _(pe):
                    pe.wait_ge(ready, 1)
                    with pe.Fori(0, n_it) as i:
                        for s in range(RING):
                            u = i * RING + s
                            pe.wait_ge(picked, u + 1)
                            pe.wait_ge(added, u * G + (LAG - 1) * G)
                            for t in range(G):
                                mm = nc.tensor.matmul(sum_ps[s][:, t * F:(t + 1) * F], pick[s][:, t * P:(t + 1) * P],
                                                      msg[:, ds((u * G + t) * F, F)], start=True, stop=True)
                            mm.then_inc(summed, 1)
        with Scope(nc, "rto") as M:
            rows = M.sb("rows", [P, 48])
            inv = M.sb("inv", [P, NB * 4])
            agg = M.sb("agg", [P, NB * 16])
            norm = M.sb("norm", [P, NB * 16])
            logits = M.sb("logits", [P, NB * 4])
            ld, chain = M.sem("ld"), M.sem("chain")
            a3 = acc[:, :].rearrange("p (b f) -> p b f", f=F)
            g3 = agg[:, :].rearrange("p (b f) -> p b f", f=16)
            i3 = inv[:, :].rearrange("p (b h) -> p b h", h=4)
            with nc.Block() as block:
                @block.sync
                def _(sp):
                    loads(sp, ld, [(rows[:, 0:16], broadcast_rows(a["L1_ffn_b_gat"])),
                                   (rows[:, 16:32], broadcast_rows(a["L1_ffn_ln_gamma"])),
                                   (rows[:, 32:48], broadcast_rows(a["L1_ffn_ln_beta"]))])
                    sp.wait_ge(ld, 48)

                @block.vector
                def _(dve):
                    link = serial(dve, chain)
                    link(nc.vector.tensor_scalar(i3, a3[:, :, 16:20], 1e-16, None, ALU.add))
                    link(nc.vector.reciprocal(inv[:, :], inv[:, :]))
                    for hd in range(4):
                        c = slice(hd * 4, hd * 4 + 4)
                        last = nc.vector.tensor_tensor(g3[:, :, c], a3[:, :, c], i3[:, :, hd:hd + 1].to_broadcast([P, NB, 4]),
                                                       ALU.mult)
                    link(last)
                    dve.wait_ge(ld, 48)
                    link(nc.vector.tensor_tensor(g3, g3, rows[:, 0:16].unsqueeze(1).to_broadcast([P, NB, 16]), ALU.add))
            layer_norm(nc, "rt", agg, norm, width=16, scale=rows[:, 16:32], shift=rows[:, 32:48])
            with nc.Block() as block:
                @block.vector
                def _(dve):
                    link = serial(dve, chain, 7 - 7 + 4)
                    link(nc.vector.tensor_reduce(logits[:, :].rearrange("p (b e) -> p b e", e=4),
                                                 norm[:, :].rearrange("p (b h e) -> p b e h", h=4, e=4), AX.X, ALU.add))
                    link(nc.vector.tensor_scalar(logits[:, :], logits[:, :], 0.25, None, ALU.mult))
            gating(nc, "rt", logits, gates, 4)


def load_nodes(nc, x_in, x):
    full = N // P
    with Scope(nc, "nodes") as L:
        zeroed, got = L.sem("zeroed"), L.sem("got")
        with nc.Block() as block:
            @block.vector
            def _(dve):
                nc.vector.memset(x[:, full * D:], 0.0).then_inc(zeroed, 1)

            @block.sync
            def _(sp):
                sp.dma_start(x[:, 0:full * D].rearrange("p (b d) -> p b d", d=D),
                             x_in[0:full * P, :].rearrange("(b p) d -> p b d", p=P)).then_inc(got, 16)
                sp.wait_ge(zeroed, 1)
                sp.dma_start(x[0:N - full * P, full * D:], x_in[full * P:N, :]).then_inc(got, 16)
                sp.wait_ge(got, 32)


def store_nodes(nc, x, out):
    full = N // P
    with Scope(nc, "out") as L:
        put = L.sem("put")
        with nc.Block() as block:
            @block.sync
            def _(sp):
                sp.dma_start(out[0:full * P, :].rearrange("(b p) d -> p b d", p=P),
                             x[:, 0:full * D].rearrange("p (b d) -> p b d", d=D)).then_inc(put, 16)
                sp.dma_start(out[full * P:N, :], x[0:N - full * P, full * D:]).then_inc(put, 16)
                sp.wait_ge(put, 32)


GNN = edge_plan(53125 + 625, 16)
ROUTE = edge_plan(32768 + N, 2)


def program(nc, a, out, stop=9):
    with Scope(nc, "all") as S:
        C = make_constants(nc, S)
        x = S.sb("x", [P, NB * D])
        load_nodes(nc, a["x"], x)
        gnn_sorted = nc.dram_tensor("gnn_sorted", [GNN.out * P, GNN.width], F32).ap()
        route_sorted = nc.dram_tensor("route_sorted", [ROUTE.out * P, ROUTE.width], F32).ap()
        table = nc.dram_tensor("table", [NPAD, D], F32).ap()
        route_table = nc.dram_tensor("route_table", [NPAD, 20], F32).ap()
        oht_src = nc.dram_tensor("oht_src", [P, GNN.out * P], BF16).ap()
        oht_dst = nc.dram_tensor("oht_dst", [P, GNN.out * P], BF16).ap()
        block_of = S.sb("block_of", [1, GNN.out], I32)
        if stop in (0, 1, 2, 9):
            sort_edges(nc, C, GNN, "g", a["gnn_src"], a["gnn_dst"], a["gnn_attr"], gnn_sorted, block_of)
            with Scope(nc, "gnn") as T:
                E = Edges(T, "g", GNN)
                with Scope(nc, "recs") as U:
                    rec = U.sb("rec", [P, GNN.out * GNN.width])
                    prepare_edges(nc, C, E, "g", gnn_sorted, rec)
                    equivariant_layer(nc, C, T, a, E, block_of, x, table)
                if stop >= 1:
                    with Scope(nc, "ffn0") as U:
                        xn = U.sb("xn", [P, NB * D])
                        rows = U.sb("rows", [P, 2 * D])
                        load_rows(nc, "ffn0", rows, [a["L0_ffn_gamma"], a["L0_ffn_beta"]])
                        layer_norm(nc, "f0", x, xn)
                        layer_norm(nc, "f1", xn, xn, scale=rows[:, 0:D], shift=rows[:, D:])
                        experts(nc, C, "0", xn, x, 8, a, "L0_ffn_W1", "L0_ffn_b1", "L0_ffn_W2", "L0_ffn_b2",
                                wr="L0_ffn_Wr", br="L0_ffn_br")
                if stop >= 2:
                    with Scope(nc, "gats") as U:
                        h = U.sb("h", [P, NB * D])
                        acc = U.sb("acc", [P, NB * (D + 4)])
                        layer_norm(nc, "g", x, h)
                        turned_one_hots(nc, C, "g", E, [(E.src_low, oht_src), (E.low_b, oht_dst)])
                        for n in (1, 2, 3):
                            gat_layer(nc, C, U, a, n, E, block_of, h, acc, table, oht_src, oht_dst)
                            gat_output(nc, a, n, acc, h, x)
        if stop >= 3:
            with Scope(nc, "route") as T:
                xn = T.sb("xn", [P, NB * D])
                gates = T.sb("gates", [P, NB * 4])
                layer_norm(nc, "r", x, xn)
                with Scope(nc, "routes") as U:
                    sort_edges(nc, C, ROUTE, "r", a["route_src"], a["route_dst"], None, route_sorted, block_of)
                    E = Edges(U, "r", ROUTE)
                    rec = U.sb("rec", [P, ROUTE.out * ROUTE.width])
                    prepare_edges(nc, C, E, "r", route_sorted, rec)
                    turned_one_hots(nc, C, "r", E, [(E.low_b, oht_dst)])
                    router(nc, C, U, a, E, block_of, xn, route_table, oht_dst, gates)
                experts(nc, C, "1", xn, x, 4, a, "L1_ffn_W1", "L1_ffn_b1", "L1_ffn_W2", "L1_ffn_b2", gates=gates)
        store_nodes(nc, x, out)


def load_rows(nc, tag, rows, vectors):
    with Scope(nc, f"rows{tag}") as L:
        ld = L.sem("ld")
        with nc.Block() as block:
            @block.sync
            def _(sp):
                sp.wait_ge(ld, loads(sp, ld, [(rows[:, k * D:(k + 1) * D], broadcast_rows(v))
                                              for k, v in enumerate(vectors)]))


def cut_edges(plan, src, dst, loops):
    fill = plan.tiles * P - plan.edges
    loops = np.arange(loops, dtype=np.int32)
    return (np.concatenate([src, loops, np.zeros(fill, np.int32)]).reshape(P, -1),
            np.concatenate([dst, loops, np.full(fill, KEY_PAD, np.int32)]).reshape(P, -1))


def layout(inputs):
    a = {k: np.ascontiguousarray(v) for k, v in inputs.items()}
    src, dst = a.pop("src"), a.pop("dst")
    e4, e8 = a.pop("edge_attr_4"), a.pop("edge_attr_8")
    a["gnn_src"], a["gnn_dst"] = cut_edges(GNN, src, dst, 625)
    route = a.pop("L1_ffn_edge_index")
    a["route_src"], a["route_dst"] = cut_edges(ROUTE, route[0], route[1], N)
    attr = np.zeros((GNN.tiles * P, GNN.width), np.float32)
    attr[:len(src), 2:6] = e4
    attr[:len(src), 6:14] = e8
    a["gnn_attr"] = attr.reshape(P, -1)
    z = np.zeros((NPAD, 1), np.float32)
    z[:N] = a["node_vec1"]
    a["node_vec1"] = np.ascontiguousarray(z.reshape(NB, P).T)
    for b in ("L0_ffn_b1", "L1_ffn_b1"):
        a[b] = np.ascontiguousarray(a[b].reshape(-1, P).T)
    return a


def kernel(**inputs):
    import concourse.bacc as _bacc
    from concourse.bass_utils import run_bass_kernel_spmd as _run

    arrays = {f"in_{k}": v for k, v in layout(inputs).items()}
    nc = _bacc.Bacc("TRN2", target_bir_lowering=False, num_devices=1)
    a = {k[3:]: nc.dram_tensor(k, v.shape, mybir.dt.from_np(v.dtype), kind="ExternalInput").ap()
         for k, v in arrays.items()}
    out = nc.dram_tensor("out_0", (N, D), F32, kind="ExternalOutput").ap()
    program(nc, a, out)
    r = _run(nc, [arrays], core_ids=[0])
    return r.results[0]["out_0"]
```

```python
import numpy as np
from contextlib import ExitStack
from collections import namedtuple

import concourse.bass as bass
from concourse import mybir

F32 = mybir.dt.float32
BF16 = mybir.dt.bfloat16
I32 = mybir.dt.int32
ALU = mybir.AluOpType
ACT = mybir.ActivationFunctionType
AX = mybir.AxisListType
ds = bass.ds

P = 128
N = 3125
D = 256
NB = -(-N // P)
NPAD = NB * P
SORT_G = 3
G = 4
EARLY = 12
LAG = 2
RING = 4
FAR = -1.0e30
KEY_PAD = NPAD


Plan = namedtuple("Plan", "edges tiles out width rows")
Constants = namedtuple("Constants", "ident ident_b ramp ramp_b part before upper ones")


def edge_plan(edges, width):
    step = RING * SORT_G
    tiles = -(-(-(-edges // P)) // step) * step
    fill = tiles * P - edges
    worst = (edges + NB * (P - 1)) // P + -(-fill // P)
    out = -(-worst // (RING * G)) * RING * G
    return Plan(edges, tiles, out, width, out // G)


def serial(eng, sem, base=0):
    n = [0]

    def step(ins):
        ins.then_inc(sem, 1)
        n[0] += 1
        eng.wait_ge(sem, base + n[0])
    return step


def there(v, groups):
    return not isinstance(v, int) or 0 <= v < groups


def after(eng, sem, count):
    if not isinstance(count, int) or count > 0:
        eng.wait_ge(sem, count)


def run_steps(eng, step, groups, ahead, begin=None, peeled=1):
    n_it = groups // RING
    begin = begin or (lambda i: None)
    for u in range(-ahead, peeled * RING):
        if u >= 0 and u % RING == 0:
            begin(u // RING)
        step(u, u % RING, u // RING)
    with eng.Fori(peeled, n_it - 1) as i:
        begin(i)
        for s in range(RING):
            step(i * RING + s, s, i)
    begin(n_it - 1)
    for u in range((n_it - 1) * RING, groups):
        step(u, u % RING, u // RING)


def turn_nodes(nc, M, C, block, take, width, parts, consume, multiply=None, ready=()):
    rows = width // parts
    block_in = [M.sb(f"block_in{s}", [P, width]) for s in range(2)]
    turned = [M.sb(f"turned{s}", [rows, parts * P]) for s in range(2)]
    t_ps = [M.ps(f"t_ps{s}", [P, 512]) for s in range(2)]
    o_ps = [M.ps(f"o_ps{s}", [P, 512]) for s in range(2)]
    taken, flipped, copied, made, consumed, gate = (
        M.sem(s) for s in ("taken", "flipped", "copied", "made", "consumed", "gate"))

    @block.scalar
    def _(act):
        def step(u, s, i):
            if there(u + 2, NB):
                after(act, flipped, u + 1)
                take(u + 2, block_in[s % 2]).then_inc(taken, 1)
            if there(u + 1, NB):
                act.wait_ge(flipped, u + 2)
                after(act, consumed, u)
                nc.scalar.activation(turned[(s + 1) % 2][:, :], t_ps[(s + 1) % 2][0:rows, 0:parts * P],
                                     ACT.Copy).then_inc(copied, 1)
        run_steps(act, step, NB, 2)

    @block.tensor
    def _(pe):
        def step(u, s, i):
            if there(u + 1, NB):
                pe.wait_ge(taken, u + 2)
                after(pe, copied, u)
                pe.sem_inc(gate, 1)
                for k in range(parts):
                    mm = nc.tensor.transpose(t_ps[(s + 1) % 2][0:rows, k * P:(k + 1) * P],
                                             block_in[(s + 1) % 2][:, k * rows:(k + 1) * rows], C.ident[:, :])
                mm.then_inc(flipped, 1)
            if there(u, NB) and multiply:
                pe.wait_ge(copied, u + 1)
                after(pe, consumed, u - 1)
                pe.sem_inc(gate, 1)
                multiply(turned[s % 2], o_ps[s % 2]).then_inc(made, 1)
        for sem, count in ready:
            pe.wait_ge(sem, count)
        run_steps(pe, step, NB, 1)

    def consumer(dve):
        def step(u, s, i):
            dve.wait_ge(made if multiply else copied, u + 1)
            consume(u, s, i, turned[s % 2], o_ps[s % 2]).then_inc(consumed, 1)
        run_steps(dve, step, NB, 0)
        dve.wait_ge(consumed, NB)
    return consumer


def over_nodes(eng, step):
    with eng.Fori(0, NB // RING) as i:
        for s in range(RING):
            step(i * RING + s, s, i)
    for b in range(NB // RING * RING, NB):
        step(b, b % RING, b // RING)


class Blocks:

    def __init__(self, eng, name, block_of):
        self.eng, self.block_of = eng, block_of
        self.regs = [eng.alloc_register(f"{name}{t}") for t in range(RING * G)]

    def load(self, i):
        self.eng.load(self.regs, self.block_of[0:1, ds(i * (RING * G), RING * G)])
        self.of = [self.eng.snap(r, min_val=0, max_val=NB - 1) for r in self.regs]


class Scope:

    def __init__(self, nc, name):
        self.nc, self.name, self.ctx, self.used = nc, name, ExitStack(), []

    def __enter__(self):
        self.ctx.__enter__()
        return self

    def __exit__(self, *a):
        if self.used and a[0] is None:
            self.nc.clear_and_free_semaphores(self.used)
            self.nc.all_engine_barrier()
        return self.ctx.__exit__(*a)

    def sb(self, name, shape, dt=F32):
        return self.ctx.enter_context(self.nc.sbuf_tensor(f"{self.name}_{name}", shape, dt))

    def ps(self, name, shape, dt=F32):
        return self.ctx.enter_context(self.nc.psum_tensor(f"{self.name}_{name}", shape, dt))

    def sem(self, name):
        self.used.append(self.nc.alloc_semaphore(f"{self.name}_{name}"))
        return self.used[-1]

    def sems(self, name, n):
        return [self.sem(f"{name}{i}") for i in range(n)]


def make_constants(nc, S):
    c = Constants(
        ident=S.sb("ident", [P, P]), ident_b=S.sb("ident_b", [P, P], BF16),
        ramp=S.sb("ramp", [P, P]), ramp_b=S.sb("ramp_b", [P, P], BF16),
        part=S.sb("part", [P, 1]), before=S.sb("before", [P, P]), upper=S.sb("upper", [P, P]),
        ones=S.sb("ones", [P, 1]))
    with Scope(nc, "const") as L:
        ramp_i = L.sb("ramp_i", [P, P], I32)
        part_i = L.sb("part_i", [P, 1], I32)
        made = L.sem("made")
        chain = L.sem("chain")
        with nc.Block() as block:
            @block.gpsimd
            def _(pool):
                nc.gpsimd.iota(ramp_i[:, :], [[1, P]], base=0, channel_multiplier=0).then_inc(made, 1)
                nc.gpsimd.iota(part_i[:, :], [[0, 1]], base=0, channel_multiplier=1).then_inc(made, 1)

            @block.vector
            def _(dve):
                link = serial(dve, chain)
                dve.wait_ge(made, 2)
                nc.vector.memset(c.ones[:, :], 1.0)
                link(nc.vector.tensor_copy(c.ramp[:, :], ramp_i[:, :]))
                link(nc.vector.tensor_copy(c.ramp_b[:, :], ramp_i[:, :]))
                link(nc.vector.tensor_copy(c.part[:, :], part_i[:, :]))
                link(nc.vector.tensor_scalar(c.ident[:, :], c.ramp[:, :], c.part[:, :], None, ALU.is_equal))
                link(nc.vector.tensor_scalar(c.before[:, :], c.ramp[:, :], c.part[:, :], None, ALU.is_lt))
                link(nc.vector.tensor_scalar(c.upper[:, :], c.ramp[:, :], c.part[:, :], None, ALU.is_gt))
                link(nc.vector.tensor_copy(c.ident_b[:, :], c.ident[:, :]))
    return c


def sort_edges(nc, C, plan, tag, src, dst, attr, sorted_dram, block_of):
    T, KT, W, g = plan.tiles, plan.out, plan.width, SORT_G
    H = NB + 1
    with Scope(nc, f"sort{tag}") as L:
        src_i = L.sb("src_i", [P, T], I32)
        dst_i = L.sb("dst_i", [P, T], I32)
        blk_i = L.sb("blk_i", [P, T], I32)
        low_i = L.sb("low_i", [P, T], I32)
        key = L.sb("key", [P, T])
        key1 = L.sb("key1", [P, T])
        blk = L.sb("blk", [P, T], BF16)
        blk128 = L.sb("blk128", [P, T], BF16)
        low = L.sb("low", [P, T], BF16)
        rec = L.sb("rec", [P, T * W])
        rec3 = rec[:, :].rearrange("p (t w) -> p t w", w=W)
        empty = L.sb("empty", [P, 16 * W])
        oh_low = [L.sb(f"oh_low{s}", [P, g * P], BF16) for s in range(RING)]
        oh_blk = [L.sb(f"oh_blk{s}", [P, g * H], BF16) for s in range(RING)]
        zero_b = L.sb("zero_b", [P, P], BF16)
        hist_ps = L.ps("hist_ps", [P, 512])
        loaded, chain, blank, chain2 = L.sem("loaded"), L.sem("chain"), L.sem("blank"), L.sem("chain2")
        oh_made, hist_done = L.sem("oh_made"), L.sem("hist_done")

        def one_hots(s, t):
            nc.vector.tensor_tensor(
                oh_low[s][:, :].rearrange("p (t d) -> p t d", t=g),
                C.ramp_b[:, :].unsqueeze(1).to_broadcast([P, g, P]),
                low[:, ds(t, g)].unsqueeze(2).to_broadcast([P, g, P]), ALU.is_equal)
            return nc.vector.tensor_tensor(
                oh_blk[s][:, :].rearrange("p (t d) -> p t d", t=g),
                C.ramp_b[:, 0:H].unsqueeze(1).to_broadcast([P, g, H]),
                blk[:, ds(t, g)].unsqueeze(2).to_broadcast([P, g, H]), ALU.is_equal)

        with nc.Block() as block:
            @block.sync
            def _(sp):
                sp.dma_start(src_i[:, :], src).then_inc(loaded, 16)
                sp.dma_start(dst_i[:, :], dst).then_inc(loaded, 16)
                if attr is not None:
                    sp.dma_start(rec[:, :], attr).then_inc(loaded, 16)

            @block.gpsimd
            def _(pool):
                nc.gpsimd.memset(zero_b[:, :], 0.0)

            @block.vector
            def _(dve):
                link = serial(dve, chain)
                e3 = empty[:, :].rearrange("p (t w) -> p t w", w=W)
                link(nc.vector.memset(empty[:, :], 0.0))
                link(nc.vector.memset(e3[:, :, 1:2], -1.0))
                dve.wait_ge(loaded, 48 if attr is not None else 32)
                nc.vector.tensor_copy(key[:, :], dst_i[:, :])
                nc.vector.tensor_scalar(blk_i[:, :], dst_i[:, :], 7, None, ALU.arith_shift_right)
                nc.vector.tensor_scalar(low_i[:, :], dst_i[:, :], P - 1, None, ALU.bitwise_and)
                link(nc.vector.tensor_copy(rec3[:, :, 0], src_i[:, :]))
                nc.vector.tensor_copy(blk[:, :], blk_i[:, :])
                nc.vector.tensor_scalar(blk128[:, :], blk_i[:, :], float(P), None, ALU.mult)
                nc.vector.tensor_copy(low[:, :], low_i[:, :])
                link(nc.vector.tensor_scalar(key1[:, :], key[:, :], 1.0, None, ALU.add))
                link(nc.vector.scalar_tensor_tensor(key1[:, :], key[:, :], float(KEY_PAD), key1[:, :],
                                                    ALU.is_lt, ALU.mult))
                link(nc.vector.tensor_scalar(rec3[:, :, 1], key1[:, :], -1.0, None, ALU.add))

        with nc.Block() as block:
            @block.sync
            def _(sp):
                flat = sorted_dram.rearrange("(p k) w -> p (k w)", p=P)
                for k in range(0, KT, 16):
                    n = min(16, KT - k)
                    sp.dma_start(flat[:, k * W:(k + n) * W], empty[:, 0:n * W]).then_inc(blank, 16)
                sp.wait_ge(blank, 16 * -(-KT // 16))

            @block.vector
            def _(dve):
                with dve.Fori(0, T // (RING * g)) as i:
                    for s in range(RING):
                        dve.wait_ge(hist_done, i * RING + s + 1)
                        one_hots(s, i * (RING * g) + s * g).then_inc(oh_made, 1)

            @block.tensor
            def _(pe):
                nc.tensor.matmul(hist_ps[0:H, 0:P], zero_b[:, 0:H], zero_b[:, :], start=True, stop=False)
                pe.sem_inc(hist_done, RING)
                with pe.Fori(0, T // (RING * g)) as i:
                    for s in range(RING):
                        pe.wait_ge(oh_made, i * RING + s + 1)
                        for q in range(g):
                            mm = nc.tensor.matmul(hist_ps[0:H, 0:P], oh_blk[s][:, q * H:(q + 1) * H],
                                                  oh_low[s][:, q * P:(q + 1) * P], start=False, stop=False)
                        mm.then_inc(hist_done, 1)
                nc.tensor.matmul(hist_ps[0:H, 0:P], zero_b[:, 0:H], zero_b[:, :], start=False, stop=True)

        first = L.sb("first", [P, P])
        with Scope(nc, f"base{tag}") as B:
            hist = B.sb("hist", [P, P])
            run = B.sb("run", [P, P])
            zero = B.sb("zero", [P, P])
            room = B.sb("room", [P, 2])
            room_i = B.sb("room_i", [P, 2], I32)
            start_blk = B.sb("start_blk", [P, 1])
            tile_i = B.sb("tile_i", [P, KT], I32)
            tile_f = B.sb("tile_f", [P, KT])
            begun = B.sb("begun", [P, KT])
            ps = B.ps("ps", [P, 512])
            ps2 = B.ps("ps2", [P, 512])
            bchain, tiles_made, roomy, excl, cmp, summed = (
                B.sem(n) for n in ("chain", "tiles_made", "roomy", "excl", "cmp", "summed"))
            with nc.Block() as block:
                @block.gpsimd
                def _(pool):
                    nc.gpsimd.iota(tile_i[:, :], [[P, KT]], base=0, channel_multiplier=0).then_inc(tiles_made, 1)

                @block.vector
                def _(dve):
                    link = serial(dve, bchain)
                    nc.vector.memset(zero[:, :], 0.0)
                    link(nc.vector.tensor_copy(hist[0:H, :], hist_ps[0:H, 0:P]))
                    link(nc.vector.tensor_tensor_scan(run[0:H, :], zero[0:H, :], hist[0:H, :], 0.0,
                                                      ALU.add, ALU.add))
                    link(nc.vector.tensor_scalar(room[0:H, 0:1], run[0:H, P - 1:P], float(P - 1), None, ALU.add))
                    link(nc.vector.tensor_copy(room_i[0:H, 0:1], room[0:H, 0:1]))
                    link(nc.vector.tensor_scalar(room_i[0:H, 1:2], room_i[0:H, 0:1], -P, None, ALU.bitwise_and))
                    nc.vector.tensor_copy(room[0:H, 1:2], room_i[0:H, 1:2]).then_inc(roomy, 1)
                    dve.wait_ge(excl, 1)
                    link(nc.vector.tensor_copy(start_blk[0:H, :], ps[0:H, 0:1]))
                    link(nc.vector.tensor_tensor(run[0:H, :], run[0:H, :], hist[0:H, :], ALU.subtract))
                    link(nc.vector.tensor_scalar(first[0:H, :], run[0:H, :], start_blk[0:H, :], None, ALU.add))
                    dve.wait_ge(tiles_made, 1)
                    link(nc.vector.tensor_copy(tile_f[:, :], tile_i[:, :]))
                    nc.vector.tensor_scalar(begun[0:NB, :], tile_f[0:NB, :], start_blk[0:NB, :], None,
                                            ALU.is_ge).then_inc(cmp, 1)
                    dve.wait_ge(summed, 1)
                    link(nc.vector.tensor_scalar(block_of[0:1, 0:KT], ps2[0:1, 0:KT], -1.0, None, ALU.add))

                @block.tensor
                def _(pe):
                    pe.wait_ge(roomy, 1)
                    nc.tensor.matmul(ps[0:H, 0:1], C.upper[0:H, 0:H], room[0:H, 1:2],
                                     start=True, stop=True).then_inc(excl, 1)
                    pe.wait_ge(cmp, 1)
                    nc.tensor.matmul(ps2[0:1, 0:KT], C.ones[0:NB, 0:1], begun[0:NB, :],
                                     start=True, stop=True).then_inc(summed, 1)

        blkT_ps = [L.ps(f"blkT_ps{s}", [P, 1024], BF16) for s in range(2)]
        row_ps = [L.ps(f"row_ps{s}", [P, 512]) for s in range(2)]
        at_ps = [L.ps(f"at_ps{s}", [P, 512]) for s in range(2)]
        blkT = [L.sb(f"blkT{s}", [P, g * P]) for s in range(2)]
        snap = [L.sb(f"snap{s}", [P, g * P]) for s in range(2)]
        scrap = L.sb("scrap", [P, 2 * g * P])
        place = [L.sb(f"place{s}", [P, 2 * g]) for s in range(2)]
        place_i = [L.sb(f"place_i{s}", [P, g], I32) for s in range(RING)]
        rec_out = [L.sb(f"rec_out{s}", [P, g * W]) for s in range(RING)]
        oh2, blkT_made, blkT_copied, rows_made, compared, snapped, counted, looked, added, placed, rec_ready, gate = (
            L.sem(n) for n in ("oh2", "blkT_made", "blkT_copied", "rows_made", "compared", "snapped", "counted",
                               "looked", "added", "placed", "rec_ready", "gate"))
        sent = L.sems("sent", RING)
        V = T // g
        with nc.Block() as block:
            @block.vector
            def _(dve):
                def step(u, s, i):
                    if there(u + 1, V):
                        dve.wait_ge(rows_made, u + 2)
                        after(dve, placed, u)
                        for q in range(g):
                            last = nc.vector.scalar_tensor_tensor(
                                scrap[:, q * P:(q + 1) * P], row_ps[(s + 1) % 2][:, q * P:(q + 1) * P],
                                key[:, ds((u + 1) * g + q, 1)], C.before[:, :], ALU.is_equal, ALU.mult,
                                accum_out=place[(s + 1) % 2][:, q:q + 1])
                        last.then_inc(compared, 1)
                    if there(u + 2, V):
                        one_hots((s + 2) % RING, (u + 2) * g).then_inc(oh2, 1)
                    if there(u, V):
                        dve.wait_ge(looked, u * g + 3 * g)
                        for q in range(g):
                            last = nc.vector.scalar_tensor_tensor(
                                scrap[:, (g + q) * P:(g + q + 1) * P], at_ps[s % 2][:, q * P:(q + 1) * P], 1.0,
                                oh_low[s][:, q * P:(q + 1) * P], ALU.mult, ALU.mult,
                                accum_out=place[s % 2][:, g + q:g + q + 1])
                        last.then_inc(added, 1)
                        dve.wait_ge(added, u + 3)
                        after(dve, sent[s], i * (16 * g))
                        nc.vector.tensor_tensor(place_i[s][:, :], place[s % 2][:, 0:g], place[s % 2][:, g:2 * g],
                                                ALU.add).then_inc(placed, 1)
                dve.sem_inc(added, 2)
                dve.sem_inc(compared, 2)
                run_steps(dve, step, V, 2)

            @block.scalar
            def _(act):
                def snapshot(u, s, q):
                    act.wait_ge(counted, u * g + (q + g))
                    if q == 0:
                        act.wait_ge(looked, u * g + g)
                    nc.scalar.activation(snap[s % 2][0:H, q * P:(q + 1) * P], hist_ps[0:H, 0:P],
                                         ACT.Copy).then_inc(snapped, 1)

                def step(u, s, i):
                    if there(u, V):
                        snapshot(u, s, 0)
                        after(act, sent[s], i * (16 * g))
                        nc.scalar.activation(rec_out[s][:, :], rec[:, ds(u * (g * W), g * W)],
                                             ACT.Copy).then_inc(rec_ready, 1)
                        snapshot(u, s, 1)
                    if there(u + 1, V):
                        act.wait_ge(blkT_made, u + 2)
                        act.wait_ge(looked, u * g + 2 * g)
                        nc.scalar.activation(blkT[(s + 1) % 2][0:H, :], blkT_ps[(s + 1) % 2][0:H, 0:g * P],
                                             ACT.Copy).then_inc(blkT_copied, 1)
                    if there(u, V):
                        snapshot(u, s, 2)
                run_steps(act, step, V, 1)

            @block.tensor
            def _(pe):
                def count(u, s, q):
                    pe.wait_ge(snapped, u * g + (q + 1))
                    nc.tensor.matmul(hist_ps[0:H, 0:P], oh_blk[s][:, q * H:(q + 1) * H],
                                     oh_low[s][:, q * P:(q + 1) * P], start=False, stop=False,
                                     skip_group_check=True).then_inc(counted, 1)
                    nc.tensor.matmul(at_ps[s % 2][:, q * P:(q + 1) * P], blkT[s % 2][0:H, q * P:(q + 1) * P],
                                     snap[s % 2][0:H, q * P:(q + 1) * P], start=True, stop=True).then_inc(looked, 1)

                def step(u, s, i):
                    s1 = (s + 1) % RING
                    if there(u, V):
                        pe.wait_ge(blkT_copied, u + 1)
                        pe.wait_ge(added, u + 1)
                        count(u, s, 0)
                    if there(u + 1, V):
                        pe.wait_ge(oh2, u + 2)
                        for q in range(g):
                            mm = nc.tensor.transpose(blkT_ps[s1 % 2][0:H, q * P:(q + 1) * P],
                                                     oh_blk[s1][:, q * H:(q + 1) * H], C.ident_b[:, :])
                        mm.then_inc(blkT_made, 1)
                    if there(u, V):
                        count(u, s, 1)
                    if there(u + 1, V):
                        pe.wait_ge(compared, u + 2)
                        for q in range(g):
                            out = row_ps[s1 % 2][:, q * P:(q + 1) * P]
                            nc.tensor.matmul(out, blk128[:, ds((u + 1) * g + q, 1)].to_broadcast([P, P]),
                                             C.ident_b[:, :], start=True, stop=False)
                            mm = nc.tensor.matmul(out, low[:, ds((u + 1) * g + q, 1)].to_broadcast([P, P]),
                                                  C.ident_b[:, :], start=False, stop=True)
                        mm.then_inc(rows_made, 1)
                    if there(u, V):
                        count(u, s, 2)

                nc.tensor.matmul(hist_ps[0:H, 0:P], C.ident[0:H, 0:H], first[0:H, :],
                                 start=True, stop=False, skip_group_check=True).then_inc(counted, g)
                pe.sem_inc(looked, 2 * g)
                run_steps(pe, step, V, 1)
                nc.tensor.matmul(hist_ps[0:H, 0:P], zero_b[:, 0:H], zero_b[:, :], start=False, stop=True,
                                 skip_group_check=True)

            @block.gpsimd
            def _(pool):
                with pool.Fori(0, V // RING) as i:
                    for s in range(RING):
                        u = i * RING + s
                        pool.wait_ge(rec_ready, u + 1)
                        pool.wait_ge(placed, u + 1)
                        nc.gpsimd.sem_inc(gate, 1)
                        for q in range(g):
                            nc.gpsimd.indirect_dma_start(
                                sorted_dram, bass.IndirectOffsetOnAxis(ap=place_i[s][:, q:q + 1], axis=0),
                                rec_out[s][:, q * W:(q + 1) * W], None).then_inc(sent[s], 16)
                for s in range(RING):
                    pool.wait_ge(sent[s], V // RING * 16 * g)


def loads(eng, sem, pairs):
    for dst, src in pairs:
        eng.dma_start(dst, src).then_inc(sem, 16)
    return 16 * len(pairs)


class Edges:

    def __init__(self, S, tag, plan):
        KT, R = plan.out, plan.rows
        self.plan = plan
        self.src = S.sb(f"{tag}src", [P, KT], I32)
        self.low = S.sb(f"{tag}low", [P, KT])
        self.low_b = S.sb(f"{tag}low_b", [P, KT], BF16)
        self.src_low = S.sb(f"{tag}src_low", [P, KT], BF16)
        self.src_blk = S.sb(f"{tag}src_blk", [P, KT], BF16)
        self.cut = S.sb(f"{tag}cut", [P, 4 * 512])
        self.cut_back = S.sb(f"{tag}cut_back", [P, 4 * 512])
        self.out_first = S.sb(f"{tag}out_first", [P, 512])
        self.out_last = S.sb(f"{tag}out_last", [P, 512])
        self.joins = S.sb(f"{tag}joins", [4, R + 1])
        self.carry_on = S.sb(f"{tag}carry_on", [4, R])
        self.carry_back = S.sb(f"{tag}carry_back", [4, R])
        self.rec3 = None


def prepare_edges(nc, C, E, tag, rec_dram, rec):
    KT, W, R = E.plan.out, E.plan.width, E.plan.rows
    E.rec3 = rec[:, :].rearrange("p (k w) -> p k w", w=W)
    with Scope(nc, f"prep{tag}") as L:
        a_i = L.sb("a_i", [P, KT], I32)
        b_i = L.sb("b_i", [P, KT], I32)
        b_f = L.sb("b_f", [P, KT])
        dst_s = L.sb("dst_s", [P, 512])
        dst_ps = L.ps("dst_ps", [P, 512])
        ends_ps = L.ps("ends_ps", [4, 512])
        ends = L.sb("ends", [4, 2 * R])
        whole = L.sb("whole", [4, R])
        got, chain, turned, copied, ended = (L.sem(n) for n in ("got", "chain", "turned", "copied", "ended"))
        with nc.Block() as block:
            @block.sync
            def _(sp):
                by_tile = rec_dram.rearrange("(k r) w -> r k w", r=P)
                for k in range(0, KT, 8 * G):
                    n = min(8 * G, KT - k)
                    sp.dma_start(E.rec3[:, k:k + n, :], by_tile[:, k:k + n, :]).then_inc(got, 16)

            @block.tensor
            def _(pe):
                pe.wait_ge(got, 16 * -(-KT // (8 * G)))
                for q in range(G):
                    mm = nc.tensor.transpose(dst_ps[0:R, q * P:(q + 1) * P], E.rec3[:, q::G, 1], C.ident[:, :])
                mm.then_inc(turned, 1)
                pe.wait_ge(copied, 1)
                nc.tensor.transpose(ends_ps[0:4, 0:R], dst_s[0:R, 0:1].to_broadcast([R, 4]), C.ident[0:R, 0:R])
                nc.tensor.transpose(ends_ps[0:4, R:2 * R], dst_s[0:R, 511:512].to_broadcast([R, 4]),
                                    C.ident[0:R, 0:R]).then_inc(ended, 1)

            @block.vector
            def _(dve):
                link = serial(dve, chain)
                dve.wait_ge(got, 16 * -(-KT // (8 * G)))
                nc.vector.tensor_copy(E.src[:, :], E.rec3[:, :, 0])
                link(nc.vector.tensor_copy(a_i[:, :], E.rec3[:, :, 0]))
                link(nc.vector.tensor_scalar(b_i[:, :], a_i[:, :], 7, None, ALU.arith_shift_right))
                link(nc.vector.tensor_copy(E.src_blk[:, :], b_i[:, :]))
                link(nc.vector.tensor_scalar(b_i[:, :], a_i[:, :], P - 1, None, ALU.bitwise_and))
                link(nc.vector.tensor_copy(E.src_low[:, :], b_i[:, :]))
                link(nc.vector.tensor_copy(a_i[:, :], E.rec3[:, :, 1]))
                link(nc.vector.tensor_scalar(b_i[:, :], a_i[:, :], P - 1, None, ALU.bitwise_and))
                link(nc.vector.tensor_copy(E.low[:, :], b_i[:, :]))
                link(nc.vector.tensor_scalar(b_f[:, :], E.rec3[:, :, 1], 0.0, 1024.0, ALU.min, ALU.mult))
                link(nc.vector.tensor_tensor(E.low[:, :], E.low[:, :], b_f[:, :], ALU.add))
                link(nc.vector.tensor_copy(E.low_b[:, :], E.low[:, :]))
                dve.wait_ge(turned, 1)
                nc.vector.tensor_copy(dst_s[0:R, :], dst_ps[0:R, :]).then_inc(copied, 1)
                dve.wait_ge(copied, 1)
                cut = E.cut[0:R, :].rearrange("p (h j) -> p h j", h=4)
                back = E.cut_back[0:R, :].rearrange("p (h j) -> p h j", h=4)
                nc.vector.memset(cut[:, :, 0:1], FAR)
                nc.vector.memset(back[:, :, 511:512], FAR)
                for h in range(4):
                    nc.vector.tensor_tensor(cut[:, h, 1:512], dst_s[0:R, 1:512], dst_s[0:R, 0:511], ALU.not_equal)
                    nc.vector.tensor_tensor(back[:, h, 0:511], dst_s[0:R, 1:512], dst_s[0:R, 0:511], ALU.not_equal)
                nc.vector.tensor_scalar(E.out_first[0:R, :], dst_s[0:R, :], dst_s[0:R, 0:1], FAR,
                                        ALU.not_equal, ALU.mult)
                link(nc.vector.tensor_scalar(E.out_last[0:R, :], dst_s[0:R, :], dst_s[0:R, 511:512], FAR,
                                             ALU.not_equal, ALU.mult))
                nc.vector.tensor_scalar(cut[:, :, 1:512], cut[:, :, 1:512], FAR, None, ALU.mult)
                link(nc.vector.tensor_scalar(back[:, :, 0:511], back[:, :, 0:511], FAR, None, ALU.mult))
                dve.wait_ge(ended, 1)
                link(nc.vector.tensor_copy(ends[:, :], ends_ps[0:4, 0:2 * R]))
                link(nc.vector.memset(E.joins[:, :], FAR))
                link(nc.vector.tensor_tensor(E.joins[:, 1:R], ends[:, 1:R], ends[:, R:2 * R - 1], ALU.not_equal))
                link(nc.vector.tensor_scalar(E.joins[:, 1:R], E.joins[:, 1:R], FAR, None, ALU.mult))
                link(nc.vector.tensor_tensor(whole[:, :], ends[:, 0:R], ends[:, R:2 * R], ALU.not_equal))
                link(nc.vector.tensor_scalar(whole[:, :], whole[:, :], FAR, None, ALU.mult))
                link(nc.vector.tensor_tensor(E.carry_on[:, :], whole[:, :], E.joins[:, 0:R], ALU.add))
                link(nc.vector.tensor_tensor(E.carry_back[:, :], whole[:, :], E.joins[:, 1:R + 1], ALU.add))


def layer_norm(nc, tag, src, dst, width=D, eps=1e-5, scale=None, shift=None):
    with Scope(nc, f"ln{tag}") as L:
        stats = L.sb("stats", [P, NB * 6])
        mean = L.sb("mean", [P, NB])
        gap = L.sb("gap", [P, NB])
        dev = L.sb("dev", [P, NB])
        counted, var_ready, root, chain, normed = (
            L.sem(n) for n in ("counted", "var_ready", "root", "chain", "normed"))
        s6 = stats[:, :].rearrange("p (b t) -> p b t", t=6)
        with nc.Block() as block:
            @block.vector
            def _(dve):
                link = serial(dve, chain)
                over_nodes(dve, lambda b, s, i: nc.vector.bn_stats(
                    stats[:, ds(b * 6, 6)], src[:, ds(b * width, width)]).then_inc(counted, 1))
                dve.wait_ge(counted, NB)
                nc.vector.tensor_tensor(mean[:, :], s6[:, :, 1], s6[:, :, 4], ALU.add)
                nc.vector.tensor_tensor(dev[:, :], s6[:, :, 2], s6[:, :, 5], ALU.add)
                link(nc.vector.tensor_tensor(gap[:, :], s6[:, :, 1], s6[:, :, 4], ALU.subtract))
                link(nc.vector.tensor_tensor(gap[:, :], gap[:, :], gap[:, :], ALU.mult))
                link(nc.vector.tensor_scalar(dev[:, :], dev[:, :], 1.0 / width, eps, ALU.mult, ALU.add))
                nc.vector.tensor_scalar(mean[:, :], mean[:, :], 0.5, None, ALU.mult)
                nc.vector.scalar_tensor_tensor(dev[:, :], gap[:, :], 0.25, dev[:, :], ALU.mult,
                                               ALU.add).then_inc(var_ready, 1)
                dve.wait_ge(root, 1)
                link(nc.vector.reciprocal(dev[:, :], dev[:, :]))
                over_nodes(dve, lambda b, s, i: nc.vector.tensor_scalar(
                    dst[:, ds(b * width, width)], src[:, ds(b * width, width)], mean[:, ds(b, 1)], dev[:, ds(b, 1)],
                    ALU.subtract, ALU.mult).then_inc(normed, 1))
                if scale is not None:
                    dve.wait_ge(normed, NB)
                    d3 = dst[:, :].rearrange("p (b d) -> p b d", d=width)
                    link(nc.vector.tensor_tensor(d3, d3, scale.unsqueeze(1).to_broadcast([P, NB, width]), ALU.mult))
                    link(nc.vector.tensor_tensor(d3, d3, shift.unsqueeze(1).to_broadcast([P, NB, width]), ALU.add))

            @block.scalar
            def _(act):
                act.wait_ge(var_ready, 1)
                nc.scalar.activation(dev[:, :], dev[:, :], ACT.Sqrt).then_inc(root, 1)


MUL = 64
MSG = 8 * MUL


def equivariant_layer(nc, C, S, a, E, block_of, x, table):
    KT = E.plan.out
    with Scope(nc, "eq") as L:
        z = L.sb("z", [P, NB])
        z8 = L.sb("z8", [P, NB])
        with Scope(nc, "eqn") as M:
            xn = M.sb("xn", [P, NB * D])
            layer_norm(nc, "eq", x, xn)
            w = M.sb("w", [MUL, 4 * MUL])
            row = [M.sb(f"row{s}", [P, D]) for s in range(RING)]
            ld, zed, rowed, chain = (M.sem(n) for n in ("ld", "zed", "rowed", "chain"))
            stored = M.sems("stored", RING)
            with nc.Block() as block:
                @block.sync
                def _(sp):
                    loads(sp, ld, [(w[:, 0:64], a["L0_gnn_W_sc0"]), (w[:, 64:128], a["L0_gnn_W_lin1_0"]),
                                   (w[:, 128:192], a["L0_gnn_W_sc1"]), (w[:, 192:256], a["L0_gnn_W_lin1_1"]),
                                   (z[:, :], a["node_vec1"])])

                    def store(b, s, i):
                        sp.wait_ge(rowed, b + 1)
                        sp.dma_start(table[ds(b * P, P), 0:D], row[s][:, :]).then_inc(stored[s], 16)
                    over_nodes(sp, store)
                    for s in range(RING):
                        sp.wait_ge(stored[s], 16 * -(-(NB - s) // RING))

                def take(b, out):
                    xb = xn[:, ds(b * D, D)]
                    nc.scalar.activation(out[:, 0:MUL], xb[:, 0:MUL], ACT.Copy)
                    return nc.scalar.activation(out[:, MUL:D].rearrange("p (c u) -> p u c", c=3),
                                                xb[:, MUL:D].rearrange("p (u c) -> p u c", c=3), ACT.Copy)

                def multiply(turned, out):
                    for j in range(4):
                        k = 0 if j == 0 else 2 * MUL
                        mm = nc.tensor.matmul(out[:, j * P:(j + 1) * P], turned[:, j * P:(j + 1) * P],
                                              w[:, k:k + 2 * MUL], start=True, stop=True)
                    return mm

                def consume(b, s, i, turned, out):
                    o3 = out[:, :].rearrange("p (j k v) -> p j k v", j=4, k=2)
                    after(nc.vector, stored[s], i * 16)
                    nc.vector.tensor_scalar(row[s][:, :].rearrange("p (j v) -> p j v", j=4),
                                            o3[:, :, 1, :], z8[:, ds(b, 1)], None, ALU.mult).then_inc(rowed, 1)
                    xb = x[:, ds(b * D, D)]
                    nc.vector.scalar_tensor_tensor(xb[:, 0:MUL], o3[:, 0, 0, :], z8[:, ds(b, 1)], xb[:, 0:MUL],
                                                   ALU.mult, ALU.add)
                    x3 = xb[:, MUL:].rearrange("p (u c) -> p c u", c=3)
                    return nc.vector.scalar_tensor_tensor(x3, o3[:, 1:4, 0, :], z8[:, ds(b, 1)], x3, ALU.mult, ALU.add)

                consumer = turn_nodes(nc, M, C, block, take, D, 4, consume, multiply, [(ld, 80), (zed, 1)])

                @block.vector
                def _(dve):
                    link = serial(dve, chain)
                    dve.wait_ge(ld, 80)
                    w3 = w[:, :].rearrange("p (g k v) -> p g k v", g=2, k=2)
                    link(nc.vector.tensor_scalar(w3[:, :, 0, :], w3[:, :, 0, :], float(np.float32(np.sin(np.pi / 8))),
                                                 None, ALU.mult))
                    nc.vector.tensor_scalar(z8[:, :], z[:, :], MUL ** -0.5, None, ALU.mult).then_inc(zed, 1)
                    dve.wait_ge(zed, 1)
                    consumer(dve)

        acc = L.sb("acc", [P, NB * 512])
        with Scope(nc, "eqe") as M:
            fc0 = M.sb("fc0", [G * 8, G * MUL])
            fc1 = M.sb("fc1", [2 * MUL, 4 * MUL])
            idx = [M.sb(f"idx{s}", [P, G], I32) for s in range(RING)]
            got = [M.sb(f"got{s}", [P, G * D]) for s in range(RING)]
            attr = [M.sb(f"attr{s}", [P, G * 8]) for s in range(2)]
            attrT = M.sb("attrT", [G * 8, P])
            hid = [M.sb(f"hid{s}", [2 * MUL, G * MUL]) for s in range(2)]
            pick = [M.sb(f"pick{s}", [P, G * P]) for s in range(2)]
            sized = [M.sb(f"sized{s}", [P, G * MSG]) for s in range(2)]
            of_d = [M.sb(f"of_d{s}", [P, G * 3 * MUL]) for s in range(2)]
            msg = [M.sb(f"msg{s}", [P, G * MSG]) for s in range(2)]
            small_ps = M.ps("small_ps", [P, 512])
            hid_ps = M.ps("hid_ps", [P, 512])
            w_ps = [M.ps(f"w_ps{s}", [P, 1024]) for s in range(2)]
            sum_ps = [M.ps(f"sum_ps{s}", [P, 512]) for s in range(2)]
            ld, ready, chain, idxed, attred, turned, copied, hidden, silued, weighted = (
                M.sem(n) for n in ("ld", "ready", "chain", "idxed", "attred", "turned", "copied", "hidden", "silued",
                                   "weighted"))
            sized_act, multed, sized_pool, d_summed, messaged, summed, added, gate, cleared = (
                M.sem(n) for n in ("sized_act", "multed", "sized_pool", "d_summed", "messaged", "summed", "added",
                                   "gate", "cleared"))
            d_part = [t[:, :].rearrange("p (t f) -> p t f", t=G)[:, :, 7 * MUL:] for t in sized]
            d_of = [t[:, :].rearrange("p (t c u) -> p t c u", t=G, c=3) for t in of_d]
            arrived = M.sems("arrived", RING)
            V = KT // G
            n_it = V // RING

            AHEAD = 4

            with nc.Block() as block:
                @block.sync
                def _(sp):
                    sp.wait_ge(cleared, 2)
                    loads(sp, ld, [(fc0[8 * t:8 * t + 8, MUL * k:MUL * k + MUL], a["L0_gnn_fc_w0"])
                                   for t, k in enumerate((0, 2, 1, 3))]
                          + [(fc1[k * MUL:(k + 1) * MUL, to * MUL:(to + 1) * MUL],
                              a["L0_gnn_fc_w1"][:, w * MUL:(w + 1) * MUL])
                             for k in range(2) for to, w in enumerate((0, 2, 1, 3))])

                @block.gpsimd
                def _(pool):
                    nc.gpsimd.memset(fc0[:, :], 0.0).then_inc(cleared, 1)

                    def size(v, s):
                        nc.gpsimd.tensor_tensor(
                            d_of[s % 2],
                            got[s][:, :].rearrange("p (t f) -> p t f", t=G)[:, :, MUL:].rearrange(
                                "p t (c u) -> p t c u", c=3),
                            E.rec3[:, ds(v * G, G), 3:6].unsqueeze(3).to_broadcast([P, G, 3, MUL]),
                            ALU.mult).then_inc(multed, 1)
                        pool.wait_ge(multed, v + 1)
                        nc.gpsimd.tensor_tensor(d_part[s % 2], d_of[s % 2][:, :, 0, :], d_of[s % 2][:, :, 1, :],
                                                ALU.add).then_inc(sized_pool, 1)

                    def step(u, s, i):
                        if there(u + 2, V):
                            s2 = (s + 2) % RING
                            pool.wait_ge(arrived[s2], (i + (1 + (s + 2) // RING)) * (16 * G))
                            after(pool, messaged, (u + 1) * G)
                            size(u + 2, s2)
                        if there(u + 4, V):
                            pool.wait_ge(idxed, u + 5)
                            nc.gpsimd.sem_inc(gate, 1)
                            for t in range(G):
                                nc.gpsimd.indirect_dma_start(
                                    got[s][:, t * D:(t + 1) * D], None, table[:, 0:D],
                                    bass.IndirectOffsetOnAxis(ap=idx[s][:, t:t + 1], axis=0)).then_inc(arrived[s], 16)

                    run_steps(pool, step, V, AHEAD)

                @block.vector
                def _(dve):
                    blks = Blocks(dve, "eqe_blk", block_of)
                    link = serial(dve, chain)
                    nc.vector.memset(acc[:, :], 0.0).then_inc(cleared, 1)
                    dve.wait_ge(cleared, 2)
                    dve.wait_ge(ld, 16 * (G + 8))
                    link(nc.vector.tensor_scalar(fc1[:, :], fc1[:, :], MUL ** -0.5, None, ALU.mult))
                    nc.vector.tensor_scalar(fc1[:, 3 * MUL:], fc1[:, 3 * MUL:], 3 ** -0.5, None,
                                            ALU.mult).then_inc(ready, 1)
                    dve.wait_ge(ready, 1)

                    def message_ad(s):
                        return nc.vector.tensor_tensor(
                            msg[s % 2][:, :].rearrange("p (t g u) -> p t g u", t=G, u=MUL)[:, :, 0::7],
                            w_ps[s % 2][:, :].rearrange("p (t g u) -> p t g u", t=G, u=MUL)[:, :, 0::3],
                            sized[s % 2][:, :].rearrange("p (t g u) -> p t g u", t=G, u=MUL)[:, :, 0::7], ALU.mult)

                    def message(s, t):
                        part = slice(t * MSG + MUL, (t + 1) * MSG - MUL)
                        return nc.vector.tensor_tensor(
                            msg[s % 2][:, part].rearrange("p (g c u) -> p g c u", g=2, c=3),
                            w_ps[s % 2][:, t * D + MUL:t * D + 3 * MUL].rearrange("p (g u) -> p g u", g=2).unsqueeze(2)
                            .to_broadcast([P, 2, 3, MUL]),
                            sized[s % 2][:, part].rearrange("p (g c u) -> p g c u", g=2, c=3), ALU.mult)

                    def step(u, s, i):
                        if there(u + 1, V):
                            after(dve, summed, (u + 1) * G)
                            nc.vector.tensor_tensor(
                                pick[(s + 1) % 2][:, :].rearrange("p (t d) -> p t d", t=G),
                                C.ramp[:, :].unsqueeze(1).to_broadcast([P, G, P]),
                                E.low[:, ds((u + 1) * G, G)].unsqueeze(2).to_broadcast([P, G, P]), ALU.is_equal)
                            dve.wait_ge(sized_pool, u + 2)
                            nc.vector.tensor_tensor(d_part[(s + 1) % 2], d_part[(s + 1) % 2], d_of[(s + 1) % 2][:, :, 2, :],
                                                    ALU.add).then_inc(d_summed, 1)
                            dve.wait_ge(weighted, u + 2)
                            dve.wait_ge(sized_act, u + 2)
                        for t in range(G):
                            if there(u + 1, V):
                                last = message(s + 1, t)
                                if t == 0:
                                    dve.wait_ge(d_summed, u + 2)
                                    last = message_ad(s + 1)
                                last.then_inc(messaged, 1)
                            if there(u, V):
                                dve.wait_ge(summed, u * G + (t + 1 + G))
                                dve.wait_ge(added, u * G + (t + 2))
                                dst = acc[:, ds(blks.of[s * G + t] * 512, 512)]
                                nc.vector.tensor_tensor(dst, dst, sum_ps[t % 2][:, :], ALU.add).then_inc(added, 1)

                    dve.sem_inc(added, 2)
                    run_steps(dve, step, V, AHEAD, blks.load)

                @block.scalar
                def _(act):
                    def step(u, s, i):
                        if there(u + 4, V):
                            after(act, turned, u + 3)
                            nc.scalar.activation(attr[s % 2][:, :].rearrange("p (t f) -> p t f", t=G),
                                                 E.rec3[:, ds((u + 4) * G, G), 6:14], ACT.Copy).then_inc(attred, 1)
                            after(act, sized_pool, u + 1)
                            after(act, sized_act, u + 1)
                            nc.scalar.activation(idx[s][:, :], E.src[:, ds((u + 4) * G, G)], ACT.Copy).then_inc(idxed, 1)
                        if there(u + 2, V):
                            s2 = (s + 2) % RING
                            act.wait_ge(arrived[s2], (i + (1 + (s + 2) // RING)) * (16 * G))
                            after(act, messaged, (u + 1) * G)
                            for t in range(G):
                                row = got[s2][:, t * D:(t + 1) * D]
                                to = sized[s % 2][:, t * MSG:(t + 1) * MSG]
                                of = [E.rec3[:, ds((u + 2) * G + t, 1), 2 + c] for c in range(4)]
                                last = nc.scalar.activation(to[:, 0:D], row, ACT.Copy, scale=of[0])
                                for c in range(3):
                                    last = nc.scalar.activation(to[:, (4 + c) * MUL:(5 + c) * MUL], row[:, 0:MUL], ACT.Copy,
                                                                scale=of[1 + c])
                            last.then_inc(sized_act, 1)
                        if there(u + 3, V):
                            act.wait_ge(hidden, u + 4)
                            after(act, weighted, u + 2)
                            nc.scalar.activation(hid[(s + 1) % 2][:, :], hid_ps[:, 0:G * MUL], ACT.Silu,
                                                 scale=8 ** -0.5).then_inc(silued, 1)
                        if there(u + 4, V):
                            act.wait_ge(turned, u + 5)
                            after(act, hidden, u + 4)
                            nc.scalar.activation(attrT[:, :], small_ps[0:G * 8, 0:P], ACT.Copy).then_inc(copied, 1)

                    run_steps(act, step, V, AHEAD)

                @block.tensor
                def _(pe):
                    def ahead(u, s):
                        if there(u + 3, V):
                            pe.wait_ge(copied, u + 4)
                            after(pe, silued, u + 3)
                            for k in range(2):
                                mm = nc.tensor.matmul(hid_ps[:, k * P:(k + 1) * P], fc0[:, k * P:(k + 1) * P],
                                                      attrT[:, :], start=True, stop=True)
                            mm.then_inc(hidden, 1)
                        if there(u + 4, V):
                            pe.wait_ge(attred, u + 5)
                            after(pe, copied, u + 4)
                            nc.tensor.transpose(small_ps[0:G * 8, 0:P], attr[s % 2][:, :],
                                                C.ident[:, :]).then_inc(turned, 1)

                    def step(u, s, i):
                        for t in range(G):
                            if there(u, V):
                                pe.wait_ge(messaged, u * G + (t + 1))
                                pe.wait_ge(added, u * G + (t + 1))
                                lhs = pick[s % 2][:, t * P:(t + 1) * P]
                                m = msg[s % 2][:, t * MSG:(t + 1) * MSG]
                                o = sum_ps[t % 2]
                                nc.tensor.matmul(o[:, :], lhs, m, start=True, stop=True).then_inc(summed, 1)
                            if there(u + 2, V):
                                if t == 0:
                                    pe.wait_ge(silued, u + 3)
                                if t % 2 == 0:
                                    after(pe, messaged, u * G + (t + 2))
                                half = slice(t // 2 * MUL, (t // 2 + 1) * MUL)
                                mm = nc.tensor.matmul(w_ps[s % 2][:, t * D:(t + 1) * D],
                                                      hid[s % 2][half, t % 2 * P:(t % 2 + 1) * P], fc1[half, :],
                                                      start=True, stop=True)
                                if t == G - 1:
                                    mm.then_inc(weighted, 1)
                            if t == 1:
                                ahead(u, s)

                    pe.sem_inc(summed, G)
                    pe.wait_ge(ready, 1)
                    pe.wait_ge(ld, 16 * (G + 8))
                    run_steps(pe, step, V, AHEAD)

        with Scope(nc, "eqo") as M:
            w2 = M.sb("w2", [P, 2 * MUL])
            ld, ready = (M.sem(n) for n in ("ld", "ready"))
            with nc.Block() as block:
                @block.sync
                def _(sp):
                    w0, w1 = a["L0_gnn_W_lin2_0"], a["L0_gnn_W_lin2_1"]
                    loads(sp, ld, [(w2[:, 0:64], w0),
                                   (w2[0:64, 64:128], w1[64:128, :]), (w2[64:128, 64:128], w1[0:64, :])])

                def take(b, out):
                    sums = acc[:, ds(b * 512, 512)]
                    nc.scalar.activation(out[:, 0:2 * MUL].rearrange("p (g u) -> p g u", g=2),
                                         sums.rearrange("p (g u) -> p g u", u=MUL)[:, 0::7], ACT.Copy)
                    for g in range(2):
                        last = nc.scalar.activation(
                            out[:, 2 * MUL:].rearrange("p (c g u) -> p c g u", g=2, c=3)[:, :, g, :],
                            sums[:, (1 + 3 * g) * MUL:(4 + 3 * g) * MUL].rearrange("p (c u) -> p c u", c=3), ACT.Copy)
                    return last

                def multiply(turned, out):
                    for j in range(4):
                        mm = nc.tensor.matmul(out[:, j * MUL:(j + 1) * MUL], turned[:, j * P:(j + 1) * P],
                                              w2[:, 0:MUL] if j == 0 else w2[:, MUL:], start=True, stop=True)
                    return mm

                def consume(b, s, i, turned, out):
                    xb = x[:, ds(b * D, D)]
                    nc.vector.scalar_tensor_tensor(xb[:, 0:MUL], out[:, 0:MUL], z[:, ds(b, 1)], xb[:, 0:MUL],
                                                   ALU.mult, ALU.add)
                    x3 = xb[:, MUL:].rearrange("p (u c) -> p c u", c=3)
                    return nc.vector.scalar_tensor_tensor(x3, out[:, MUL:D].rearrange("p (c u) -> p c u", c=3),
                                                          z[:, ds(b, 1)], x3, ALU.mult, ALU.add)

                consumer = turn_nodes(nc, M, C, block, take, 512, 4, consume, multiply, [(ld, 48), (ready, 1)])

                @block.vector
                def _(dve):
                    dve.wait_ge(ld, 48)
                    k = float(np.float32(np.cos(np.pi / 8))) / np.sqrt(16.0) / np.sqrt(2.0 * MUL)
                    nc.vector.tensor_scalar(w2[:, :], w2[:, :], float(k), None, ALU.mult).then_inc(ready, 1)
                    consumer(dve)


def broadcast_rows(ap):
    return ap.partition_broadcast(P)


def gating(nc, tag, logits, gates, n):
    with Scope(nc, f"gate{tag}") as L:
        above = L.sb("above", [P, NB * n * n])
        ties = L.sb("ties", [P, NB * n * n])
        early = L.sb("early", [P, n * n])
        rank = L.sb("rank", [P, NB * n])
        top = L.sb("top", [P, NB])
        ramp = L.sb("ramp", [P, n])
        chain, expd, ready, ramped = L.sem("chain"), L.sem("expd"), L.sem("ready"), L.sem("ramped")
        l3 = logits[:, :].rearrange("p (b e) -> p b e", e=n)
        g3 = gates[:, :].rearrange("p (b e) -> p b e", e=n)
        r3 = rank[:, :].rearrange("p (b e) -> p b e", e=n)
        with nc.Block() as block:
            @block.gpsimd
            def _(pool):
                nc.gpsimd.iota(ramp[:, :], [[1, n]], base=0, channel_multiplier=0,
                               allow_small_or_imprecise_dtypes=True).then_inc(ramped, 1)

            @block.vector
            def _(dve):
                link = serial(dve, chain)
                dve.wait_ge(ramped, 1)
                e3 = early[:, :].rearrange("p (e f) -> p e f", e=n)
                link(nc.vector.tensor_tensor(e3, ramp[:, :].unsqueeze(1).to_broadcast([P, n, n]),
                                             ramp[:, :].unsqueeze(2).to_broadcast([P, n, n]), ALU.is_lt))
                link(nc.vector.tensor_reduce(top[:, :], l3, AX.X, ALU.max))
                nc.vector.tensor_tensor(g3, l3, top[:, :].unsqueeze(2).to_broadcast([P, NB, n]),
                                        ALU.subtract).then_inc(ready, 1)
                for e in range(n):
                    for out, op in ((above, ALU.is_gt), (ties, ALU.is_equal)):
                        last = nc.vector.tensor_tensor(
                            out[:, :].rearrange("p (b e f) -> p b e f", e=n, f=n)[:, :, e, :], l3,
                            l3[:, :, e:e + 1].to_broadcast([P, NB, n]), op)
                link(last)
                t3 = ties[:, :].rearrange("p (b k) -> p b k", b=NB)
                link(nc.vector.tensor_tensor(t3, t3, early[:, :].unsqueeze(1).to_broadcast([P, NB, n * n]), ALU.mult))
                link(nc.vector.tensor_tensor(above[:, :], above[:, :], ties[:, :], ALU.add))
                link(nc.vector.tensor_reduce(rank[:, :], above[:, :].rearrange("p (k f) -> p k f", f=n), AX.X, ALU.add))
                dve.wait_ge(expd, 1)
                link(nc.vector.scalar_tensor_tensor(gates[:, :], rank[:, :], 1.5, gates[:, :], ALU.is_lt, ALU.mult))
                link(nc.vector.tensor_reduce(top[:, :], g3, AX.X, ALU.add))
                link(nc.vector.reciprocal(top[:, :], top[:, :]))
                link(nc.vector.tensor_tensor(g3, g3, top[:, :].unsqueeze(2).to_broadcast([P, NB, n]), ALU.mult))

            @block.scalar
            def _(act):
                act.wait_ge(ready, 1)
                nc.scalar.activation(gates[:, :], gates[:, :], ACT.Exp).then_inc(expd, 1)


HID = 512


def experts(nc, C, tag, xn, x, n, a, w1, b1, w2, b2, wr=None, br=None, gates=None):
    KD, KH = D // P, HID // P
    with Scope(nc, f"moe{tag}") as L:
        xnT = L.sb("xnT", [P, KD * NPAD])
        xnT3 = xnT[:, :].rearrange("p (k n) -> p k n", k=KD)
        if gates is None:
            gates = L.sb("gates", [P, NB * n])
            logits = L.sb("logits", [P, NB * n])
        with Scope(nc, f"moet{tag}") as M:
            wr_s = M.sb("wr", [P, KD * n])
            br_s = M.sb("br", [P, n])
            ld = M.sem("ld")
            with nc.Block() as block:
                @block.sync
                def _(sp):
                    if wr is not None:
                        loads(sp, ld, [(wr_s[:, k * n:(k + 1) * n], a[wr][k * P:(k + 1) * P, :]) for k in range(KD)]
                              + [(br_s[:, :], broadcast_rows(a[br]))])

                def take(b, out):
                    return nc.scalar.activation(out[:, :], xn[:, ds(b * D, D)], ACT.Copy)

                def route(turned, out):
                    for k in range(KD):
                        mm = nc.tensor.matmul(out[:, 0:n], turned[:, k * P:(k + 1) * P],
                                              wr_s[:, k * n:(k + 1) * n], start=k == 0, stop=k == KD - 1)
                    return mm

                def keep(b, s, i, turned, out):
                    last = nc.vector.tensor_copy(xnT3[:, :, ds(b * P, P)], turned[:, :].rearrange("p (k n) -> p k n", k=KD))
                    if wr is not None:
                        last = nc.vector.tensor_tensor(logits[:, ds(b * n, n)], out[:, 0:n], br_s[:, :], ALU.add)
                    return last

                if wr is None:
                    consumer = turn_nodes(nc, M, C, block, take, D, KD, keep)
                else:
                    consumer = turn_nodes(nc, M, C, block, take, D, KD, keep, route, [(ld, 16 * (KD + 1))])

                @block.vector
                def _(dve):
                    if wr is not None:
                        dve.wait_ge(ld, 16 * (KD + 1))
                    consumer(dve)
        if wr is not None:
            gating(nc, tag, logits, gates, n)
        with Scope(nc, f"moeb{tag}") as M:
            b2_s = M.sb("b2", [n, D])
            ld = M.sem("ld")
            with nc.Block() as block:
                @block.sync
                def _(sp):
                    sp.dma_start(b2_s[:, :], a[b2]).then_inc(ld, 16)

                def take(b, out):
                    return nc.scalar.activation(out[:, :], gates[:, ds(b * n, n)], ACT.Copy)

                def multiply(turned, out):
                    return nc.tensor.matmul(out[:, 0:D], turned[:, :], b2_s[:, :], start=True, stop=True)

                def consume(b, s, i, turned, out):
                    xb = x[:, ds(b * D, D)]
                    return nc.vector.tensor_tensor(xb, xb, out[:, 0:D], ALU.add)

                consumer = turn_nodes(nc, M, C, block, take, n, 1, consume, multiply, [(ld, 16)])

                @block.vector
                def _(dve):
                    consumer(dve)
        BG = 5
        NG = BG * P
        groups = NB // BG
        half = NG // 2
        with Scope(nc, f"moee{tag}") as M:
            w1_s = [M.sb(f"w1_{s}", [P, KD * HID]) for s in range(2)]
            w2_s = [M.sb(f"w2_{s}", [P, KH * D]) for s in range(2)]
            b1_s = [M.sb(f"b1_{s}", [P, KH]) for s in range(2)]
            h = [M.sb(f"h{s}", [P, KH * NG]) for s in range(2)]
            h_ps = [M.ps(f"h_ps{s}", [P, 512]) for s in range(4)]
            y_ps = [M.ps(f"y_ps{s}", [P, 512]) for s in range(2)]
            gelued, up, down, added, done = (
                M.sem(s) for s in ("gelued", "up", "down", "added", "done"))
            ld = M.sems("ld", 2)
            per = groups * KH * 2
            with nc.Block() as block:
                @block.sync
                def _(sp):
                    with sp.Fori(0, n // 2) as i:
                        for s in range(2):
                            sp.wait_ge(done, i * 2 + s + 1)
                            e = i * 2 + s
                            sp.dma_start(b1_s[s][:, :], a[b1][:, ds(e * KH, KH)]).then_inc(ld[s], 16)
                            sp.dma_start(w1_s[s][:, :].rearrange("p (k h) -> p k h", k=KD),
                                         a[w1][ds(e, 1), :, :].rearrange("o (k p) h -> p (o k) h", p=P)).then_inc(ld[s], 16)
                            sp.dma_start(w2_s[s][:, :].rearrange("p (k d) -> p k d", k=KH),
                                         a[w2][ds(e, 1), :, :].rearrange("o (k p) d -> p (o k) d", p=P)).then_inc(ld[s], 16)

                @block.tensor
                def _(pe):
                    pe.sem_inc(done, 2)
                    pe.sem_inc(down, BG)
                    with pe.Fori(0, n // 2) as i:
                        for s in range(2):
                            pe.wait_ge(ld[s], i * 48 + 48)

                            def first_layer(gr):
                                for m in range(KH):
                                    for r in range(2):
                                        c = s * per + gr * KH * 2 + m * 2 + r
                                        pe.wait_ge(gelued, i * (2 * per) + c + 1)
                                        for k in range(KD):
                                            mm = nc.tensor.matmul(
                                                h_ps[c % 4][:, 0:half],
                                                w1_s[s][:, k * HID + m * P:k * HID + (m + 1) * P],
                                                xnT[:, k * NPAD + gr * NG + r * half:k * NPAD + gr * NG + (r + 1) * half],
                                                start=k == 0, stop=k == KD - 1)
                                        mm.then_inc(up, 1)

                            def second_layer(gr):
                                v = s * groups + gr
                                pe.wait_ge(gelued, i * (2 * per) + (v + 1) * KH * 2 + 4)
                                for j in range(BG):
                                    c = v * BG + j
                                    pe.wait_ge(added, i * (2 * groups * BG) + c + 1)
                                    for m in range(KH):
                                        mm = nc.tensor.matmul(
                                            y_ps[c % 2][:, 0:D], h[v % 2][:, m * NG + j * P:m * NG + (j + 1) * P],
                                            w2_s[s][:, m * D:(m + 1) * D], start=m == 0, stop=m == KH - 1)
                                    mm.then_inc(down, 1)

                            first_layer(0)
                            for gr in range(1, groups):
                                first_layer(gr)
                                second_layer(gr - 1)
                            second_layer(groups - 1)
                            pe.wait_ge(down, i * (2 * groups * BG) + ((s + 1) * groups + 1) * BG)
                            pe.sem_inc(done, 1)

                @block.scalar
                def _(act):
                    act.sem_inc(gelued, 4)
                    with act.Fori(0, n // 2) as i:
                        for s in range(2):
                            act.wait_ge(ld[s], i * 48 + 48)
                            for gr in range(groups):
                                v = s * groups + gr
                                if v >= 1:
                                    act.wait_ge(down, i * (2 * groups * BG) + v * BG)
                                for m in range(KH):
                                    for r in range(2):
                                        c = v * KH * 2 + m * 2 + r
                                        act.wait_ge(up, i * (2 * per) + c + 1)
                                        nc.scalar.activation(
                                            h[v % 2][:, m * NG + r * half:m * NG + (r + 1) * half],
                                            h_ps[c % 4][:, 0:half], ACT.Gelu,
                                            bias=b1_s[s][:, m:m + 1]).then_inc(gelued, 1)

                @block.vector
                def _(dve):
                    dve.sem_inc(added, 2)
                    with dve.Fori(0, n // 2) as i:
                        for s in range(2):
                            for b in range(NB):
                                c = s * NB + b
                                dve.wait_ge(down, i * (2 * NB) + c + BG + 1)
                                if b == 0:
                                    dve.wait_ge(added, i * (2 * NB) + c + 2)
                                xb = x[:, b * D:(b + 1) * D]
                                nc.vector.scalar_tensor_tensor(
                                    xb, y_ps[c % 2][:, 0:D], gates[:, ds(i * 2 + (b * n + s), 1)], xb,
                                    ALU.mult, ALU.add).then_inc(added, 1)


def turned_one_hots(nc, C, tag, E, lists):
    KT, K = E.plan.out, len(lists)
    SLOTS = 8
    with Scope(nc, f"oht{tag}") as L:
        ps = [L.ps(f"ps{s}", [P, 512]) for s in range(SLOTS)]
        row = [L.sb(f"row{s}", [P, G * P], BF16) for s in range(SLOTS)]
        oh = [L.sb(f"oh{s}", [P, G * P], BF16) for s in range(SLOTS)]
        rows, copied, compared = L.sem("rows"), L.sem("copied"), L.sem("compared")
        put = L.sems("put", SLOTS)
        n_it = KT * K // (SLOTS * G)
        with nc.Block() as block:
            @block.tensor
            def _(pe):
                pe.sem_inc(copied, SLOTS)
                with pe.Fori(0, n_it) as i:
                    for s in range(SLOTS):
                        u = i * SLOTS + s
                        columns = lists[s % K][0]
                        pe.wait_ge(copied, u + 1)
                        for t in range(G):
                            mm = nc.tensor.matmul(ps[s][:, t * P:(t + 1) * P],
                                                  columns[:, ds(i * (SLOTS // K * G) + (s // K * G + t), 1)]
                                                  .to_broadcast([P, P]), C.ident_b[:, :], start=True, stop=True)
                        mm.then_inc(rows, 1)

            @block.scalar
            def _(act):
                act.sem_inc(compared, SLOTS)
                with act.Fori(0, n_it) as i:
                    for s in range(SLOTS):
                        u = i * SLOTS + s
                        act.wait_ge(rows, u + 1)
                        act.wait_ge(compared, u + 1)
                        nc.scalar.activation(row[s][:, :], ps[s][:, :], ACT.Copy).then_inc(copied, 1)

            @block.vector
            def _(dve):
                for p in put:
                    dve.sem_inc(p, 16)
                with dve.Fori(0, n_it) as i:
                    for s in range(SLOTS):
                        u = i * SLOTS + s
                        dve.wait_ge(copied, u + SLOTS + 1)
                        dve.wait_ge(put[s], i * 16 + 16)
                        nc.vector.tensor_scalar(oh[s][:, :], row[s][:, :], C.part[:, :], None,
                                                ALU.is_equal).then_inc(compared, 1)

            @block.sync
            def _(sp):
                with sp.Fori(0, n_it) as i:
                    for s in range(SLOTS):
                        u = i * SLOTS + s
                        out = lists[s % K][1]
                        sp.wait_ge(compared, u + SLOTS + 1)
                        sp.dma_start(out[:, ds(i * (SLOTS // K * G * P) + s // K * G * P, G * P)],
                                     oh[s][:, :]).then_inc(put[s], 16)
                for s in range(SLOTS):
                    sp.wait_ge(put[s], 16 * (n_it + 1))


def split_bf16(nc, link, src, parts, rest):
    for j, part in enumerate(parts):
        link(nc.vector.tensor_copy(part, src if j == 0 else rest))
        if j < 2:
            link(nc.vector.tensor_tensor(rest, src if j == 0 else rest, part, ALU.subtract))


def segment_softmax(nc, C, tag, E, scores):
    KT, R = E.plan.out, E.plan.rows
    with Scope(nc, f"seg{tag}") as L:
        upto = L.sb("upto", [P, 2048])
        peak = L.sb("peak", [P, 2048])
        chain, leaky, flipped, ends, ended, carried, carry_t, spread, shifted, back, expd = (
            L.sem(n) for n in ("chain", "leaky", "flipped", "ends", "ended", "carried", "carry_t", "spread",
                               "shifted", "back", "expd"))
        s3 = scores[:, :].rearrange("p (k h) -> p k h", h=4)
        rows = L.sb("rows", [4, 2 * P])
        runs = L.sb("runs", [4, 2 * P])
        carry = L.sb("carry", [P, 8])
        with Scope(nc, f"sega{tag}") as M:
            e_ps = M.ps("e_ps", [P, 2048])
            small = M.ps("small", [P, 512])
            with nc.Block() as block:
                @block.vector
                def _(dve):
                    link = serial(dve, chain)
                    nc.vector.scalar_tensor_tensor(scores[:, :], scores[:, :], 0.2, scores[:, :], ALU.mult,
                                                   ALU.max).then_inc(leaky, 1)
                    dve.wait_ge(flipped, 1)
                    link(nc.vector.tensor_tensor_scan(upto[0:R, :], E.cut[0:R, :], e_ps[0:R, :], FAR, ALU.add, ALU.max))
                    nc.vector.tensor_tensor_scan(peak[0:R, ::-1], E.cut_back[0:R, ::-1], upto[0:R, ::-1], FAR,
                                                 ALU.add, ALU.max).then_inc(ends, 1)
                    dve.wait_ge(ended, 1)
                    link(nc.vector.tensor_copy(rows[:, 0:2 * R], small[0:4, 0:2 * R]))
                    nc.vector.memset(runs[:, 0:1], FAR)
                    link(nc.vector.memset(runs[:, 2 * R - 1:2 * R], FAR))
                    link(nc.vector.tensor_tensor_scan(runs[:, 1:R], E.carry_on[:, 0:R - 1], rows[:, R:2 * R - 1], FAR,
                                                      ALU.add, ALU.max))
                    link(nc.vector.tensor_tensor_scan(runs[:, 2 * R - 2:R - 1:-1], E.carry_back[:, R - 1:0:-1],
                                                      rows[:, R - 1:0:-1], FAR, ALU.add, ALU.max))
                    link(nc.vector.tensor_tensor(runs[:, 0:R], runs[:, 0:R], E.joins[:, 0:R], ALU.add))
                    nc.vector.tensor_tensor(runs[:, R:2 * R], runs[:, R:2 * R], E.joins[:, 1:R + 1],
                                            ALU.add).then_inc(carried, 1)
                    dve.wait_ge(carry_t, 1)
                    link(nc.vector.tensor_copy(carry[0:R, :], small[0:R, 384:392]))
                    for k, out in ((0, E.out_first), (4, E.out_last)):
                        for h in range(4):
                            part = peak[0:R, h * 512:(h + 1) * 512]
                            last = nc.vector.scalar_tensor_tensor(part, out[0:R, :], carry[0:R, k + h:k + h + 1], part,
                                                                  ALU.add, ALU.max)
                        link(last)
                    nc.vector.tensor_tensor(upto[0:R, :], e_ps[0:R, :], peak[0:R, :], ALU.subtract).then_inc(shifted, 1)

                @block.tensor
                def _(pe):
                    pe.wait_ge(leaky, 1)
                    for h in range(4):
                        for q in range(G):
                            mm = nc.tensor.transpose(e_ps[0:R, h * 512 + q * P:h * 512 + (q + 1) * P], s3[:, q::G, h],
                                                     C.ident[:, :])
                    mm.then_inc(flipped, 1)
                    pe.wait_ge(ends, 1)
                    p3 = peak[0:R, :].rearrange("p (h j) -> p h j", h=4)
                    nc.tensor.transpose(small[0:4, 0:R], p3[:, :, 0], C.ident[0:R, 0:R])
                    nc.tensor.transpose(small[0:4, R:2 * R], p3[:, :, 511], C.ident[0:R, 0:R]).then_inc(ended, 1)
                    pe.wait_ge(carried, 1)
                    nc.tensor.transpose(small[0:R, 384:388], runs[:, 0:R], C.ident[0:4, 0:4])
                    nc.tensor.transpose(small[0:R, 388:392], runs[:, R:2 * R], C.ident[0:4, 0:4]).then_inc(carry_t, 1)
        with Scope(nc, f"segb{tag}") as M:
            b_ps = M.ps("b_ps", [P, 2048])
            with nc.Block() as block:
                @block.tensor
                def _(pe):
                    for h in range(4):
                        for q in range(G):
                            mm = nc.tensor.transpose(b_ps[:, (q * 4 + h) * P:(q * 4 + h) * P + R],
                                                     upto[0:R, h * 512 + q * P:h * 512 + (q + 1) * P], C.ident[0:R, 0:R])
                    mm.then_inc(back, 1)

                @block.scalar
                def _(act):
                    act.wait_ge(back, 1)
                    for q in range(G):
                        nc.scalar.activation(
                            s3[:, q::G, :].rearrange("p r h -> p h r"),
                            b_ps[:, q * 512:(q + 1) * 512].rearrange("p (h r) -> p h r", h=4)[:, :, 0:R], ACT.Exp)


def gat_layer(nc, C, S, a, n, E, block_of, h_in, acc, table, oht_src, oht_dst):
    KT, DW = E.plan.out, D + 4
    with Scope(nc, f"gat{n}") as L:
        score = L.sb("score", [P, NB * 8])
        src3 = L.sb("src3", [P, 3 * NB * 4], BF16)
        dst3 = L.sb("dst3", [P, NB * 3 * 4], BF16)
        with Scope(nc, f"gatn{n}") as M:
            w = M.sb("w", [P, 2 * (D + 8)])
            w3 = w[:, :].rearrange("p (k f) -> p k f", k=2)
            att = M.sb("att", [P, 2 * D])
            prod = M.sb("prod", [P, 4 * D])
            row = [M.sb(f"row{s}", [P, D]) for s in range(RING)]
            rest = M.sb("rest", [P, NB * 4])
            ld, chain, ready, rowed = (M.sem(s) for s in ("ld", "chain", "ready", "rowed"))
            stored = M.sems("stored", RING)
            with nc.Block() as block:
                @block.sync
                def _(sp):
                    loads(sp, ld, [(w3[:, k, 0:D], a[f"L1_gnn_W{n}"][k * P:(k + 1) * P, :]) for k in range(2)]
                          + [(att[:, 0:D], broadcast_rows(a[f"L1_gnn_a_src{n}"].rearrange("h c -> (h c)"))),
                             (att[:, D:], broadcast_rows(a[f"L1_gnn_a_dst{n}"].rearrange("h c -> (h c)")))])

                    def store(b, s, i):
                        sp.wait_ge(rowed, b + 1)
                        sp.dma_start(table[ds(b * P, P), 0:D], row[s][:, :]).then_inc(stored[s], 16)
                    over_nodes(sp, store)
                    for s in range(RING):
                        sp.wait_ge(stored[s], 16 * -(-(NB - s) // RING))

                def take(b, out):
                    return nc.scalar.activation(out[:, :], h_in[:, ds(b * D, D)], ACT.Copy if n == 1 else ACT.Relu)

                def multiply(turned, out):
                    for k in range(2):
                        mm = nc.tensor.matmul(out[:, 0:D + 8], turned[:, k * P:(k + 1) * P], w3[:, k, :],
                                              start=k == 0, stop=k == 1)
                    return mm

                def consume(b, s, i, turned, out):
                    after(nc.vector, stored[s], i * 16)
                    nc.vector.tensor_copy(row[s][:, :], out[:, 0:D]).then_inc(rowed, 1)
                    return nc.vector.tensor_copy(score[:, ds(b * 8, 8)], out[:, D:D + 8])

                consumer = turn_nodes(nc, M, C, block, take, D, 2, consume, multiply, [(ld, 64), (ready, 1)])

                @block.vector
                def _(dve):
                    link = serial(dve, chain)
                    dve.wait_ge(ld, 64)
                    p4 = prod[:, :].rearrange("p (k g f) -> p k g f", k=2, g=2)
                    for k in range(2):
                        last = nc.vector.tensor_tensor(p4[:, k, :, :], w3[:, k, 0:D].unsqueeze(1).to_broadcast([P, 2, D]),
                                                       att[:, :].rearrange("p (g f) -> p g f", g=2), ALU.mult)
                    link(last)
                    for k in range(2):
                        last = nc.vector.tensor_reduce(
                            w3[:, k, D:D + 8], prod[:, k * 2 * D:(k + 1) * 2 * D].rearrange("p (g c) -> p g c", c=64),
                            AX.X, ALU.add)
                    last.then_inc(ready, 1)

                    consumer(dve)
                    sc3 = score[:, :].rearrange("p (b k) -> p b k", k=8)
                    part_rest = rest[:, :].rearrange("p (b h) -> p b h", h=4)
                    split_bf16(nc, link, sc3[:, :, 0:4],
                               [src3[:, :].rearrange("p (j b h) -> p j b h", j=3, h=4)[:, j] for j in range(3)], part_rest)
                    split_bf16(nc, link, sc3[:, :, 4:8],
                               [dst3[:, :].rearrange("p (b j h) -> p j b h", j=3, h=4)[:, j] for j in range(3)], part_rest)

        edge = L.sb("edge", [P, KT * 4])
        early = [L.sb(f"early{u}", [P, G * D]) for u in range(EARLY)]
        with Scope(nc, f"gats{n}") as M:
            W = (NB + 3) * 4
            os_ = [M.sb(f"os{s}", [P, G * P], BF16) for s in range(RING)]
            od_ = [M.sb(f"od{s}", [P, G * P], BF16) for s in range(RING)]
            ohb = [M.sb(f"ohb{s}", [P, G * (NB + 3)]) for s in range(2)]
            prod = [M.sb(f"prod{s}", [P, G * W]) for s in range(2)]
            r_ps = [M.ps(f"r_ps{s}", [P, 512]) for s in range(RING)]
            filled, looked, chosen, multed, reduced = (
                M.sem(s) for s in ("filled", "looked", "chosen", "multed", "reduced"))
            came = M.sems("came", RING)
            early_got = M.sem("early_got")
            n_it = KT // (RING * G)
            with nc.Block() as block:
                @block.gpsimd
                def _(pool):
                    for u in range(EARLY):
                        for t in range(G):
                            nc.gpsimd.indirect_dma_start(
                                early[u][:, t * D:(t + 1) * D], None, table[:, 0:D],
                                bass.IndirectOffsetOnAxis(ap=E.src[:, u * G + t:u * G + t + 1], axis=0)).then_inc(early_got, 16)
                    pool.wait_ge(early_got, 16 * G * EARLY)

                @block.sync
                def _(sp):
                    with sp.Fori(0, n_it) as i:
                        for s in range(RING):
                            u = i * RING + s
                            sp.wait_ge(looked, u + 1)
                            sp.dma_start(os_[s][:, :], oht_src[:, ds(u * (G * P), G * P)]).then_inc(came[s], 16)
                            sp.dma_start(od_[s][:, :], oht_dst[:, ds(u * (G * P), G * P)]).then_inc(came[s], 16)

                @block.tensor
                def _(pe):
                    blks = Blocks(pe, f"gats{n}_blk", block_of)
                    pe.sem_inc(looked, RING)
                    with pe.Fori(0, n_it) as i:
                        blks.load(i)
                        for s in range(RING):
                            u = i * RING + s
                            pe.wait_ge(came[s], i * 32 + 32)
                            pe.wait_ge(multed, u + 1)
                            for t in range(G):
                                for j in range(3):
                                    nc.tensor.matmul(r_ps[s][:, t * W:t * W + NB * 4], os_[s][:, t * P:(t + 1) * P],
                                                     src3[:, j * NB * 4:(j + 1) * NB * 4], start=j == 0, stop=j == 2)
                                mm = nc.tensor.matmul(r_ps[s][:, t * W + NB * 4:(t + 1) * W], od_[s][:, t * P:(t + 1) * P],
                                                      dst3[:, ds(blks.of[s * G + t] * 12, 12)], start=True, stop=True)
                            mm.then_inc(looked, 1)

                @block.vector
                def _(dve):
                    def choose(u, s):
                        nc.vector.tensor_tensor(
                            ohb[s % 2][:, :].rearrange("p (t b) -> p t b", t=G)[:, :, 0:NB],
                            C.ramp[:, 0:NB].unsqueeze(1).to_broadcast([P, G, NB]),
                            E.src_blk[:, ds(u * G, G)].unsqueeze(2).to_broadcast([P, G, NB]),
                            ALU.is_equal).then_inc(chosen, 1)

                    def step(u, s, more=True):
                        dve.wait_ge(chosen, u + 1)
                        dve.wait_ge(reduced, u + 1)
                        dve.wait_ge(looked, u + RING + 1)
                        nc.vector.tensor_tensor(
                            prod[s % 2][:, :].rearrange("p (b h) -> p b h", h=4),
                            r_ps[s][:, 0:G * W].rearrange("p (b h) -> p b h", h=4),
                            ohb[s % 2][:, :].unsqueeze(2).to_broadcast([P, G * (NB + 3), 4]), ALU.mult).then_inc(multed, 1)
                        if more:
                            choose(u + 1, s + 1)
                        dve.wait_ge(multed, u + RING + 1)
                        nc.vector.tensor_reduce(edge[:, ds(u * (G * 4), G * 4)].rearrange("p (t h) -> p t h", t=G),
                                                prod[s % 2][:, :].rearrange("p (t b h) -> p t h b", t=G, h=4),
                                                AX.X, ALU.add).then_inc(reduced, 1)

                    for o in ohb:
                        nc.vector.memset(o[:, :], 1.0).then_inc(filled, 1)
                    dve.wait_ge(filled, 2)
                    dve.sem_inc(multed, RING)
                    dve.sem_inc(reduced, 2)
                    choose(0, 0)
                    with dve.Fori(0, n_it - 1) as i:
                        for s in range(RING):
                            step(i * RING + s, s)
                    for s in range(RING):
                        step((n_it - 1) * RING + s, s, more=s + 1 < RING)

        segment_softmax(nc, C, f"{n}", E, edge)

        with Scope(nc, f"gata{n}") as M:
            idx = [M.sb(f"idx{s}", [P, G], I32) for s in range(RING)]
            got = [M.sb(f"got{s}", [P, G * D]) for s in range(RING)]
            msg = [M.sb(f"msg{s}", [P, G * DW]) for s in range(RING)]
            pick = [M.sb(f"pick{s}", [P, G * P]) for s in range(RING)]
            sum_ps = [M.ps(f"sum_ps{s}", [P, 512]) for s in range(LAG * G)]
            idxed, gate, weighed, copied, summed, added, cleared = (
                M.sem(s) for s in ("idxed", "gate", "weighed", "copied", "summed", "added", "cleared"))
            arrived = M.sems("arrived", RING)
            V = KT // G
            n_it = V // RING
            with nc.Block() as block:
                @block.gpsimd
                def _(pool):
                    with pool.Fori(EARLY // RING, n_it) as i:
                        for s in range(RING):
                            pool.wait_ge(idxed, i * RING + (s + 1 - EARLY))
                            nc.gpsimd.sem_inc(gate, 1)
                            for t in range(G):
                                nc.gpsimd.indirect_dma_start(
                                    got[s][:, t * D:(t + 1) * D], None, table[:, 0:D],
                                    bass.IndirectOffsetOnAxis(ap=idx[s][:, t:t + 1], axis=0)).then_inc(arrived[s], 16)

                @block.scalar
                def _(act):
                    def index(u, s):
                        nc.scalar.activation(idx[s][:, :], E.src[:, ds(u * G, G)], ACT.Copy).then_inc(idxed, 1)

                    def step(u, s, i):
                        if there(u, V) and not (isinstance(u, int) and u < EARLY + RING):
                            act.wait_ge(weighed, u - (RING - 1))
                            index(u, s)
                        after(act, summed, u - (RING - 1))
                        nc.scalar.activation(
                            msg[s][:, :].rearrange("p (t f) -> p t f", t=G)[:, :, D:DW],
                            edge[:, ds(u * (G * 4), G * 4)].rearrange("p (t h) -> p t h", t=G),
                            ACT.Copy).then_inc(copied, 1)

                    for s in range(RING):
                        index(EARLY + s, s)
                    run_steps(act, step, V, 0, peeled=EARLY // RING + 1)

                @block.vector
                def _(dve):
                    blks = Blocks(dve, f"gata{n}_blk", block_of)

                    def choose(u, s):
                        after(dve, summed, u - (RING - 1))
                        nc.vector.tensor_tensor(
                            pick[s][:, :].rearrange("p (t d) -> p t d", t=G),
                            C.ramp[:, :].unsqueeze(1).to_broadcast([P, G, P]),
                            E.low[:, ds(u * G, G)].unsqueeze(2).to_broadcast([P, G, P]), ALU.is_equal)

                    def weigh(u, s, t):
                        rows = early[u] if isinstance(u, int) and u < EARLY else got[s]
                        return nc.vector.tensor_tensor(
                            msg[s][:, t * DW:t * DW + D].rearrange("p (h c) -> p h c", h=4),
                            rows[:, t * D:(t + 1) * D].rearrange("p (h c) -> p h c", h=4),
                            edge[:, ds(u * (G * 4) + t * 4, 4)].unsqueeze(2).to_broadcast([P, 4, 64]), ALU.mult)

                    def take(u, s, t):
                        dve.wait_ge(added, u * G + (LAG * G + t))
                        dst = acc[:, ds(blks.of[s * G + t] * DW, DW)]
                        nc.vector.tensor_tensor(dst, dst, sum_ps[(s % LAG) * G + t][:, 0:DW], ALU.add).then_inc(added, 1)

                    def step(u, s, i):
                        f = (s + LAG) % RING
                        if there(u + LAG, V):
                            choose(u + LAG, f)
                            after(dve, arrived[f], (i + ((s + LAG) // RING + 1 - EARLY // RING)) * (16 * G))
                        for t in range(G):
                            if there(u + LAG, V):
                                last = weigh(u + LAG, f, t)
                            if there(u, V):
                                if t == 0:
                                    dve.wait_ge(summed, u + 1)
                                take(u, s, t)
                        if there(u + LAG, V):
                            last.then_inc(weighed, 1)

                    nc.vector.memset(acc[:, :], 0.0).then_inc(cleared, 1)
                    dve.sem_inc(added, LAG * G)
                    dve.wait_ge(cleared, 1)
                    run_steps(dve, step, V, LAG, blks.load, peeled=EARLY // RING)

                @block.tensor
                def _(pe):
                    with pe.Fori(0, n_it) as i:
                        for s in range(RING):
                            u = i * RING + s
                            pe.wait_ge(copied, u + 1)
                            pe.wait_ge(weighed, u + 1)
                            pe.wait_ge(added, u * G + G)
                            for t in range(G):
                                mm = nc.tensor.matmul(sum_ps[(s % LAG) * G + t][:, 0:DW], pick[s][:, t * P:(t + 1) * P],
                                                      msg[s][:, t * DW:(t + 1) * DW], start=True, stop=True)
                            mm.then_inc(summed, 1)


def gat_output(nc, a, n, acc, h, x):
    DW = D + 4
    with Scope(nc, f"gato{n}") as L:
        bias = L.sb("bias", [P, D])
        inv = L.sb("inv", [P, NB * 4])
        norm = L.sb("norm", [P, NB])
        ld, chain, squares, root = L.sem("ld"), L.sem("chain"), L.sem("squares"), L.sem("root")
        a3 = acc[:, :].rearrange("p (b f) -> p b f", f=DW)
        h3 = h[:, :].rearrange("p (b d) -> p b d", d=D)
        i3 = inv[:, :].rearrange("p (b h) -> p b h", h=4)
        with nc.Block() as block:
            @block.sync
            def _(sp):
                sp.dma_start(bias[:, :], broadcast_rows(a[f"L1_gnn_b{n}"])).then_inc(ld, 16)

            @block.vector
            def _(dve):
                link = serial(dve, chain)
                link(nc.vector.tensor_scalar(i3, a3[:, :, D:DW], 1e-16, None, ALU.add))
                link(nc.vector.reciprocal(inv[:, :], inv[:, :]))
                for hd in range(4):
                    c = slice(hd * 64, (hd + 1) * 64)
                    last = nc.vector.tensor_tensor(h3[:, :, c], a3[:, :, c], i3[:, :, hd:hd + 1].to_broadcast([P, NB, 64]),
                                                   ALU.mult)
                link(last)
                dve.wait_ge(ld, 16)
                link(nc.vector.tensor_tensor(h3, h3, bias[:, :].unsqueeze(1).to_broadcast([P, NB, D]), ALU.add))
                if n == 3:
                    sq = acc[:, 0:NB * D]
                    link(nc.vector.tensor_tensor(sq, h[:, :], h[:, :], ALU.mult))
                    nc.vector.tensor_reduce(norm[:, :], sq.rearrange("p (b d) -> p b d", d=D), AX.X,
                                            ALU.add).then_inc(squares, 1)
                    dve.wait_ge(root, 1)
                    link(nc.vector.tensor_scalar(norm[:, :], norm[:, :], 1e-12, None, ALU.max))
                    link(nc.vector.reciprocal(norm[:, :], norm[:, :]))
                    link(nc.vector.tensor_tensor(h3, h3, norm[:, :].unsqueeze(2).to_broadcast([P, NB, D]), ALU.mult))
                    link(nc.vector.tensor_tensor(x[:, :], x[:, :], h[:, :], ALU.add))

            if n == 3:
                @block.scalar
                def _(act):
                    act.wait_ge(squares, 1)
                    nc.scalar.activation(norm[:, :], norm[:, :], ACT.Sqrt).then_inc(root, 1)


def router(nc, C, S, a, E, block_of, xn, table, oht_dst, gates):
    KT, F = E.plan.out, 20
    with Scope(nc, "rt") as L:
        dst3 = L.sb("dst3", [P, 3 * NB * 4], BF16)
        with Scope(nc, "rtn") as M:
            w = M.sb("w", [P, 2 * 16])
            att = M.sb("att", [P, 32])
            all_in = M.sb("all_in", [P, NB * 24])
            prod = M.sb("prod", [P, NB * 16])
            rest = M.sb("rest", [P, NB * 4])
            ld, chain, ready, stored = (M.sem(s) for s in ("ld", "chain", "ready", "stored"))
            a3 = all_in[:, :].rearrange("p (b f) -> p b f", f=24)
            with nc.Block() as block:
                @block.sync
                def _(sp):
                    loads(sp, ld, [(w[:, k * 16:(k + 1) * 16], a["L1_ffn_W_gat"][k * P:(k + 1) * P, :]) for k in range(2)]
                          + [(att[:, 0:16], broadcast_rows(a["L1_ffn_att_src"].rearrange("h c -> (h c)"))),
                             (att[:, 16:], broadcast_rows(a["L1_ffn_att_dst"].rearrange("h c -> (h c)")))])
                    sp.wait_ge(ready, 1)
                    sp.dma_start(table.rearrange("(b p) f -> p b f", p=P), a3[:, :, 0:F]).then_inc(stored, 16)
                    sp.wait_ge(stored, 16)

                def take(b, out):
                    return nc.scalar.activation(out[:, :], xn[:, ds(b * D, D)], ACT.Copy)

                def multiply(turned, out):
                    for k in range(2):
                        mm = nc.tensor.matmul(out[:, 0:16], turned[:, k * P:(k + 1) * P], w[:, k * 16:(k + 1) * 16],
                                              start=k == 0, stop=k == 1)
                    return mm

                def consume(b, s, i, turned, out):
                    return nc.vector.tensor_copy(all_in[:, ds(b * 24, 16)], out[:, 0:16])

                consumer = turn_nodes(nc, M, C, block, take, D, 2, consume, multiply, [(ld, 64)])

                @block.vector
                def _(dve):
                    link = serial(dve, chain)
                    consumer(dve)
                    dve.wait_ge(ld, 64)
                    p3 = prod[:, :].rearrange("p (b f) -> p b f", f=16)
                    for g in range(2):
                        link(nc.vector.tensor_tensor(p3, a3[:, :, 0:16], att[:, g * 16:(g + 1) * 16].unsqueeze(1)
                                                     .to_broadcast([P, NB, 16]), ALU.mult))
                        link(nc.vector.tensor_reduce(a3[:, :, 16 + 4 * g:20 + 4 * g],
                                                     prod[:, :].rearrange("p (b h c) -> p b h c", h=4, c=4), AX.X, ALU.add))
                    dve.sem_inc(ready, 1)
                    parts = [dst3[:, :].rearrange("p (b j h) -> p j b h", j=3, h=4)[:, j] for j in range(3)]
                    split_bf16(nc, link, a3[:, :, 20:24], parts, rest[:, :].rearrange("p (b h) -> p b h", h=4))

        msg = L.sb("msg", [P, KT * F])
        edge = L.sb("edge", [P, KT * 4])
        with Scope(nc, "rts") as M:
            idx = [M.sb(f"idx{s}", [P, G], I32) for s in range(RING)]
            got = [M.sb(f"got{s}", [P, G * F]) for s in range(RING)]
            od_ = [M.sb(f"od{s}", [P, G * P], BF16) for s in range(RING)]
            d_ps = [M.ps(f"d_ps{s}", [P, 512]) for s in range(RING)]
            idxed, gate, looked, taken = (M.sem(s) for s in ("idxed", "gate", "looked", "taken"))
            arrived, came = M.sems("arrived", RING), M.sems("came", RING)
            n_it = KT // (RING * G)
            with nc.Block() as block:
                @block.gpsimd
                def _(pool):
                    with pool.Fori(0, n_it) as i:
                        for s in range(RING):
                            pool.wait_ge(idxed, i * RING + s + 1)
                            nc.gpsimd.sem_inc(gate, 1)
                            for t in range(G):
                                nc.gpsimd.indirect_dma_start(
                                    got[s][:, t * F:(t + 1) * F], None, table,
                                    bass.IndirectOffsetOnAxis(ap=idx[s][:, t:t + 1], axis=0)).then_inc(arrived[s], 16)

                @block.scalar
                def _(act):
                    with act.Fori(0, n_it) as i:
                        for s in range(RING):
                            u = i * RING + s
                            act.wait_ge(taken, u + 1)
                            nc.scalar.activation(idx[s][:, :], E.src[:, ds(u * G, G)], ACT.Copy).then_inc(idxed, 1)

                @block.sync
                def _(sp):
                    with sp.Fori(0, n_it) as i:
                        for s in range(RING):
                            u = i * RING + s
                            sp.wait_ge(looked, u + 1)
                            sp.dma_start(od_[s][:, :], oht_dst[:, ds(u * (G * P), G * P)]).then_inc(came[s], 16)

                @block.tensor
                def _(pe):
                    blks = Blocks(pe, "rts_blk", block_of)
                    pe.sem_inc(looked, RING)
                    with pe.Fori(0, n_it) as i:
                        blks.load(i)
                        for s in range(RING):
                            u = i * RING + s
                            pe.wait_ge(came[s], i * 16 + 16)
                            pe.wait_ge(taken, u + 1)
                            for t in range(G):
                                for j in range(3):
                                    mm = nc.tensor.matmul(d_ps[s][:, t * 4:(t + 1) * 4], od_[s][:, t * P:(t + 1) * P],
                                                          dst3[:, ds(blks.of[s * G + t] * 12 + j * 4, 4)],
                                                          start=j == 0, stop=j == 2)
                            mm.then_inc(looked, 1)

                @block.vector
                def _(dve):
                    dve.sem_inc(taken, RING)
                    with dve.Fori(0, n_it) as i:
                        for s in range(RING):
                            u = i * RING + s
                            dve.wait_ge(arrived[s], (i + 1) * (16 * G))
                            nc.vector.tensor_copy(msg[:, ds(u * (G * F), G * F)], got[s][:, :])
                            dve.wait_ge(looked, u + RING + 1)
                            nc.vector.tensor_tensor(
                                edge[:, ds(u * (G * 4), G * 4)].rearrange("p (t h) -> p t h", t=G),
                                got[s][:, :].rearrange("p (t f) -> p t f", t=G)[:, :, 16:20],
                                d_ps[s][:, 0:G * 4].rearrange("p (t h) -> p t h", t=G), ALU.add).then_inc(taken, 1)

        segment_softmax(nc, C, "r", E, edge)

        acc = L.sb("acc", [P, NB * F])
        with Scope(nc, "rta") as M:
            pick = [M.sb(f"pick{s}", [P, G * P]) for s in range(RING)]
            sum_ps = [M.ps(f"sum_ps{s}", [P, 512]) for s in range(RING)]
            chain, ready, picked, summed, added = (M.sem(s) for s in ("chain", "ready", "picked", "summed", "added"))
            m3 = msg[:, :].rearrange("p (k f) -> p k f", f=F)
            e3 = edge[:, :].rearrange("p (k h) -> p k h", h=4)
            n_it = KT // (RING * G)
            with nc.Block() as block:
                @block.vector
                def _(dve):
                    blks = Blocks(dve, "rta_blk", block_of)
                    link = serial(dve, chain)
                    nc.vector.memset(acc[:, :], 0.0)
                    for hd in range(4):
                        c = slice(hd * 4, hd * 4 + 4)
                        nc.vector.tensor_tensor(m3[:, :, c], m3[:, :, c], e3[:, :, hd:hd + 1].to_broadcast([P, KT, 4]),
                                                ALU.mult)
                    link(nc.vector.tensor_copy(m3[:, :, 16:20], e3))
                    dve.sem_inc(ready, 1)

                    def choose(u, s, t):
                        return nc.vector.tensor_scalar(pick[s][:, t * P:(t + 1) * P], C.ramp[:, :],
                                                       E.low[:, ds(u * G + t, 1)], None, ALU.is_equal)

                    def step(u, s, more=True):
                        for t in range(G):
                            if more:
                                last = choose(u + LAG, (s + LAG) % RING, t)
                            if t == 0:
                                dve.wait_ge(summed, u + 1)
                            dve.wait_ge(added, u * G + (t + LAG * G))
                            dst = acc[:, ds(blks.of[s * G + t] * F, F)]
                            nc.vector.tensor_tensor(dst, dst, sum_ps[s][:, t * F:(t + 1) * F], ALU.add).then_inc(added, 1)
                        if more:
                            last.then_inc(picked, 1)

                    dve.sem_inc(added, LAG * G)
                    for u in range(LAG):
                        for t in range(G):
                            last = choose(u, u, t)
                        last.then_inc(picked, 1)
                    with dve.Fori(0, n_it - 1) as i:
                        blks.load(i)
                        for s in range(RING):
                            step(i * RING + s, s)
                    blks.load(n_it - 1)
                    for s in range(RING):
                        step((n_it - 1) * RING + s, s, more=s + LAG < RING)

                @block.tensor
                def _(pe):
                    pe.wait_ge(ready, 1)
                    with pe.Fori(0, n_it) as i:
                        for s in range(RING):
                            u = i * RING + s
                            pe.wait_ge(picked, u + 1)
                            pe.wait_ge(added, u * G + (LAG - 1) * G)
                            for t in range(G):
                                mm = nc.tensor.matmul(sum_ps[s][:, t * F:(t + 1) * F], pick[s][:, t * P:(t + 1) * P],
                                                      msg[:, ds((u * G + t) * F, F)], start=True, stop=True)
                            mm.then_inc(summed, 1)
        with Scope(nc, "rto") as M:
            rows = M.sb("rows", [P, 48])
            inv = M.sb("inv", [P, NB * 4])
            agg = M.sb("agg", [P, NB * 16])
            norm = M.sb("norm", [P, NB * 16])
            logits = M.sb("logits", [P, NB * 4])
            ld, chain = M.sem("ld"), M.sem("chain")
            a3 = acc[:, :].rearrange("p (b f) -> p b f", f=F)
            g3 = agg[:, :].rearrange("p (b f) -> p b f", f=16)
            i3 = inv[:, :].rearrange("p (b h) -> p b h", h=4)
            with nc.Block() as block:
                @block.sync
                def _(sp):
                    loads(sp, ld, [(rows[:, 0:16], broadcast_rows(a["L1_ffn_b_gat"])),
                                   (rows[:, 16:32], broadcast_rows(a["L1_ffn_ln_gamma"])),
                                   (rows[:, 32:48], broadcast_rows(a["L1_ffn_ln_beta"]))])
                    sp.wait_ge(ld, 48)

                @block.vector
                def _(dve):
                    link = serial(dve, chain)
                    link(nc.vector.tensor_scalar(i3, a3[:, :, 16:20], 1e-16, None, ALU.add))
                    link(nc.vector.reciprocal(inv[:, :], inv[:, :]))
                    for hd in range(4):
                        c = slice(hd * 4, hd * 4 + 4)
                        last = nc.vector.tensor_tensor(g3[:, :, c], a3[:, :, c], i3[:, :, hd:hd + 1].to_broadcast([P, NB, 4]),
                                                       ALU.mult)
                    link(last)
                    dve.wait_ge(ld, 48)
                    link(nc.vector.tensor_tensor(g3, g3, rows[:, 0:16].unsqueeze(1).to_broadcast([P, NB, 16]), ALU.add))
            layer_norm(nc, "rt", agg, norm, width=16, scale=rows[:, 16:32], shift=rows[:, 32:48])
            with nc.Block() as block:
                @block.vector
                def _(dve):
                    link = serial(dve, chain, 4)
                    link(nc.vector.tensor_reduce(logits[:, :].rearrange("p (b e) -> p b e", e=4),
                                                 norm[:, :].rearrange("p (b h e) -> p b e h", h=4, e=4), AX.X, ALU.add))
                    link(nc.vector.tensor_scalar(logits[:, :], logits[:, :], 0.25, None, ALU.mult))
            gating(nc, "rt", logits, gates, 4)


def load_nodes(nc, x_in, x):
    full = N // P
    with Scope(nc, "nodes") as L:
        zeroed, got = L.sem("zeroed"), L.sem("got")
        with nc.Block() as block:
            @block.vector
            def _(dve):
                nc.vector.memset(x[:, full * D:], 0.0).then_inc(zeroed, 1)

            @block.sync
            def _(sp):
                sp.dma_start(x[:, 0:full * D].rearrange("p (b d) -> p b d", d=D),
                             x_in[0:full * P, :].rearrange("(b p) d -> p b d", p=P)).then_inc(got, 16)
                sp.wait_ge(zeroed, 1)
                sp.dma_start(x[0:N - full * P, full * D:], x_in[full * P:N, :]).then_inc(got, 16)
                sp.wait_ge(got, 32)


def store_nodes(nc, x, out):
    full = N // P
    with Scope(nc, "out") as L:
        put = L.sem("put")
        with nc.Block() as block:
            @block.sync
            def _(sp):
                sp.dma_start(out[0:full * P, :].rearrange("(b p) d -> p b d", p=P),
                             x[:, 0:full * D].rearrange("p (b d) -> p b d", d=D)).then_inc(put, 16)
                sp.dma_start(out[full * P:N, :], x[0:N - full * P, full * D:]).then_inc(put, 16)
                sp.wait_ge(put, 32)


GNN = edge_plan(53125 + 625, 16)
ROUTE = edge_plan(32768 + N, 2)


def program(nc, a, out, stop=9):
    with Scope(nc, "all") as S:
        C = make_constants(nc, S)
        x = S.sb("x", [P, NB * D])
        load_nodes(nc, a["x"], x)
        gnn_sorted = nc.dram_tensor("gnn_sorted", [GNN.out * P, GNN.width], F32).ap()
        route_sorted = nc.dram_tensor("route_sorted", [ROUTE.out * P, ROUTE.width], F32).ap()
        table = nc.dram_tensor("table", [NPAD, D], F32).ap()
        route_table = nc.dram_tensor("route_table", [NPAD, 20], F32).ap()
        oht_src = nc.dram_tensor("oht_src", [P, GNN.out * P], BF16).ap()
        oht_dst = nc.dram_tensor("oht_dst", [P, GNN.out * P], BF16).ap()
        block_of = S.sb("block_of", [1, GNN.out], I32)
        if stop in (0, 1, 2, 9):
            sort_edges(nc, C, GNN, "g", a["gnn_src"], a["gnn_dst"], a["gnn_attr"], gnn_sorted, block_of)
            with Scope(nc, "gnn") as T:
                E = Edges(T, "g", GNN)
                with Scope(nc, "recs") as U:
                    rec = U.sb("rec", [P, GNN.out * GNN.width])
                    prepare_edges(nc, C, E, "g", gnn_sorted, rec)
                    equivariant_layer(nc, C, T, a, E, block_of, x, table)
                if stop >= 1:
                    with Scope(nc, "ffn0") as U:
                        xn = U.sb("xn", [P, NB * D])
                        rows = U.sb("rows", [P, 2 * D])
                        load_rows(nc, "ffn0", rows, [a["L0_ffn_gamma"], a["L0_ffn_beta"]])
                        layer_norm(nc, "f0", x, xn)
                        layer_norm(nc, "f1", xn, xn, scale=rows[:, 0:D], shift=rows[:, D:])
                        experts(nc, C, "0", xn, x, 8, a, "L0_ffn_W1", "L0_ffn_b1", "L0_ffn_W2", "L0_ffn_b2",
                                wr="L0_ffn_Wr", br="L0_ffn_br")
                if stop >= 2:
                    with Scope(nc, "gats") as U:
                        h = U.sb("h", [P, NB * D])
                        acc = U.sb("acc", [P, NB * (D + 4)])
                        layer_norm(nc, "g", x, h)
                        turned_one_hots(nc, C, "g", E, [(E.src_low, oht_src), (E.low_b, oht_dst)])
                        for n in (1, 2, 3):
                            gat_layer(nc, C, U, a, n, E, block_of, h, acc, table, oht_src, oht_dst)
                            gat_output(nc, a, n, acc, h, x)
        if stop >= 3:
            with Scope(nc, "route") as T:
                xn = T.sb("xn", [P, NB * D])
                gates = T.sb("gates", [P, NB * 4])
                layer_norm(nc, "r", x, xn)
                with Scope(nc, "routes") as U:
                    sort_edges(nc, C, ROUTE, "r", a["route_src"], a["route_dst"], None, route_sorted, block_of)
                    E = Edges(U, "r", ROUTE)
                    rec = U.sb("rec", [P, ROUTE.out * ROUTE.width])
                    prepare_edges(nc, C, E, "r", route_sorted, rec)
                    turned_one_hots(nc, C, "r", E, [(E.low_b, oht_dst)])
                    router(nc, C, U, a, E, block_of, xn, route_table, oht_dst, gates)
                experts(nc, C, "1", xn, x, 4, a, "L1_ffn_W1", "L1_ffn_b1", "L1_ffn_W2", "L1_ffn_b2", gates=gates)
        store_nodes(nc, x, out)


def load_rows(nc, tag, rows, vectors):
    with Scope(nc, f"rows{tag}") as L:
        ld = L.sem("ld")
        with nc.Block() as block:
            @block.sync
            def _(sp):
                sp.wait_ge(ld, loads(sp, ld, [(rows[:, k * D:(k + 1) * D], broadcast_rows(v))
                                              for k, v in enumerate(vectors)]))


def cut_edges(plan, src, dst, loops):
    fill = plan.tiles * P - plan.edges
    loops = np.arange(loops, dtype=np.int32)
    return (np.concatenate([src, loops, np.zeros(fill, np.int32)]).reshape(P, -1),
            np.concatenate([dst, loops, np.full(fill, KEY_PAD, np.int32)]).reshape(P, -1))


def layout(inputs):
    a = {k: np.ascontiguousarray(v) for k, v in inputs.items()}
    src, dst = a.pop("src"), a.pop("dst")
    e4, e8 = a.pop("edge_attr_4"), a.pop("edge_attr_8")
    a["gnn_src"], a["gnn_dst"] = cut_edges(GNN, src, dst, 625)
    route = a.pop("L1_ffn_edge_index")
    a["route_src"], a["route_dst"] = cut_edges(ROUTE, route[0], route[1], N)
    attr = np.zeros((GNN.tiles * P, GNN.width), np.float32)
    attr[:len(src), 2:6] = e4
    attr[:len(src), 6:14] = e8
    a["gnn_attr"] = attr.reshape(P, -1)
    z = np.zeros((NPAD, 1), np.float32)
    z[:N] = a["node_vec1"]
    a["node_vec1"] = np.ascontiguousarray(z.reshape(NB, P).T)
    for b in ("L0_ffn_b1", "L1_ffn_b1"):
        a[b] = np.ascontiguousarray(a[b].reshape(-1, P).T)
    return a


def kernel(**inputs):
    import concourse.bacc as _bacc
    from concourse.bass_utils import run_bass_kernel_spmd as _run

    arrays = {f"in_{k}": v for k, v in layout(inputs).items()}
    nc = _bacc.Bacc("TRN2", target_bir_lowering=False, num_devices=1)
    a = {k[3:]: nc.dram_tensor(k, v.shape, mybir.dt.from_np(v.dtype), kind="ExternalInput").ap()
         for k, v in arrays.items()}
    out = nc.dram_tensor("out_0", (N, D), F32, kind="ExternalOutput").ap()
    program(nc, a, out)
    r = _run(nc, [arrays], core_ids=[0])
    return r.results[0]["out_0"]
```
